# Optimizing a Trainium2 kernel written in Bass

```python
import numpy as np
import jax
import jax.numpy as jnp

def _softmax(x, axis=-1):
    return jax.nn.softmax(x, axis=axis)

def _gelu(x):
    return jax.nn.gelu(x, approximate=True)

def _silu(x):
    return jax.nn.silu(x)

def _sigmoid(x):
    return jax.nn.sigmoid(x)

def _layernorm(x, axis=-1, eps=1e-05):
    m = jnp.mean(x, axis=axis, keepdims=True)
    v = jnp.var(x, axis=axis, keepdims=True)
    return (x - m) / jnp.sqrt(v + eps)

def _scatter_add(tgt, idx, src, axis=0):
    return tgt.at[idx].add(src)

def _segment_sum(src, seg, n):
    return jax.ops.segment_sum(src, seg, n)
kernel_name = 'mk_flamingo_gated_d4_seqx_r8_ce1ccc'

def setup_inputs(seed: int=0):
    np.random.seed(seed)
    _w = jnp.asarray

    def _rec_inputs():
        import jax
        import jax.numpy as jnp
        _rk = jax.random.key(seed)
        x = -0.0002928 + 1 * jax.random.normal(jax.random.fold_in(_rk, 1), (4, 512, 128), jnp.float32)
        _lenS = 512 - jax.random.randint(jax.random.fold_in(_rk, 7), (4,), 0, max(1, 512 // 4) + 1, jnp.int32)
        _lenS2 = 77 - jax.random.randint(jax.random.fold_in(_rk, 8), (4,), 0, max(1, 77 // 4) + 1, jnp.int32)
        _ctx_1024P = jax.random.normal(jax.random.fold_in(_rk, 11), (4, 16, 128), jnp.float32)
        _ctx_1024c = jax.random.dirichlet(jax.random.fold_in(_rk, 511), 0.3 * jnp.ones((16,), jnp.float32), (4, 77))
        _ctx_1024t = jnp.einsum('bsk,bkd->bsd', _ctx_1024c, _ctx_1024P)
        _ctx_1024t = _ctx_1024t * jax.lax.rsqrt(jnp.mean(jnp.square(_ctx_1024t)) + 1e-12) * 0.953939
        ctx_1024 = -1.39393e-06 + 0.999914 * (_ctx_1024t + 0.3 * jax.random.normal(jax.random.fold_in(_rk, 611), (4, 77, 128), jnp.float32))
        _validS = jnp.arange(512)[None, :] < _lenS[:, None]
        _validS2 = jnp.arange(77)[None, :] < _lenS2[:, None]
        _causal = jnp.tril(jnp.ones((512, 512), dtype=bool))
        mask_BxSxS2_ff1 = jnp.where(jnp.ones((4, 512, 77), dtype=bool), 1.0, 0.0).astype(jnp.float32)
        mask_BxS2_bf0 = jnp.logical_not(jnp.ones((4, 77), dtype=bool))
        mask_BxS2_bf1 = jnp.ones((4, 77), dtype=bool)
        _g = jax.random.normal(jax.random.fold_in(_rk, 9001), (2, 4), jnp.float32)
        _g = jnp.sign(_g) * jnp.maximum(jnp.abs(_g), 1.0) + (_g == 0) * 1.0
        g_xattn = _g[0]
        g_ffn = _g[1]
        return (x, ctx_1024, mask_BxSxS2_ff1, mask_BxS2_bf0, mask_BxS2_bf1, g_xattn, g_ffn)
    x, ctx_1024, mask_BxSxS2_ff1, mask_BxS2_bf0, mask_BxS2_bf1, g_xattn, g_ffn = _rec_inputs()

    def _L0_xattn_setup():
        import jax, jax.numpy as jnp
        import numpy as np
        HIDDEN = 128
        NUM_HEADS = 16
        HEAD_DIM = HIDDEN // NUM_HEADS
        B, LQ, LK = (2, 256, 256)

        def _split_heads(x):
            b, l, _ = x.shape
            return x.reshape(b, l, NUM_HEADS, HEAD_DIM).transpose(0, 2, 1, 3)
        key = jax.random.key(seed)
        ks = jax.random.split(key, 9)
        s = 1.0 / np.sqrt(HIDDEN)
        return {'hidden_states_query': jax.random.normal(ks[0], (B, LQ, HIDDEN), jnp.float32), 'hidden_states_key': jax.random.normal(ks[1], (B, LK, HIDDEN), jnp.float32), 'attention_mask': jnp.ones((B, LQ, LK), jnp.float32), 'Wq': jax.random.normal(ks[2], (HIDDEN, HIDDEN), jnp.float32) * s, 'bq': jax.random.normal(ks[3], (HIDDEN,), jnp.float32) * s, 'Wk': jax.random.normal(ks[4], (HIDDEN, HIDDEN), jnp.float32) * s, 'bk': jax.random.normal(ks[5], (HIDDEN,), jnp.float32) * s, 'Wv': jax.random.normal(ks[6], (HIDDEN, HIDDEN), jnp.float32) * s, 'bv': jax.random.normal(ks[7], (HIDDEN,), jnp.float32) * s}
    _L0_xattn_all = _L0_xattn_setup()
    _L0_xattn_in = {k: v for k, v in _L0_xattn_all.items() if k in ('Wq', 'bq', 'Wk', 'bk', 'Wv', 'bv')}
    del _L0_xattn_all

    def _L0_ffn_setup():
        import jax, jax.numpy as jnp
        import numpy as np
        EPS = 1e-06
        LN_EPS = 1e-05

        def _absmean_core(W):
            gamma = jnp.mean(jnp.abs(W)) + EPS
            Ws = W / gamma
            Wq = jnp.sign(Ws) * jnp.minimum(jnp.round(jnp.abs(Ws)), 1.0)
            return (Wq, gamma)

        @jax.custom_vjp
        def absmean(W):
            return _absmean_core(W)[0]

        def _absmean_fwd(W):
            Wq, gamma = _absmean_core(W)
            return (Wq, gamma)

        def _absmean_bwd(gamma, g):
            return (g / gamma,)
        absmean.defvjp(_absmean_fwd, _absmean_bwd)

        def layernorm(x, w, b, eps=LN_EPS):
            mu = jnp.mean(x, axis=-1, keepdims=True)
            var = jnp.mean((x - mu) ** 2, axis=-1, keepdims=True)
            return (x - mu) * jax.lax.rsqrt(var + eps) * w + b
        key = jax.random.key(seed)
        k1, k2, k3 = jax.random.split(key, 3)
        d, h = (128, 512)
        B, T = (8, 256)
        return {'x': jax.random.normal(k1, (B, T, d), jnp.float32), 'W_fc': jax.random.normal(k2, (h, d), jnp.float32), 'ln_w': jnp.ones((h,), jnp.float32), 'ln_b': jnp.zeros((h,), jnp.float32), 'W_proj': jax.random.normal(k3, (d, h), jnp.float32)}
    _L0_ffn_all = _L0_ffn_setup()
    _L0_ffn_in = {k: v for k, v in _L0_ffn_all.items() if k in ('W_fc', 'ln_w', 'ln_b', 'W_proj')}
    del _L0_ffn_all

    def _L1_xattn_setup():
        import jax, jax.numpy as jnp
        import numpy as np
        DIM = 128
        N_HEADS = 16
        HEAD_DIM = DIM // N_HEADS
        MAX_DIST = 128
        B, S = (2, 256)

        def _rel_bias(bias_table, q_len, k_len):
            q_pos = jnp.arange(q_len)
            k_pos = jnp.arange(k_len)
            rel = jnp.clip(k_pos[None, :] - q_pos[:, None], -MAX_DIST, MAX_DIST) + MAX_DIST
            bias = bias_table[rel]
            return jnp.transpose(bias, (2, 0, 1))
        key = jax.random.key(seed)
        ks = jax.random.split(key, 16)
        inp = {'query': jax.random.normal(ks[0], (B, S, DIM), jnp.float32), 'key': jax.random.normal(ks[1], (B, S, DIM), jnp.float32), 'value': jax.random.normal(ks[2], (B, S, DIM), jnp.float32), 'key_padding_mask': jnp.zeros((B, S), dtype=bool), 'Wq': jax.random.normal(ks[3], (DIM, DIM), jnp.float32) * DIM ** (-0.5), 'bq': jnp.zeros((DIM,), jnp.float32), 'Wk': jax.random.normal(ks[4], (DIM, DIM), jnp.float32) * DIM ** (-0.5), 'bk': jnp.zeros((DIM,), jnp.float32), 'Wv': jax.random.normal(ks[5], (DIM, DIM), jnp.float32) * DIM ** (-0.5), 'bv': jnp.zeros((DIM,), jnp.float32), 'Wo': jax.random.normal(ks[6], (DIM, DIM), jnp.float32) * DIM ** (-0.5), 'bo': jnp.zeros((DIM,), jnp.float32), 'logit_scale': jax.random.normal(ks[7], (N_HEADS,), jnp.float32) * 0.1, 'bias_table': jax.random.normal(ks[8], (2 * MAX_DIST + 1, N_HEADS), jnp.float32) * 0.02}
        return inp
    _L1_xattn_all = _L1_xattn_setup()
    _L1_xattn_in = {k: v for k, v in _L1_xattn_all.items() if k in ('Wq', 'bq', 'Wk', 'bk', 'Wv', 'bv', 'Wo', 'bo', 'logit_scale', 'bias_table')}
    del _L1_xattn_all

    def _L1_ffn_setup():
        import jax, jax.numpy as jnp
        import numpy as np
        D = 128
        H = 512
        E = 64
        K = 3
        B, S = (2, 256)
        C = 64
        key = jax.random.key(seed)
        ks = jax.random.split(key, 6)
        s = 0.02
        return {'x': jax.random.normal(ks[0], (B, S, D), jnp.float32), 'gate_w': jax.random.normal(ks[1], (D, E), jnp.float32) * s, 'gate_b': jnp.zeros((E,), jnp.float32), 'w1': jax.random.normal(ks[2], (E, D, H), jnp.float32) * s, 'b1': jnp.zeros((E, H), jnp.float32), 'w2': jax.random.normal(ks[3], (E, H, D), jnp.float32) * s, 'b2': jnp.zeros((E, D), jnp.float32)}
    _L1_ffn_all = _L1_ffn_setup()
    _L1_ffn_in = {k: v for k, v in _L1_ffn_all.items() if k in ('gate_w', 'gate_b', 'w1', 'b1', 'w2', 'b2')}
    del _L1_ffn_all

    def _L2_xattn_setup():
        import jax, jax.numpy as jnp
        import numpy as np
        DIM = 128
        DIM_LATENT = 128
        DIM_HEAD = 64
        HEADS = 16
        INNER = HEADS * DIM_HEAD

        def layernorm(x, g, b, eps=1e-05):
            m = jnp.mean(x, axis=-1, keepdims=True)
            v = jnp.mean((x - m) ** 2, axis=-1, keepdims=True)
            return (x - m) / jnp.sqrt(v + eps) * g + b

        def rmsnorm(x, gamma, eps=1e-08):
            n = jnp.linalg.norm(x, axis=-1, keepdims=True) * x.shape[-1] ** (-0.5)
            return x / jnp.maximum(n, eps) * gamma
        key = jax.random.key(seed)
        ks = jax.random.split(key, 8)
        b, n, m = (4, 512, 64)
        x = jax.random.normal(ks[0], (b, n, DIM), dtype=jnp.float32)
        latents = jax.random.normal(ks[1], (b, m, DIM_LATENT), dtype=jnp.float32)
        mask = jnp.ones((b, n), dtype=bool)
        s = 0.02
        return {'x': x, 'latents': latents, 'mask': mask, 'ln_x_g': jnp.ones((DIM,), jnp.float32), 'ln_x_b': jnp.zeros((DIM,), jnp.float32), 'ln_l_g': jnp.ones((DIM_LATENT,), jnp.float32), 'ln_l_b': jnp.zeros((DIM_LATENT,), jnp.float32), 'qn_g': jnp.ones((DIM_HEAD,), jnp.float32), 'kn_g': jnp.ones((DIM_HEAD,), jnp.float32), 'Wq': jax.random.normal(ks[2], (DIM_LATENT, INNER), jnp.float32) * s, 'Wkv': jax.random.normal(ks[3], (DIM, 2 * INNER), jnp.float32) * s, 'Wout': jax.random.normal(ks[4], (INNER, DIM_LATENT), jnp.float32) * s, 'bout': jnp.zeros((DIM_LATENT,), jnp.float32)}
    _L2_xattn_all = _L2_xattn_setup()
    _L2_xattn_in = {k: v for k, v in _L2_xattn_all.items() if k in ('ln_x_g', 'ln_x_b', 'ln_l_g', 'ln_l_b', 'qn_g', 'kn_g', 'Wq', 'Wkv', 'Wout', 'bout')}
    del _L2_xattn_all

    def _L2_ffn_setup():
        import jax, jax.numpy as jnp
        import numpy as np
        D = 128
        F = 352
        E = 8
        TOP_K = 2
        key = jax.random.key(seed)
        ks = jax.random.split(key, 6)
        std = 0.02
        x = jax.random.normal(ks[0], (2, 256, D), dtype=jnp.float32)
        router_w = jax.random.normal(ks[1], (D, E), dtype=jnp.float32) * std
        w1 = jax.random.normal(ks[2], (E, D, F), dtype=jnp.float32) * std
        v1 = jax.random.normal(ks[3], (E, D, F), dtype=jnp.float32) * std
        w2 = jax.random.normal(ks[4], (E, F, D), dtype=jnp.float32) * std
        bias = jnp.zeros((D,), dtype=jnp.float32)
        return {'x': x, 'router_w': router_w, 'w1': w1, 'v1': v1, 'w2': w2, 'bias': bias}
    _L2_ffn_all = _L2_ffn_setup()
    _L2_ffn_in = {k: v for k, v in _L2_ffn_all.items() if k in ('router_w', 'w1', 'v1', 'w2', 'bias')}
    del _L2_ffn_all

    def _L3_xattn_setup():
        import jax, jax.numpy as jnp
        import numpy as np
        DIM = 128
        N_HEADS = 16
        HEAD_DIM = DIM // N_HEADS
        EPS = 1e-06
        Q_THETA = 32.0
        K_THETA = 1000.0

        def precompute_freqs_1d(dim, seq_len, theta):
            freqs = theta ** (-jnp.arange(0, dim, 2, dtype=jnp.float32) / dim)
            t = jnp.arange(seq_len, dtype=jnp.float32)
            ang = t[:, None] * freqs[None, :]
            return (jnp.cos(ang), jnp.sin(ang))

        def rms_norm(x, w):
            var = jnp.mean(x * x, axis=-1, keepdims=True)
            return x * jax.lax.rsqrt(var + EPS) * w

        def apply_rope(t, cos, sin):
            cos = cos[None, None, :, :]
            sin = sin[None, None, :, :]
            t1, t2 = jnp.split(t, 2, axis=-1)
            return jnp.concatenate([t1 * cos - t2 * sin, t2 * cos + t1 * sin], axis=-1)
        key = jax.random.key(seed)
        ks = jax.random.split(key, 8)
        B, T, S = (128, 64, 48)
        s = 1.0 / np.sqrt(DIM)
        return {'x': jax.random.normal(ks[0], (B, T, DIM), jnp.float32), 'context': jax.random.normal(ks[1], (B, S, DIM), jnp.float32), 'Wq': jax.random.normal(ks[2], (DIM, DIM), jnp.float32) * s, 'Wk': jax.random.normal(ks[3], (DIM, DIM), jnp.float32) * s, 'Wv': jax.random.normal(ks[4], (DIM, DIM), jnp.float32) * s, 'Wo': jax.random.normal(ks[5], (DIM, DIM), jnp.float32) * s, 'q_norm_w': jnp.ones((HEAD_DIM,), jnp.float32), 'k_norm_w': jnp.ones((HEAD_DIM,), jnp.float32)}
    _L3_xattn_all = _L3_xattn_setup()
    _L3_xattn_in = {k: v for k, v in _L3_xattn_all.items() if k in ('Wq', 'Wk', 'Wv', 'Wo', 'q_norm_w', 'k_norm_w')}
    del _L3_xattn_all

    def _L3_ffn_setup():
        import jax, jax.numpy as jnp
        import numpy as np
        DIM = 128
        MOE_HID = 64
        SHARED_HID = 256
        N_EXPERTS = 16
        TOP_K = 2
        NORM_TOPK_PROB = True
        key = jax.random.key(seed)
        ks = jax.random.split(key, 9)
        s = 0.02
        x = jax.random.normal(ks[0], (2, 128, DIM), dtype=jnp.float32)
        Wg = jax.random.normal(ks[1], (N_EXPERTS, DIM), dtype=jnp.float32) * s
        We_gate = jax.random.normal(ks[2], (N_EXPERTS, MOE_HID, DIM), dtype=jnp.float32) * s
        We_up = jax.random.normal(ks[3], (N_EXPERTS, MOE_HID, DIM), dtype=jnp.float32) * s
        We_down = jax.random.normal(ks[4], (N_EXPERTS, DIM, MOE_HID), dtype=jnp.float32) * s
        Ws_gate = jax.random.normal(ks[5], (SHARED_HID, DIM), dtype=jnp.float32) * s
        Ws_up = jax.random.normal(ks[6], (SHARED_HID, DIM), dtype=jnp.float32) * s
        Ws_down = jax.random.normal(ks[7], (DIM, SHARED_HID), dtype=jnp.float32) * s
        Wsg = jax.random.normal(ks[8], (1, DIM), dtype=jnp.float32) * s
        return {'x': x, 'Wg': Wg, 'We_gate': We_gate, 'We_up': We_up, 'We_down': We_down, 'Ws_gate': Ws_gate, 'Ws_up': Ws_up, 'Ws_down': Ws_down, 'Wsg': Wsg}
    _L3_ffn_all = _L3_ffn_setup()
    _L3_ffn_in = {k: v for k, v in _L3_ffn_all.items() if k in ('Wg', 'We_gate', 'We_up', 'We_down', 'Ws_gate', 'Ws_up', 'Ws_down', 'Wsg')}
    del _L3_ffn_all
    return {'x': x, 'ctx_1024': ctx_1024, 'mask_BxSxS2_ff1': mask_BxSxS2_ff1, 'mask_BxS2_bf0': mask_BxS2_bf0, 'mask_BxS2_bf1': mask_BxS2_bf1, 'g_xattn': g_xattn, 'g_ffn': g_ffn, 'L0_xattn_Wq': _L0_xattn_in['Wq'], 'L0_xattn_bq': _L0_xattn_in['bq'], 'L0_xattn_Wk': _L0_xattn_in['Wk'], 'L0_xattn_bk': _L0_xattn_in['bk'], 'L0_xattn_Wv': _L0_xattn_in['Wv'], 'L0_xattn_bv': _L0_xattn_in['bv'], 'L0_ffn_W_fc': _L0_ffn_in['W_fc'], 'L0_ffn_ln_w': _L0_ffn_in['ln_w'], 'L0_ffn_ln_b': _L0_ffn_in['ln_b'], 'L0_ffn_W_proj': _L0_ffn_in['W_proj'], 'L1_xattn_Wq': _L1_xattn_in['Wq'], 'L1_xattn_bq': _L1_xattn_in['bq'], 'L1_xattn_Wk': _L1_xattn_in['Wk'], 'L1_xattn_bk': _L1_xattn_in['bk'], 'L1_xattn_Wv': _L1_xattn_in['Wv'], 'L1_xattn_bv': _L1_xattn_in['bv'], 'L1_xattn_Wo': _L1_xattn_in['Wo'], 'L1_xattn_bo': _L1_xattn_in['bo'], 'L1_xattn_logit_scale': _L1_xattn_in['logit_scale'], 'L1_xattn_bias_table': _L1_xattn_in['bias_table'], 'L1_ffn_gate_w': _L1_ffn_in['gate_w'], 'L1_ffn_gate_b': _L1_ffn_in['gate_b'], 'L1_ffn_w1': _L1_ffn_in['w1'], 'L1_ffn_b1': _L1_ffn_in['b1'], 'L1_ffn_w2': _L1_ffn_in['w2'], 'L1_ffn_b2': _L1_ffn_in['b2'], 'L2_xattn_ln_x_g': _L2_xattn_in['ln_x_g'], 'L2_xattn_ln_x_b': _L2_xattn_in['ln_x_b'], 'L2_xattn_ln_l_g': _L2_xattn_in['ln_l_g'], 'L2_xattn_ln_l_b': _L2_xattn_in['ln_l_b'], 'L2_xattn_qn_g': _L2_xattn_in['qn_g'], 'L2_xattn_kn_g': _L2_xattn_in['kn_g'], 'L2_xattn_Wq': _L2_xattn_in['Wq'], 'L2_xattn_Wkv': _L2_xattn_in['Wkv'], 'L2_xattn_Wout': _L2_xattn_in['Wout'], 'L2_xattn_bout': _L2_xattn_in['bout'], 'L2_ffn_router_w': _L2_ffn_in['router_w'], 'L2_ffn_w1': _L2_ffn_in['w1'], 'L2_ffn_v1': _L2_ffn_in['v1'], 'L2_ffn_w2': _L2_ffn_in['w2'], 'L2_ffn_bias': _L2_ffn_in['bias'], 'L3_xattn_Wq': _L3_xattn_in['Wq'], 'L3_xattn_Wk': _L3_xattn_in['Wk'], 'L3_xattn_Wv': _L3_xattn_in['Wv'], 'L3_xattn_Wo': _L3_xattn_in['Wo'], 'L3_xattn_q_norm_w': _L3_xattn_in['q_norm_w'], 'L3_xattn_k_norm_w': _L3_xattn_in['k_norm_w'], 'L3_ffn_Wg': _L3_ffn_in['Wg'], 'L3_ffn_We_gate': _L3_ffn_in['We_gate'], 'L3_ffn_We_up': _L3_ffn_in['We_up'], 'L3_ffn_We_down': _L3_ffn_in['We_down'], 'L3_ffn_Ws_gate': _L3_ffn_in['Ws_gate'], 'L3_ffn_Ws_up': _L3_ffn_in['Ws_up'], 'L3_ffn_Ws_down': _L3_ffn_in['Ws_down'], 'L3_ffn_Wsg': _L3_ffn_in['Wsg']}

def reference(x, ctx_1024, mask_BxSxS2_ff1, mask_BxS2_bf0, mask_BxS2_bf1, g_xattn, g_ffn, L0_xattn_Wq, L0_xattn_bq, L0_xattn_Wk, L0_xattn_bk, L0_xattn_Wv, L0_xattn_bv, L0_ffn_W_fc, L0_ffn_ln_w, L0_ffn_ln_b, L0_ffn_W_proj, L1_xattn_Wq, L1_xattn_bq, L1_xattn_Wk, L1_xattn_bk, L1_xattn_Wv, L1_xattn_bv, L1_xattn_Wo, L1_xattn_bo, L1_xattn_logit_scale, L1_xattn_bias_table, L1_ffn_gate_w, L1_ffn_gate_b, L1_ffn_w1, L1_ffn_b1, L1_ffn_w2, L1_ffn_b2, L2_xattn_ln_x_g, L2_xattn_ln_x_b, L2_xattn_ln_l_g, L2_xattn_ln_l_b, L2_xattn_qn_g, L2_xattn_kn_g, L2_xattn_Wq, L2_xattn_Wkv, L2_xattn_Wout, L2_xattn_bout, L2_ffn_router_w, L2_ffn_w1, L2_ffn_v1, L2_ffn_w2, L2_ffn_bias, L3_xattn_Wq, L3_xattn_Wk, L3_xattn_Wv, L3_xattn_Wo, L3_xattn_q_norm_w, L3_xattn_k_norm_w, L3_ffn_Wg, L3_ffn_We_gate, L3_ffn_We_up, L3_ffn_We_down, L3_ffn_Ws_gate, L3_ffn_Ws_up, L3_ffn_Ws_down, L3_ffn_Wsg):
    import jax
    import jax.numpy as jnp

    def _L0_xattn_ref(hidden_states_query, hidden_states_key, attention_mask, Wq, bq, Wk, bk, Wv, bv):
        import jax, jax.numpy as jnp
        import numpy as np
        HIDDEN = 128
        NUM_HEADS = 16
        HEAD_DIM = HIDDEN // NUM_HEADS
        B, LQ, LK = (2, 256, 256)

        def _split_heads(x):
            b, l, _ = x.shape
            return x.reshape(b, l, NUM_HEADS, HEAD_DIM).transpose(0, 2, 1, 3)
        q = _split_heads(hidden_states_query @ Wq.T + bq)
        k = _split_heads(hidden_states_key @ Wk.T + bk)
        v = _split_heads(hidden_states_key @ Wv.T + bv)
        scale = 1.0 / np.sqrt(HEAD_DIM)
        scores = jnp.einsum('bhqd,bhkd->bhqk', q * scale, k)
        scores = scores + ((1.0 - attention_mask) * -10000.0)[:, None, :, :]
        probs = jax.nn.softmax(scores, axis=-1)
        ctx = jnp.einsum('bhqk,bhkd->bhqd', probs, v)
        b, h, lq, d = ctx.shape
        return ctx.transpose(0, 2, 1, 3).reshape(b, lq, h * d)

    def _L0_ffn_ref(x, W_fc, ln_w, ln_b, W_proj):
        import jax, jax.numpy as jnp
        import numpy as np
        EPS = 1e-06
        LN_EPS = 1e-05

        def _absmean_core(W):
            gamma = jnp.mean(jnp.abs(W)) + EPS
            Ws = W / gamma
            Wq = jnp.sign(Ws) * jnp.minimum(jnp.round(jnp.abs(Ws)), 1.0)
            return (Wq, gamma)

        @jax.custom_vjp
        def absmean(W):
            return _absmean_core(W)[0]

        def _absmean_fwd(W):
            Wq, gamma = _absmean_core(W)
            return (Wq, gamma)

        def _absmean_bwd(gamma, g):
            return (g / gamma,)
        absmean.defvjp(_absmean_fwd, _absmean_bwd)

        def layernorm(x, w, b, eps=LN_EPS):
            mu = jnp.mean(x, axis=-1, keepdims=True)
            var = jnp.mean((x - mu) ** 2, axis=-1, keepdims=True)
            return (x - mu) * jax.lax.rsqrt(var + eps) * w + b
        h = jnp.einsum('btd,hd->bth', x, absmean(W_fc))
        h = jax.nn.gelu(h, approximate=False)
        h = layernorm(h, ln_w, ln_b)
        return jnp.einsum('bth,dh->btd', h, absmean(W_proj))

    def _L1_xattn_ref(query, key, value, key_padding_mask, Wq, bq, Wk, bk, Wv, bv, Wo, bo, logit_scale, bias_table):
        import jax, jax.numpy as jnp
        import numpy as np
        DIM = 128
        N_HEADS = 16
        HEAD_DIM = DIM // N_HEADS
        MAX_DIST = 128
        B, S = (2, 256)

        def _rel_bias(bias_table, q_len, k_len):
            q_pos = jnp.arange(q_len)
            k_pos = jnp.arange(k_len)
            rel = jnp.clip(k_pos[None, :] - q_pos[:, None], -MAX_DIST, MAX_DIST) + MAX_DIST
            bias = bias_table[rel]
            return jnp.transpose(bias, (2, 0, 1))
        b, tq, _ = query.shape
        tk = key.shape[1]

        def proj(x, W, bias):
            y = x @ W + bias
            return y.reshape(b, -1, N_HEADS, HEAD_DIM).transpose(0, 2, 1, 3)
        q = proj(query, Wq, bq)
        k = proj(key, Wk, bk)
        v = proj(value, Wv, bv)
        base_scale = HEAD_DIM ** (-0.5)
        scale = base_scale * jnp.minimum(jnp.exp(logit_scale), 4.0)
        scores = jnp.einsum('bhqd,bhkd->bhqk', q, k) * scale[None, :, None, None]
        scores = scores + _rel_bias(bias_table, tq, tk)[None]
        neg = -jnp.finfo(scores.dtype).max
        scores = jnp.where(key_padding_mask[:, None, None, :], neg, scores)
        attn = jax.nn.softmax(scores, axis=-1)
        out = jnp.einsum('bhqk,bhkd->bhqd', attn, v)
        out = out.transpose(0, 2, 1, 3).reshape(b, tq, DIM)
        out = out @ Wo + bo
        return out

    def _L1_ffn_ref(x, gate_w, gate_b, w1, b1, w2, b2):
        import jax, jax.numpy as jnp
        import numpy as np
        D = 128
        H = 512
        E = 64
        K = 3
        B, S = (2, 256)
        C = 64
        xf = x.reshape(-1, D)
        T = xf.shape[0]
        logits = xf @ gate_w + gate_b
        top_l, top_i = jax.lax.top_k(logits, K)
        gates = jax.nn.softmax(top_l, axis=-1)
        fe = top_i.reshape(-1)
        fg = gates.reshape(-1)
        tok = jnp.repeat(jnp.arange(T), K)
        oh = jax.nn.one_hot(fe, E, dtype=jnp.int32)
        pos = (jnp.cumsum(oh, axis=0) * oh).sum(-1) - 1
        valid = pos < C
        buf = jnp.zeros((E, C, D), x.dtype).at[fe, pos].set(xf[tok], mode='drop')
        h = jax.nn.gelu(jnp.einsum('ecd,edh->ech', buf, w1) + b1[:, None, :], approximate=False)
        y = jnp.einsum('ech,ehd->ecd', h, w2) + b2[:, None, :]
        rows = y[fe, jnp.minimum(pos, C - 1)] * (fg * valid.astype(x.dtype))[:, None]
        out = jnp.zeros_like(xf).at[tok].add(rows)
        return out.reshape(x.shape)

    def _L2_xattn_ref(x, latents, mask, ln_x_g, ln_x_b, ln_l_g, ln_l_b, qn_g, kn_g, Wq, Wkv, Wout, bout):
        import jax, jax.numpy as jnp
        import numpy as np
        DIM = 128
        DIM_LATENT = 128
        DIM_HEAD = 64
        HEADS = 16
        INNER = HEADS * DIM_HEAD

        def layernorm(x, g, b, eps=1e-05):
            m = jnp.mean(x, axis=-1, keepdims=True)
            v = jnp.mean((x - m) ** 2, axis=-1, keepdims=True)
            return (x - m) / jnp.sqrt(v + eps) * g + b

        def rmsnorm(x, gamma, eps=1e-08):
            n = jnp.linalg.norm(x, axis=-1, keepdims=True) * x.shape[-1] ** (-0.5)
            return x / jnp.maximum(n, eps) * gamma
        b, n, _ = x.shape
        m = latents.shape[1]
        h, d = (HEADS, DIM_HEAD)
        scale = d ** (-0.5)
        xn = layernorm(x, ln_x_g, ln_x_b)
        ln = layernorm(latents, ln_l_g, ln_l_b)
        q = (ln @ Wq).reshape(b, m, h, d).transpose(0, 2, 1, 3)
        kv = jnp.concatenate([xn @ Wkv, ln @ Wkv], axis=1)
        kv = kv.reshape(b, n + m, 2, h, d)
        k = kv[:, :, 0].transpose(0, 2, 1, 3)
        v = kv[:, :, 1].transpose(0, 2, 1, 3)
        qn = rmsnorm(q, qn_g) * scale
        kn = rmsnorm(k, kn_g)
        sim = jnp.einsum('bhid,bhjd->bhij', qn, kn)
        max_neg = -jnp.finfo(sim.dtype).max
        padded_mask = jnp.concatenate([mask, jnp.ones((b, m), bool)], axis=1)
        sim = jnp.where(padded_mask[:, None, None, :], sim, max_neg)
        attn = jax.nn.softmax(sim.astype(jnp.float32), axis=-1).astype(sim.dtype)
        out = jnp.einsum('bhij,bhjd->bhid', attn, v)
        out = out.transpose(0, 2, 1, 3).reshape(b, m, h * d)
        return out @ Wout + bout

    def _L2_ffn_ref(x, router_w, w1, v1, w2, bias):
        import jax, jax.numpy as jnp
        import numpy as np
        D = 128
        F = 352
        E = 8
        TOP_K = 2
        B, S, d = x.shape
        xt = x.reshape(B * S, d)
        scores = jax.nn.softmax(xt @ router_w, axis=-1)
        expert_weights, expert_idx = jax.lax.top_k(scores, TOP_K)
        h = jax.nn.gelu(jnp.einsum('td,edf->tef', xt, w1), approximate=False) * jnp.einsum('td,edf->tef', xt, v1)
        y = jnp.einsum('tef,efd->ted', h, w2)
        yk = jnp.take_along_axis(y, expert_idx[:, :, None], axis=1)
        out = jnp.sum(expert_weights[:, :, None] * yk, axis=1) + bias
        return out.reshape(B, S, d)

    def _L3_xattn_ref(x, context, Wq, Wk, Wv, Wo, q_norm_w, k_norm_w):
        import jax, jax.numpy as jnp
        import numpy as np
        DIM = 128
        N_HEADS = 16
        HEAD_DIM = DIM // N_HEADS
        EPS = 1e-06
        Q_THETA = 32.0
        K_THETA = 1000.0

        def precompute_freqs_1d(dim, seq_len, theta):
            freqs = theta ** (-jnp.arange(0, dim, 2, dtype=jnp.float32) / dim)
            t = jnp.arange(seq_len, dtype=jnp.float32)
            ang = t[:, None] * freqs[None, :]
            return (jnp.cos(ang), jnp.sin(ang))

        def rms_norm(x, w):
            var = jnp.mean(x * x, axis=-1, keepdims=True)
            return x * jax.lax.rsqrt(var + EPS) * w

        def apply_rope(t, cos, sin):
            cos = cos[None, None, :, :]
            sin = sin[None, None, :, :]
            t1, t2 = jnp.split(t, 2, axis=-1)
            return jnp.concatenate([t1 * cos - t2 * sin, t2 * cos + t1 * sin], axis=-1)
        B, T, C = x.shape
        S = context.shape[1]
        H, D = (N_HEADS, HEAD_DIM)
        q = (x @ Wq.T).reshape(B, T, H, D).transpose(0, 2, 1, 3)
        k = (context @ Wk.T).reshape(B, S, H, D).transpose(0, 2, 1, 3)
        v = (context @ Wv.T).reshape(B, S, H, D).transpose(0, 2, 1, 3)
        q = rms_norm(q, q_norm_w)
        k = rms_norm(k, k_norm_w)
        q_cos, q_sin = precompute_freqs_1d(D, T, Q_THETA)
        k_cos, k_sin = precompute_freqs_1d(D, S, K_THETA)
        q = apply_rope(q, q_cos, q_sin)
        k = apply_rope(k, k_cos, k_sin)
        scale = D ** (-0.5)
        attn = jnp.einsum('bhtd,bhsd->bhts', q, k) * scale
        attn = jax.nn.softmax(attn, axis=-1)
        out = jnp.einsum('bhts,bhsd->bhtd', attn, v)
        out = out.transpose(0, 2, 1, 3).reshape(B, T, C)
        return out @ Wo.T

    def _L3_ffn_ref(x, Wg, We_gate, We_up, We_down, Ws_gate, Ws_up, Ws_down, Wsg):
        import jax, jax.numpy as jnp
        import numpy as np
        DIM = 128
        MOE_HID = 64
        SHARED_HID = 256
        N_EXPERTS = 16
        TOP_K = 2
        NORM_TOPK_PROB = True
        B, S, D = x.shape
        xt = x.reshape(-1, D)
        gates = jax.nn.softmax(xt @ Wg.T, axis=-1)
        scores, inds = jax.lax.top_k(gates, TOP_K)
        if NORM_TOPK_PROB:
            scores = scores / jnp.sum(scores, axis=-1, keepdims=True)
        g = jnp.einsum('td,ehd->teh', xt, We_gate)
        u = jnp.einsum('td,ehd->teh', xt, We_up)
        h = jax.nn.silu(g) * u
        y_all = jnp.einsum('teh,edh->ted', h, We_down)
        y_sel = jnp.take_along_axis(y_all, inds[:, :, None], axis=1)
        y = jnp.sum(y_sel * scores[:, :, None], axis=1)
        shared = jax.nn.silu(xt @ Ws_gate.T) * (xt @ Ws_up.T) @ Ws_down.T
        y = y + jax.nn.sigmoid(xt @ Wsg.T) * shared
        return y.reshape(B, S, D)
    x = x + jnp.tanh(g_xattn[0]) * _L0_xattn_ref(_layernorm(x, axis=-1), ctx_1024, mask_BxSxS2_ff1, L0_xattn_Wq, L0_xattn_bq, L0_xattn_Wk, L0_xattn_bk, L0_xattn_Wv, L0_xattn_bv)
    x = x + jnp.tanh(g_ffn[0]) * _L0_ffn_ref(_layernorm(x, axis=-1), L0_ffn_W_fc, L0_ffn_ln_w, L0_ffn_ln_b, L0_ffn_W_proj)
    x = x + jnp.tanh(g_xattn[1]) * _L1_xattn_ref(_layernorm(x, axis=-1), ctx_1024, ctx_1024, mask_BxS2_bf0, L1_xattn_Wq, L1_xattn_bq, L1_xattn_Wk, L1_xattn_bk, L1_xattn_Wv, L1_xattn_bv, L1_xattn_Wo, L1_xattn_bo, L1_xattn_logit_scale, L1_xattn_bias_table)
    x = x + jnp.tanh(g_ffn[1]) * _L1_ffn_ref(_layernorm(x, axis=-1), L1_ffn_gate_w, L1_ffn_gate_b, L1_ffn_w1, L1_ffn_b1, L1_ffn_w2, L1_ffn_b2)
    x = x + jnp.tanh(g_xattn[2]) * _L2_xattn_ref(ctx_1024, _layernorm(x, axis=-1), mask_BxS2_bf1, L2_xattn_ln_x_g, L2_xattn_ln_x_b, L2_xattn_ln_l_g, L2_xattn_ln_l_b, L2_xattn_qn_g, L2_xattn_kn_g, L2_xattn_Wq, L2_xattn_Wkv, L2_xattn_Wout, L2_xattn_bout)
    x = x + jnp.tanh(g_ffn[2]) * _L2_ffn_ref(_layernorm(x, axis=-1), L2_ffn_router_w, L2_ffn_w1, L2_ffn_v1, L2_ffn_w2, L2_ffn_bias)
    x = x + jnp.tanh(g_xattn[3]) * _L3_xattn_ref(_layernorm(x, axis=-1), ctx_1024, L3_xattn_Wq, L3_xattn_Wk, L3_xattn_Wv, L3_xattn_Wo, L3_xattn_q_norm_w, L3_xattn_k_norm_w)
    x = x + jnp.tanh(g_ffn[3]) * _L3_ffn_ref(_layernorm(x, axis=-1), L3_ffn_Wg, L3_ffn_We_gate, L3_ffn_We_up, L3_ffn_We_down, L3_ffn_Ws_gate, L3_ffn_Ws_up, L3_ffn_Ws_down, L3_ffn_Wsg)
    return x

_drawn_inputs = setup_inputs


def setup_inputs(seed=0):
    import zlib

    import numpy as np

    out = dict(_drawn_inputs(seed))
    spreads = {'L0_ffn_ln_w': (1.0, 0.2),
     'L0_ffn_ln_b': (0.0, 0.1),
     'L1_xattn_bq': (0.0, 0.8),
     'L1_xattn_bk': (0.0, 2.0),
     'L1_xattn_bv': (0.0, 0.8),
     'L1_xattn_bo': (0.0, 0.8),
     'L1_ffn_gate_b': (0.0, 0.8),
     'L1_ffn_b1': (0.0, 0.8),
     'L1_ffn_b2': (0.0, 2.0),
     'L2_xattn_ln_x_g': (1.0, 0.6),
     'L2_xattn_ln_x_b': (0.0, 0.8),
     'L2_xattn_ln_l_g': (1.0, 0.6),
     'L2_xattn_ln_l_b': (0.0, 0.8),
     'L2_xattn_qn_g': (1.0, 0.6),
     'L2_xattn_kn_g': (1.0, 0.6),
     'L2_xattn_bout': (0.0, 0.8),
     'L2_ffn_bias': (0.0, 0.8),
     'L3_xattn_q_norm_w': (1.0, 0.6),
     'L3_xattn_k_norm_w': (1.0, 0.6)}
    factors = {'g_ffn': 8.0,
     'L0_xattn_Wq': 8.0,
     'L0_xattn_bq': 8.0,
     'L0_xattn_Wk': 8.0,
     'L0_xattn_bk': 64.0,
     'L1_xattn_Wq': 3.951,
     'L1_xattn_Wk': 4.111,
     'L1_xattn_logit_scale': 25.082,
     'L1_xattn_bias_table': 64.0,
     'L1_ffn_gate_w': 8.0,
     'L1_ffn_w1': 8.0,
     'L1_ffn_w2': 8.0,
     'L2_xattn_Wq': 8.0,
     'L2_xattn_Wkv': 8.0,
     'L2_xattn_Wout': 8.0,
     'L2_ffn_router_w': 8.0,
     'L2_ffn_w1': 8.0,
     'L2_ffn_v1': 8.0,
     'L2_ffn_w2': 8.0,
     'L3_xattn_Wq': 46.331,
     'L3_xattn_Wk': 43.465,
     'L3_ffn_Wg': 8.0,
     'L3_ffn_We_gate': 8.0,
     'L3_ffn_We_up': 8.0,
     'L3_ffn_We_down': 8.0,
     'L3_ffn_Ws_gate': 8.0,
     'L3_ffn_Ws_up': 8.0,
     'L3_ffn_Ws_down': 8.0,
     'L3_ffn_Wsg': 8.0}
    for name, (base, spread) in spreads.items():
        noise = np.random.default_rng([zlib.crc32(name.encode()), seed]).standard_normal(out[name].shape)
        drawn = base * np.exp(spread * noise) if base else spread * noise
        out[name] = jnp.asarray(drawn.astype(out[name].dtype))
    for name, factor in factors.items():
        out[name] = (out[name] * factor).astype(out[name].dtype)
    return out
```

```python
from contextlib import ExitStack, contextmanager

import concourse.bass as bass
import numpy as np
from concourse import mybir

F32 = mybir.dt.float32
BF16 = mybir.dt.bfloat16
I32 = mybir.dt.int32
U32 = mybir.dt.uint32
ALU = mybir.AluOpType
ACT = mybir.ActivationFunctionType
AX = mybir.AxisListType

B, S, D = 4, 512, 128
T = B * S
P = 128
TILES = T // P
QT = S // P
SK = 77
H, DH = 16, 8
QUAD, HQ = 4, 4
ROWS = HQ * SK
CH = 3
CR = -(-ROWS // CH)
NEG = -131072.0
LN_EPS = 1e-5
LOG_EXP = "natural_log_exp_and_others"
GELU = "gelu_and_others"


def rows_of(i):
    return min(CR, ROWS - i * CR)


class Core:

    def __init__(self, nc, ctx, dram):
        self.nc, self.ctx, self.dram = nc, ctx, dram
        self.phases = []

    def sem(self, name):
        if self.phases:
            self.phases[-1].append(self.nc.alloc_semaphore(name))
            return self.phases[-1][-1]
        return self.ctx.enter_context(self.nc.semaphore(name))

    @contextmanager
    def phase(self):
        self.phases.append([])
        yield
        self.nc.clear_and_free_semaphores(self.phases.pop())
        self.nc.all_engine_barrier()

    def keep(self, name, shape, dt=F32):
        return self.ctx.enter_context(self.nc.sbuf_tensor(name, shape, dt))


def load_shared(c):
    nc, d = c.nc, c.dram
    c.xT = c.keep("xT", [P, T])
    c.xn = c.keep("xn", [P, T])
    c.center = c.keep("center", [P, P])
    c.mean = c.keep("mean", [P, P])
    c.ident = c.keep("ident", [P, P])
    c.identb = c.keep("identb", [P, P], BF16)
    c.onesb = c.keep("onesb", [P, P], BF16)
    c.headmask = c.keep("headmask", [P, H])
    c.rowmask = c.keep("rowmask", [P, CH, 32])
    c.sel = c.keep("sel", [P, QUAD * ROWS], BF16)
    c.self = c.keep("self", [P, QUAD * ROWS])
    c.ctxrep = c.keep("ctxrep", [P, B, ROWS])
    c.iota = c.keep("iota", [P, 64])
    c.gates = c.keep("gates", [P, 8])
    loaded, got, x_in = c.sem("shared_loaded"), c.sem("shared_cast"), c.sem("x_loaded")
    with nc.Block() as block:
        @block.sync
        def _(sp):
            sp.dma_start(c.xT[:, :], d["xT"]).then_inc(x_in, 16)
            for dst, src in ((c.center, "center"), (c.mean, "mean"), (c.ident, "ident"), (c.gates, "gates"),
                             (c.headmask, "headmask"), (c.self, "self"), (c.iota, "iota")):
                sp.dma_start(dst[:, :], d[src]).then_inc(loaded, 16)
            sp.dma_start(c.rowmask[:, :, :], d["rowmask"]).then_inc(loaded, 16)
            sp.dma_start(c.ctxrep[:, :, :], d["ctxrep"]).then_inc(loaded, 16)
            sp.wait_ge(x_in, 16)
            sp.wait_ge(loaded, 9 * 16)

        @block.scalar
        def _(act):
            act.wait_ge(loaded, 9 * 16)
            nc.scalar.activation(c.gates[:, :], c.gates[:, :], ACT.Tanh).then_inc(got, 1)

        @block.vector
        def _(dve):
            dve.wait_ge(loaded, 9 * 16)
            nc.vector.tensor_copy(c.identb[:, :], c.ident[:, :]).then_inc(got, 1)
            nc.vector.tensor_copy(c.sel[:, :], c.self[:, :]).then_inc(got, 1)
            nc.vector.memset(c.onesb[:, :], 1.0).then_inc(got, 1)
            dve.wait_ge(got, 4)


def layer_norm(c, name, pieces, eps=LN_EPS):
    nc = c.nc
    n = len(pieces)
    with ExitStack() as ctx, c.phase():
        cen = ctx.enter_context(nc.psum_tensor(name + "_cen", [P, 2, 512], F32))
        var = ctx.enter_context(nc.psum_tensor(name + "_var", [P, 2, 512], F32))
        sq = ctx.enter_context(nc.sbuf_tensor(name + "_sq", [P, 2, 512], F32))
        lnv = ctx.enter_context(nc.sbuf_tensor(name + "_lnv", [P, 2, 512], F32))
        rstd = ctx.enter_context(nc.sbuf_tensor(name + "_rstd", [P, 2, 512], F32))
        centred, squared, var_ready, logged, rstd_ready, normed = (
            c.sem(f"{name}_{s}") for s in ("centred", "squared", "var_ready", "logged", "rstd_ready", "normed"))
        with nc.Block() as block:
            @block.tensor
            def _(pe):
                def variance(i):
                    w = pieces[i][2]
                    pe.wait_ge(squared, i + 1)
                    nc.tensor.matmul(var[:, i % 2, :w], c.mean[:, :], sq[:, i % 2, :w],
                                     start=True, stop=True).then_inc(var_ready, 1)

                for i, (src, _, w) in enumerate(pieces):
                    if i >= 2:
                        pe.wait_ge(normed, i - 1)
                    nc.tensor.matmul(cen[:, i % 2, :w], c.center[:, :], src,
                                     start=True, stop=True).then_inc(centred, 1)
                    if i >= 1:
                        variance(i - 1)
                variance(n - 1)

            @block.scalar
            def _(act):
                def scale(i):
                    w = pieces[i][2]
                    act.wait_ge(var_ready, i + 1)
                    if i >= 2:
                        act.wait_ge(normed, i - 1)
                    nc.scalar.activation(lnv[:, i % 2, :w], var[:, i % 2, :w], ACT.Ln, bias=eps).then_inc(logged, 1)
                    act.wait_ge(logged, i + 1)
                    nc.scalar.activation(rstd[:, i % 2, :w], lnv[:, i % 2, :w], ACT.Exp,
                                         scale=-0.5).then_inc(rstd_ready, 1)

                nc.scalar.preload_act_table_set(LOG_EXP)
                for i, (_, _, w) in enumerate(pieces):
                    act.wait_ge(centred, i + 1)
                    if i >= 2:
                        act.wait_ge(var_ready, i - 1)
                    nc.scalar.activation(sq[:, i % 2, :w], cen[:, i % 2, :w], ACT.Square).then_inc(squared, 1)
                    if i >= 1:
                        scale(i - 1)
                scale(n - 1)

            @block.vector
            def _(dve):
                for i, (_, dst, w) in enumerate(pieces):
                    dve.wait_ge(rstd_ready, i + 1)
                    nc.vector.tensor_tensor(dst, cen[:, i % 2, :w], rstd[:, i % 2, :w], ALU.mult).then_inc(normed, 1)
                dve.wait_ge(normed, n)


def norm_x(c, name):
    layer_norm(c, name, [(c.xT[:, s:s + S], c.xn[:, s:s + S], S) for s in range(0, T, S)])


def head_attention(c, name, gate, wq, wk, wv, bq=None, bk=None, bv=None, wo=None, bo=None,
                   mask=False, relbias=False, rope=False):
    nc, d = c.nc, c.dram
    with ExitStack() as ctx, c.phase():
        def sb(n, shape, dt=F32):
            return ctx.enter_context(nc.sbuf_tensor(f"{name}_{n}", shape, dt))

        def ps(n, shape):
            return ctx.enter_context(nc.psum_tensor(f"{name}_{n}", shape, F32))

        def sem(n):
            return c.sem(f"{name}_{n}")

        A = ps("A", [P, 4, 512])
        TP = ps("TP", [P, 2, 512])
        O = ps("O", [P, 512])
        DEN = ps("DEN", [P, 512])
        Wq, Wk, Wv = sb("Wq", [P, P]), sb("Wk", [P, P]), sb("Wv", [P, P])
        vec = sb("vec", [P, 8])
        cv = sb("cv", [P, 4])
        kT = sb("kT", [P, B * SK])
        vexp = sb("vexp", [P, B, CH * P])
        kexp = sb("kexp", [P, QUAD * ROWS])
        kexpb = sb("kexpb", [P, QUAD * ROWS], BF16)
        vcur = sb("vcur", [P, CH * P])
        qT = sb("qT", [P, S])
        qb = sb("qb", [P, S], BF16)
        nm = sb("nm", [P, QT, P], BF16)
        negm = sb("negm", [P, S], BF16)
        prob = sb("prob", [P, 8, 512])
        lnd = sb("lnd", [P, S])
        rden = sb("rden", [P, S])
        on = sb("on", [P, S])
        up = sb("up", [P, S])
        if wo:
            Wo = sb("Wo", [P, P])
            on2 = sb("on2", [P, S])
        if mask or relbias:
            added = sb("added", [P, 2, 512])
        if mask:
            maskT = sb("maskT", [P, B * CH, S])
            maskQ = sb("maskQ", [P, B * QT, SK])
            maskQb = sb("maskQb", [P, B * QT, SK], BF16)
        if relbias:
            biasT = sb("biasT", [P, QUAD * CH, S])
            biasQ = sb("biasQ", [P, QUAD * ROWS])
            biasQb = sb("biasQb", [P, 3, QUAD * ROWS], BF16)
            keym = sb("keym", [P, B * SK], I32)
            negQ = sb("negQ", [P, B, SK], BF16)
            keep = sb("keep", [P, B * SK])
            rowm = sb("rowm", [P, B * CH], I32)
            rowkeep = sb("rowkeep", [P, B, 2 * CH])
            rowcur = sb("rowcur", [P, 2 * CH])
        if rope:
            Wqp, Wkp = sb("Wqp", [P, P]), sb("Wkp", [P, P])
            blk8 = sb("blk8", [P, P])
            qcs = sb("qcs", [P, 2, S])
            kcs = sb("kcs", [P, 2, B * SK])
            rsq, rln, rr, ra, rb = (sb(n, [P, S]) for n in ("rsq", "rln", "rr", "ra", "rb"))

        loaded, prep, kproj, kready, vproj, vready = (
            sem(n) for n in ("loaded", "prep", "kproj", "kready", "vproj", "vready"))
        x_updated, vec_done, expscale = sem("x_updated"), sem("vec_done"), sem("expscale")

        loads = [(Wq[:, :], d[wq]), (Wk[:, :], d[wk]), (Wv[:, :], d[wv]), (vec[:, :], d[name + "_vec"])]
        if wo:
            loads.append((Wo[:, :], d[wo]))
        if mask:
            loads += [(maskT[0:CR, :, :], d["maskT"]), (maskQ[:, :, :], d["maskQ"])]
        if relbias:
            loads += [(keym[:, :], d["keymask"].partition_broadcast(P)), (rowm[0:CR, :], d["rowkeymask"])]
            loads += [(biasT[0:CR, :, :], d["biasT"])]
        if rope:
            loads += [(Wqp[:, :], d[wq + "_p"]), (Wkp[:, :], d[wk + "_p"]), (blk8[:, :], d["blk8"]),
                      (qcs[:, :, :], d["qcs"]), (kcs[:, :, :], d["kcs"])]
        nload = 16 * len(loads)
        bq_loaded, bq_cast = sem("biasq_loaded"), sem("biasq_cast")
        with nc.Block() as block:
            @block.sync
            def _(sp):
                for dst, src in loads:
                    sp.dma_start(dst, src).then_inc(loaded, 16)
                if relbias:
                    for t in range(3):
                        if t:
                            sp.wait_ge(bq_cast, t)
                        sp.dma_start(biasQ[:, :], d["biasQ"][:, t, :]).then_inc(bq_loaded, 16)
                sp.wait_ge(loaded, nload)

            @block.tensor
            def _(pe):
                pe.wait_ge(loaded, nload)
                ctxall = c.ctxrep[:, :, 0:SK]
                nc.tensor.matmul(DEN[:, 0:B * SK], Wk[:, :], ctxall, start=True, stop=True).then_inc(kproj, 1)
                if rope:
                    nc.tensor.matmul(O[:, 0:B * SK], Wkp[:, :], ctxall, start=True, stop=True).then_inc(kproj, 1)
                    pe.wait_ge(prep, 1)
                    nc.tensor.matmul(A[:, 0, 0:B * SK], blk8[:, :], rsq[:, 0:B * SK],
                                     start=True, stop=True).then_inc(kproj, 1)
                for b in range(B):
                    if b >= 2:
                        pe.wait_ge(vready, b - 1)
                    for i in range(CH):
                        mm = nc.tensor.matmul(TP[0:rows_of(i), b % 2, i * P:(i + 1) * P],
                                              c.ctxrep[:, b, i * CR:i * CR + rows_of(i)], Wv[:, :],
                                              start=True, stop=True)
                    mm.then_inc(vproj, 1)

            @block.scalar
            def _(act):
                nc.scalar.preload_act_table_set(LOG_EXP)
                act.wait_ge(loaded, nload)
                if relbias:
                    nc.scalar.activation(cv[:, 3:4], vec[:, 4:5], ACT.Exp).then_inc(expscale, 1)
                if rope:
                    act.wait_ge(kproj, 1)
                    nc.scalar.activation(rsq[:, 0:B * SK], DEN[:, 0:B * SK], ACT.Square).then_inc(prep, 1)
                    act.wait_ge(kproj, 3)
                    nc.scalar.activation(rln[:, 0:B * SK], A[:, 0, 0:B * SK], ACT.Ln, bias=1e-6,
                                         scale=1.0 / DH).then_inc(prep, 1)
                    act.wait_ge(prep, 2)
                    nc.scalar.activation(rr[:, 0:B * SK], rln[:, 0:B * SK], ACT.Exp, scale=-0.5).then_inc(prep, 1)
                else:
                    act.wait_ge(kproj, 1)
                    nc.scalar.activation(kT[:, :], DEN[:, 0:B * SK], ACT.Identity, bias=vec[:, 1:2]).then_inc(prep, 1)

            @block.vector
            def _(dve):
                dve.wait_ge(loaded, nload)
                nc.vector.memset(nm[:, :, :], 0.0).then_inc(kready, 1)
                nc.vector.memset(vexp[:, :, :], 0.0).then_inc(vec_done, 1)
                if relbias:
                    dve.wait_ge(expscale, 1)
                    nc.vector.tensor_scalar(cv[:, 0:1], cv[:, 3:4], 4.0, DH ** -0.5, ALU.min,
                                            ALU.mult).then_inc(vec_done, 1)
                else:
                    nc.vector.memset(cv[:, 0:1], DH ** -0.5).then_inc(vec_done, 1)
                dve.wait_ge(vec_done, 2)
                nc.vector.tensor_tensor(cv[:, 1:2], vec[:, 0:1], cv[:, 0:1], ALU.mult).then_inc(vec_done, 1)
                nc.vector.tensor_tensor(cv[:, 2:3], vec[:, 3:4] if wo else vec[:, 2:3], c.gates[:, gate:gate + 1],
                                        ALU.mult).then_inc(vec_done, 1)
                dve.wait_ge(vec_done, 4)
                if rope:
                    dve.wait_ge(kproj, 2)
                    dve.wait_ge(prep, 1)
                    nc.vector.scalar_tensor_tensor(out=ra[:, 0:B * SK], in0=DEN[:, 0:B * SK], scalar=vec[:, 4:5],
                                                   in1=kcs[:, 0, :], op0=ALU.mult, op1=ALU.mult).then_inc(kready, 1)
                    nc.vector.scalar_tensor_tensor(out=rb[:, 0:B * SK], in0=O[:, 0:B * SK], scalar=vec[:, 5:6],
                                                   in1=kcs[:, 1, :], op0=ALU.mult, op1=ALU.mult).then_inc(kready, 1)
                    dve.wait_ge(kready, 3)
                    nc.vector.tensor_tensor(kT[:, :], ra[:, 0:B * SK], rb[:, 0:B * SK], ALU.add).then_inc(kready, 1)
                    dve.wait_ge(kready, 4)
                    dve.wait_ge(prep, 3)
                    nc.vector.tensor_tensor(kT[:, :], kT[:, :], rr[:, 0:B * SK], ALU.mult).then_inc(kready, 1)
                    dve.wait_ge(kready, 5)
                if relbias:
                    nc.vector.tensor_scalar(keep[:, :], keym[:, :], -1.0, 1.0, ALU.mult, ALU.add).then_inc(kready, 1)
                    nc.vector.tensor_scalar(negQ[:, :, :], keym[:, :].rearrange("p (b k) -> p b k", b=B), NEG / P,
                                            None, ALU.mult).then_inc(kready, 1)
                    rows = rowm[0:CR, :].rearrange("p (b i) -> p b i", b=B)
                    nc.vector.tensor_scalar(rowkeep[0:CR, :, 0:CH], rows, -1.0, 1.0, ALU.mult,
                                            ALU.add).then_inc(kready, 1)
                    nc.vector.tensor_scalar(rowkeep[0:CR, :, CH:], rows, NEG, None, ALU.mult).then_inc(kready, 1)
                    dve.wait_ge(kready, 5)
                    dve.wait_ge(prep, 1)
                    nc.vector.tensor_tensor(kT[:, :], kT[:, :], keep[:, :], ALU.mult).then_inc(kready, 1)
                    dve.wait_ge(kready, 6)
                if mask:
                    nc.vector.tensor_scalar(maskQb[:, :, :], maskQ[:, :, :], 1e4, -1e4, ALU.mult,
                                            ALU.add).then_inc(kready, 1)
                    nc.vector.tensor_scalar(maskT[0:CR, :, :], maskT[0:CR, :, :], 1e4, -1e4, ALU.mult,
                                            ALU.add).then_inc(kready, 1)
                    dve.wait_ge(kready, 3)
                for b in range(B):
                    dve.wait_ge(vproj, b + 1)
                    for i in range(CH):
                        r = rows_of(i)
                        ins = nc.vector.tensor_tensor(
                            vexp[0:r, b, i * P:(i + 1) * P].rearrange("p (g e) -> p g e", g=QUAD),
                            TP[0:r, b % 2, i * P:(i + 1) * P].rearrange("p (g e) -> p g e", g=QUAD),
                            c.rowmask[0:r, i:i + 1, :].broadcast_to([r, QUAD, 32]), ALU.mult)
                    ins.then_inc(vready, 1)
                dve.wait_ge(vready, B)

            @block.gpsimd
            def _(pool):
                if relbias:
                    for t in range(3):
                        pool.wait_ge(bq_loaded, 16 * (t + 1))
                        nc.gpsimd.tensor_copy(biasQb[:, t, :], biasQ[:, :]).then_inc(bq_cast, 1)
                    pool.wait_ge(bq_cast, 3)

        (q_proj, q_sq, q_ms, q_log, q_rms, q_made, q_cast, k_made, k_cast, v_copied, s_ready, s_used, nm_turned,
         negm_ready, t_ready, t_added, p_ready, pv_done, den_log, den_ready, o_normed, o_biased, y_ready,
         up_ready) = (sem(n) for n in (
            "q_proj", "q_sq", "q_ms", "q_log", "q_rms", "q_made", "q_cast", "k_made", "k_cast", "v_copied",
            "s_ready", "s_used", "nm_turned", "negm_ready", "t_ready", "t_added", "p_ready", "pv_done", "den_log",
            "den_ready", "o_normed", "o_biased", "y_ready", "up_ready"))
        U = QUAD * CH
        NS = 2 * QT
        NQ = 4 if rope else 1
        NP = 2 if rope else 1
        adds = mask or relbias
        turned = TP[:, 1, 0:S // 2].bitcast(BF16)

        def tokens(b):
            return bass.ds(b * S, S)

        with nc.Block() as block:
            @block.tensor
            def _(pe):
                with pe.Fori(0, B) as b:
                    pe.wait_ge(x_updated, b)
                    nc.tensor.matmul(A[:, 0, :], Wq[:, :], c.xn[:, tokens(b)], start=True, stop=True)\
                        .then_inc(q_proj, 1)
                    if rope:
                        nc.tensor.matmul(A[:, 1, :], Wqp[:, :], c.xn[:, tokens(b)], start=True, stop=True)\
                            .then_inc(q_proj, 1)
                        pe.wait_ge(q_sq, b + 1)
                        nc.tensor.matmul(TP[:, 0, :], blk8[:, :], rsq[:, :], start=True, stop=True)\
                            .then_inc(q_ms, 1)
                    pe.wait_ge(q_cast, b + 1)
                    pe.wait_ge(k_cast, b + 1)
                    for u in range(NS):
                        qt, half = u // 2, u % 2
                        if u >= 2:
                            pe.wait_ge(s_used, b * NS + u - 1)
                        for j in range(2):
                            g = 2 * half + j
                            out = A[:, 2 * (u % 2) + j, 0:ROWS]
                            out3 = out.rearrange("p (h k) -> p h k", h=HQ)
                            mm = nc.tensor.matmul(out, qb[:, qt * P:(qt + 1) * P],
                                                  kexpb[:, g * ROWS:(g + 1) * ROWS], start=True, stop=not adds)
                            if mask:
                                mm = nc.tensor.matmul(
                                    out3, c.identb[:, :],
                                    maskQb[:, bass.ds(b * QT + qt, 1), :].broadcast_to([P, HQ, SK]),
                                    start=False, stop=True)
                            if relbias:
                                nc.tensor.matmul(out, c.identb[:, :],
                                                 biasQb[:, min(qt, 2), g * ROWS:(g + 1) * ROWS],
                                                 start=False, stop=False)
                                mm = nc.tensor.matmul(
                                    out3, c.onesb[:, :], negQ[:, bass.ds(b, 1), :].broadcast_to([P, HQ, SK]),
                                    start=False, stop=True)
                        mm.then_inc(s_ready, 1)
                    pe.wait_ge(s_used, b * NS + NS)
                    for qt in range(QT):
                        mm = nc.tensor.transpose(turned[:, qt * P:(qt + 1) * P], nm[:, qt, :], c.identb[:, :])
                    mm.then_inc(nm_turned, 1)
                    pe.wait_ge(negm_ready, b + 1)

                    def scores(t):
                        i, g = t // QUAD, t % QUAD
                        r, at = rows_of(i), g * ROWS + i * CR
                        if t >= 2:
                            pe.wait_ge(t_added if adds else p_ready, b * U + t - 1)
                        nc.tensor.matmul(TP[0:r, t % 2, :], kexp[:, at:at + r], qT[:, :], start=True, stop=False)
                        nc.tensor.matmul(TP[0:r, t % 2, :], c.sel[:, at:at + r], negm[:, :], start=False,
                                         stop=True).then_inc(t_ready, 1)

                    def values(i):
                        r = rows_of(i)
                        pe.wait_ge(p_ready, b * U + QUAD * (i + 1))
                        for g in range(QUAD):
                            nc.tensor.matmul(O[32 * g:32 * g + 32, :], vcur[0:r, i * P + 32 * g:i * P + 32 * g + 32],
                                             prob[0:r, (QUAD * i + g) % 8, :], start=(i == 0), stop=(i == CH - 1))
                        for g in range(QUAD):
                            mm = nc.tensor.matmul(DEN[32 * g:32 * g + 32, :], c.rowmask[0:r, i, :],
                                                  prob[0:r, (QUAD * i + g) % 8, :], start=(i == 0), stop=(i == CH - 1))
                        mm.then_inc(pv_done, 1)

                    pe.wait_ge(v_copied, b + 1)
                    for i in range(CH):
                        for g in range(QUAD):
                            scores(QUAD * i + g)
                        if i:
                            values(i - 1)
                    values(CH - 1)
                    if wo:
                        pe.wait_ge(o_biased if bv else o_normed, b + 1)
                        nc.tensor.matmul(TP[:, 0, :], Wo[:, :], (on2 if bv else on)[:, :],
                                         start=True, stop=True).then_inc(y_ready, 1)

            @block.scalar
            def _(act):
                nc.scalar.preload_act_table_set(LOG_EXP)
                with act.Fori(0, B) as b:
                    act.wait_ge(x_updated, b)
                    nc.scalar.copy(vcur[:, :], vexp[:, bass.ds(b, 1), :]).then_inc(v_copied, 1)
                    act.wait_ge(q_proj, b * NP + 1)
                    if rope:
                        nc.scalar.activation(rsq[:, :], A[:, 0, :], ACT.Square).then_inc(q_sq, 1)
                        act.wait_ge(q_ms, b + 1)
                        nc.scalar.activation(rln[:, :], TP[:, 0, :], ACT.Ln, bias=DH * 1e-6).then_inc(q_log, 1)
                        act.wait_ge(q_log, b + 1)
                        nc.scalar.activation(rr[:, :], rln[:, :], ACT.Exp, scale=-0.5).then_inc(q_rms, 1)
                    else:
                        nc.scalar.activation(qT[:, :], A[:, 0, :], ACT.Identity, bias=cv[:, 1:2],
                                             scale=cv[:, 0:1]).then_inc(q_made, 1)
                    for t in range(U):
                        i = t // QUAD
                        r = rows_of(i)
                        act.wait_ge(t_added if adds else t_ready, b * U + t + 1)
                        if t >= 8:
                            act.wait_ge(pv_done, b * CH + t // QUAD - 1)
                        nc.scalar.activation(prob[0:r, t % 8, :], (added if adds else TP)[0:r, t % 2, :], ACT.Exp,
                                             bias=rowcur[0:r, CH + i:CH + i + 1] if relbias else 0.0)\
                            .then_inc(p_ready, 1)
                    act.wait_ge(pv_done, b * CH + CH)
                    nc.scalar.activation(lnd[:, :], DEN[:, :], ACT.Ln).then_inc(den_log, 1)
                    act.wait_ge(den_log, b + 1)
                    nc.scalar.activation(rden[:, :], lnd[:, :], ACT.Exp, scale=-1.0).then_inc(den_ready, 1)
                    src = on
                    act.wait_ge(o_normed, b + 1)
                    if bv and wo:
                        nc.scalar.activation(on2[:, :], on[:, :], ACT.Identity, bias=vec[:, 2:3])\
                            .then_inc(o_biased, 1)
                    if wo:
                        act.wait_ge(y_ready, b + 1)
                        src = TP[:, 0, :]
                    nc.scalar.activation(up[:, :], src if wo else on[:, :], ACT.Identity, bias=cv[:, 2:3],
                                         scale=c.gates[:, gate:gate + 1]).then_inc(up_ready, 1)

            @block.vector
            def _(dve):
                with dve.Fori(0, B) as b:
                    dve.wait_ge(x_updated, b)
                    nc.vector.tensor_tensor(kexp[:, :].rearrange("p (h k) -> p h k", h=H),
                                            kT[:, bass.ds(b * SK, SK)].rearrange("p (a k) -> p a k", a=1)
                                            .broadcast_to([P, H, SK]),
                                            c.headmask[:, :].rearrange("p (h a) -> p h a", a=1)
                                            .broadcast_to([P, H, SK]), ALU.mult).then_inc(k_made, 1)
                    if relbias:
                        nc.vector.tensor_copy(rowcur[0:CR, :], rowkeep[0:CR, bass.ds(b, 1), :]).then_inc(k_made, 1)
                    dve.wait_ge(k_made, b * (2 if relbias else 1) + (2 if relbias else 1))
                    nc.vector.tensor_copy(kexpb[:, :], kexp[:, :]).then_inc(k_cast, 1)
                    if rope:
                        dve.wait_ge(q_proj, b * 2 + 2)
                        dve.wait_ge(q_sq, b + 1)
                        nc.vector.scalar_tensor_tensor(out=ra[:, :], in0=A[:, 0, :], scalar=vec[:, 6:7],
                                                       in1=qcs[:, 0, :], op0=ALU.mult, op1=ALU.mult).then_inc(q_made, 1)
                        nc.vector.scalar_tensor_tensor(out=rb[:, :], in0=A[:, 1, :], scalar=vec[:, 7:8],
                                                       in1=qcs[:, 1, :], op0=ALU.mult, op1=ALU.mult).then_inc(q_made, 1)
                        dve.wait_ge(q_made, b * 4 + 2)
                        nc.vector.tensor_tensor(ra[:, :], ra[:, :], rb[:, :], ALU.add).then_inc(q_made, 1)
                        dve.wait_ge(q_made, b * 4 + 3)
                        dve.wait_ge(q_rms, b + 1)
                        nc.vector.tensor_tensor(qT[:, :], ra[:, :], rr[:, :], ALU.mult).then_inc(q_made, 1)
                    dve.wait_ge(q_made, b * NQ + NQ)
                    nc.vector.tensor_copy(qb[:, :], qT[:, :]).then_inc(q_cast, 1)
                    for u in range(NS):
                        qt, half = u // 2, u % 2
                        dve.wait_ge(s_ready, b * NS + u + 1)
                        nc.vector.tensor_reduce(
                            nm[:, qt, 8 * half:8 * half + 8].rearrange("p (a h) -> p a h", a=2),
                            A[:, 2 * (u % 2):2 * (u % 2) + 2, 0:ROWS].rearrange("p a (h k) -> p a h k", h=HQ),
                            AX.X, ALU.max, negate=True).then_inc(s_used, 1)
                    dve.wait_ge(nm_turned, b + 1)
                    nc.vector.tensor_copy(negm[:, :], turned).then_inc(negm_ready, 1)
                    if adds:
                        for t in range(U):
                            i, g = t // QUAD, t % QUAD
                            r = rows_of(i)
                            dve.wait_ge(t_ready, b * U + t + 1)
                            if t >= 2:
                                dve.wait_ge(p_ready, b * U + t - 1)
                            if mask:
                                nc.vector.tensor_tensor(added[0:r, t % 2, :], TP[0:r, t % 2, :],
                                                        maskT[0:r, bass.ds(b * CH + i, 1), :], ALU.add)\
                                    .then_inc(t_added, 1)
                            else:
                                nc.vector.scalar_tensor_tensor(
                                    out=added[0:r, t % 2, :], in0=biasT[0:r, g * CH + i, :],
                                    scalar=rowcur[0:r, i:i + 1], in1=TP[0:r, t % 2, :], op0=ALU.mult,
                                    op1=ALU.add).then_inc(t_added, 1)
                    dve.wait_ge(pv_done, b * CH + CH)
                    dve.wait_ge(den_ready, b + 1)
                    nc.vector.tensor_tensor(on[:, :], O[:, :], rden[:, :], ALU.mult).then_inc(o_normed, 1)
                    dve.wait_ge(up_ready, b + 1)
                    nc.vector.tensor_tensor(c.xT[:, tokens(b)], c.xT[:, tokens(b)], up[:, :], ALU.add)\
                        .then_inc(x_updated, 1)
                dve.wait_ge(x_updated, B)


def ternary_ffn(c, name, gate):
    nc, d = c.nc, c.dram
    NJ = 4
    HID = NJ * P
    with ExitStack() as ctx, c.phase():
        def sb(n, shape, dt=F32):
            return ctx.enter_context(nc.sbuf_tensor(f"{name}_{n}", shape, dt))

        def ps(n, shape):
            return ctx.enter_context(nc.psum_tensor(f"{name}_{n}", shape, F32))

        def sem(n):
            return c.sem(f"{name}_{n}")

        HP = ps("HP", [P, 2, S])
        MU, M2, Y, PRE = (ps(n, [P, S]) for n in ("MU", "M2", "Y", "PRE"))
        Wf, Wp = sb("Wf", [P, HID]), sb("Wp", [P, HID])
        Qf, Qp, Wc = sb("Qf", [P, HID]), sb("Qp", [P, HID]), sb("Wc", [P, HID])
        low = sb("low", [P, HID])
        ln = sb("ln", [P, 2 * NJ])
        st = sb("st", [P, 12])
        h, hs = sb("h", [P, NJ, S]), sb("hs", [P, NJ, S])
        mu2, v, lnv, rstd, yn, up = (sb(n, [P, S]) for n in ("mu2", "v", "lnv", "rstd", "yn", "up"))
        loaded, rounded, totals, summed, folded = (sem(n) for n in ("loaded", "rounded", "totals", "summed", "folded"))
        with nc.Block() as block:
            @block.sync
            def _(sp):
                for dst, src in ((Wf, "F0_W1"), (Wp, "F0_W2"), (ln, "F0_ln")):
                    sp.dma_start(dst[:, :], d[src]).then_inc(loaded, 16)
                sp.wait_ge(loaded, 48)

            @block.vector
            def _(dve):
                dve.wait_ge(loaded, 48)
                for n, w in ((0, Wf), (1, Wp)):
                    nc.vector.scalar_tensor_tensor(out=low[:, :], in0=w[:, :], scalar=-1.0, in1=w[:, :],
                                                   op0=ALU.mult, op1=ALU.max).then_inc(rounded, 1)
                    dve.wait_ge(rounded, 2 * n + 1)
                    nc.vector.tensor_reduce(st[:, n:n + 1], low[:, :], AX.X, ALU.add).then_inc(rounded, 1)
                    dve.wait_ge(rounded, 2 * n + 2)
                dve.wait_ge(summed, 1)
                nc.vector.tensor_scalar(st[:, 2:4], PRE[:, 0:2], float(P) / (P * HID), 1e-6, ALU.mult,
                                        ALU.add).then_inc(rounded, 1)
                dve.wait_ge(rounded, 5)
                nc.vector.tensor_scalar(st[:, 4:6], st[:, 2:4], 0.5, None, ALU.mult).then_inc(rounded, 1)
                nc.vector.tensor_scalar(st[:, 6:8], st[:, 2:4], -0.5, None, ALU.mult).then_inc(rounded, 1)
                dve.wait_ge(rounded, 7)
                for n, w, q in ((0, Wf, Qf), (1, Wp, Qp)):
                    nc.vector.tensor_scalar(low[:, :], w[:, :], st[:, 6 + n:7 + n], None, ALU.is_lt).then_inc(rounded, 1)
                    dve.wait_ge(rounded, 8 + 2 * n)
                    nc.vector.scalar_tensor_tensor(out=q[:, :], in0=w[:, :], scalar=st[:, 4 + n:5 + n], in1=low[:, :],
                                                   op0=ALU.is_gt, op1=ALU.subtract).then_inc(rounded, 1)
                    dve.wait_ge(rounded, 9 + 2 * n)
                for j in range(NJ):
                    nc.vector.tensor_scalar(Wc[:, j * P:(j + 1) * P], Qp[:, j * P:(j + 1) * P], ln[:, j:j + 1], None,
                                            ALU.mult).then_inc(rounded, 1)
                dve.wait_ge(summed, 2)
                dve.wait_ge(rounded, 15)
                for j in range(NJ):
                    nc.vector.scalar_tensor_tensor(out=Wc[:, j * P:(j + 1) * P], in0=PRE[:, P:2 * P], scalar=-1.0 / NJ,
                                                   in1=Wc[:, j * P:(j + 1) * P], op0=ALU.mult,
                                                   op1=ALU.add).then_inc(folded, 1)
                nc.vector.tensor_tensor(st[:, 8:9], PRE[:, 2 * P:2 * P + 1], c.gates[:, gate:gate + 1],
                                        ALU.mult).then_inc(folded, 1)
                dve.wait_ge(folded, NJ + 1)

            @block.tensor
            def _(pe):
                pe.wait_ge(rounded, 4)
                nc.tensor.matmul(PRE[:, 0:2], c.mean[:, :], st[:, 0:2], start=True, stop=True).then_inc(summed, 1)
                pe.wait_ge(rounded, 15)
                for j in range(NJ):
                    nc.tensor.matmul(PRE[:, P:2 * P], c.mean[:, :], Wc[:, j * P:(j + 1) * P], start=(j == 0),
                                     stop=(j == NJ - 1))
                for j in range(NJ):
                    mm = nc.tensor.matmul(PRE[:, 2 * P:2 * P + 1], Qp[:, j * P:(j + 1) * P], ln[:, NJ + j:NJ + j + 1],
                                          start=(j == 0), stop=(j == NJ - 1))
                mm.then_inc(summed, 1)

        (x_updated, h_ready, gelued, squared, acc_ready, mu_sq, var_made, var_log, rstd_ready, y_scaled, up_ready) = (
            sem(n) for n in ("x_updated", "h_ready", "gelued", "squared", "acc_ready", "mu_sq", "var_made", "var_log",
                             "rstd_ready", "y_scaled", "up_ready"))

        def tokens(b):
            return bass.ds(b * S, S)

        with nc.Block() as block:
            @block.tensor
            def _(pe):
                with pe.Fori(0, B) as b:
                    pe.wait_ge(x_updated, b)

                    def down(j):
                        first, last = j == 0, j == NJ - 1
                        pe.wait_ge(gelued, b * NJ + j + 1)
                        nc.tensor.matmul(MU[:, :], c.mean[:, :], h[:, j, :], start=first, stop=last)
                        nc.tensor.matmul(Y[:, :], Wc[:, j * P:(j + 1) * P], h[:, j, :], start=first, stop=last)
                        pe.wait_ge(squared, b * NJ + j + 1)
                        mm = nc.tensor.matmul(M2[:, :], c.mean[:, :], hs[:, j, :], start=first, stop=last)
                        if last:
                            mm.then_inc(acc_ready, 1)

                    for j in range(NJ):
                        if j >= 2:
                            pe.wait_ge(gelued, b * NJ + j - 1)
                        nc.tensor.matmul(HP[:, j % 2, :], Qf[:, j * P:(j + 1) * P], c.xn[:, tokens(b)], start=True,
                                         stop=True).then_inc(h_ready, 1)
                        if j:
                            down(j - 1)
                    down(NJ - 1)

            @block.scalar
            def _(act):
                with act.Fori(0, B) as b:
                    nc.scalar.preload_act_table_set(GELU)
                    for j in range(NJ):
                        act.wait_ge(h_ready, b * NJ + j + 1)
                        nc.scalar.activation(h[:, j, :], HP[:, j % 2, :], ACT.Gelu).then_inc(gelued, 1)
                    nc.scalar.preload_act_table_set(LOG_EXP)
                    act.wait_ge(acc_ready, b + 1)
                    nc.scalar.activation(mu2[:, :], MU[:, :], ACT.Square, scale=1.0 / NJ).then_inc(mu_sq, 1)
                    act.wait_ge(var_made, b + 1)
                    nc.scalar.activation(lnv[:, :], v[:, :], ACT.Ln, bias=LN_EPS).then_inc(var_log, 1)
                    act.wait_ge(var_log, b + 1)
                    nc.scalar.activation(rstd[:, :], lnv[:, :], ACT.Exp, scale=-0.5).then_inc(rstd_ready, 1)
                    act.wait_ge(y_scaled, b + 1)
                    nc.scalar.activation(up[:, :], yn[:, :], ACT.Identity, bias=st[:, 8:9],
                                         scale=c.gates[:, gate:gate + 1]).then_inc(up_ready, 1)

            @block.vector
            def _(dve):
                with dve.Fori(0, B) as b:
                    for j in range(NJ):
                        dve.wait_ge(gelued, b * NJ + j + 1)
                        nc.vector.tensor_tensor(hs[:, j, :], h[:, j, :], h[:, j, :], ALU.mult).then_inc(squared, 1)
                    dve.wait_ge(mu_sq, b + 1)
                    nc.vector.scalar_tensor_tensor(out=v[:, :], in0=M2[:, :], scalar=1.0 / NJ, in1=mu2[:, :],
                                                   op0=ALU.mult, op1=ALU.subtract).then_inc(var_made, 1)
                    dve.wait_ge(rstd_ready, b + 1)
                    nc.vector.tensor_tensor(yn[:, :], Y[:, :], rstd[:, :], ALU.mult).then_inc(y_scaled, 1)
                    dve.wait_ge(up_ready, b + 1)
                    nc.vector.tensor_tensor(c.xT[:, tokens(b)], c.xT[:, tokens(b)], up[:, :], ALU.add)\
                        .then_inc(x_updated, 1)
                dve.wait_ge(x_updated, B)


def router(c, ctx, name, E, weight, bias=None, softmax=True):
    nc, d = c.nc, c.dram
    top = ctx.enter_context(nc.sbuf_tensor(name + "_top", [P, TILES, 8], F32))
    place = ctx.enter_context(nc.sbuf_tensor(name + "_place", [P, TILES, 8], F32))
    with ExitStack() as own:
        L = own.enter_context(nc.psum_tensor(name + "_L", [P, TILES * 64], F32))
        w = own.enter_context(nc.sbuf_tensor(name + "_w", [P, E], F32))
        bb = own.enter_context(nc.sbuf_tensor(name + "_bb", [P, E], F32))
        s = own.enter_context(nc.sbuf_tensor(name + "_s", [P, TILES, E], F32))
        e = own.enter_context(nc.sbuf_tensor(name + "_e", [P, TILES, E], F32))
        r = own.enter_context(nc.sbuf_tensor(name + "_r", [P, 3, TILES], F32))
        pl = own.enter_context(nc.sbuf_tensor(name + "_pl", [P, TILES, 8], U32))
        loaded, logits, made, exped, found = (c.sem(f"{name}_{n}") for n in ("loaded", "logits", "made", "exped", "found"))
        Lt = L[:, 0:TILES * E].rearrange("p (t e) -> p t e", t=TILES)
        nload = 32 if bias else 16

        def per_tile(i):
            return r[:, i, :].rearrange("p (t a) -> p t a", a=1).broadcast_to([P, TILES, E])

        with nc.Block() as block:
            @block.sync
            def _(sp):
                sp.dma_start(w[:, :], d[weight]).then_inc(loaded, 16)
                if bias:
                    sp.dma_start(bb[:, :], d[bias].partition_broadcast(P)).then_inc(loaded, 16)

            @block.tensor
            def _(pe):
                pe.wait_ge(loaded, nload)
                for t in range(TILES):
                    mm = nc.tensor.matmul(L[:, t * E:(t + 1) * E], c.xn[:, t * P:(t + 1) * P], w[:, :],
                                          start=True, stop=True)
                mm.then_inc(logits, 1)

            @block.scalar
            def _(act):
                if softmax:
                    nc.scalar.preload_act_table_set(LOG_EXP)
                    act.wait_ge(made, 2)
                    nc.scalar.activation(e[:, :, :], s[:, :, :], ACT.Exp).then_inc(exped, 1)

            @block.vector
            def _(dve):
                dve.wait_ge(loaded, nload)
                dve.wait_ge(logits, 1)
                if softmax:
                    nc.vector.tensor_reduce(r[:, 0, :], Lt, AX.X, ALU.max).then_inc(made, 1)
                    dve.wait_ge(made, 1)
                    nc.vector.tensor_tensor(s[:, :, :], Lt, per_tile(0), ALU.subtract).then_inc(made, 1)
                    dve.wait_ge(exped, 1)
                    nc.vector.tensor_reduce(r[:, 1, :], e[:, :, :], AX.X, ALU.add).then_inc(made, 1)
                    dve.wait_ge(made, 3)
                    nc.vector.reciprocal(r[:, 2, :], r[:, 1, :]).then_inc(made, 1)
                    dve.wait_ge(made, 4)
                    nc.vector.tensor_tensor(s[:, :, :], e[:, :, :], per_tile(2), ALU.mult).then_inc(made, 1)
                    dve.wait_ge(made, 5)
                else:
                    nc.vector.tensor_tensor(s[:, :, :], Lt, bb[:, :].rearrange("p (a e) -> p a e", a=1)
                                            .broadcast_to([P, TILES, E]), ALU.add).then_inc(made, 1)
                    dve.wait_ge(made, 1)
                for t in range(TILES):
                    nc.vector.max(out=top[:, t, :], in_=s[:, t, :]).then_inc(found, 1)
                dve.wait_ge(found, TILES)
                for t in range(TILES):
                    nc.vector.max_index(out=pl[:, t, :], in_max=top[:, t, :], in_values=s[:, t, :]).then_inc(found, 1)
                dve.wait_ge(found, 2 * TILES)
                nc.vector.tensor_copy(place[:, :, :], pl[:, :, :]).then_inc(found, 1)
                dve.wait_ge(found, 2 * TILES + 1)
    return top, place


def expert_weights(c, ctx, name, E, top, place, normalise):
    nc = c.nc
    wt = ctx.enter_context(nc.sbuf_tensor(name + "_wt", [P, TILES, P], F32))
    with ExitStack() as own:
        hot = own.enter_context(nc.sbuf_tensor(name + "_hot", [P, 2, TILES, E], F32))
        r = own.enter_context(nc.sbuf_tensor(name + "_nr", [P, 2, TILES], F32))
        ready = c.sem(name + "_weights")

        def col(a, k):
            return a[:, :, k:k + 1].broadcast_to([P, TILES, E])

        with nc.Block() as block:
            @block.vector
            def _(dve):
                n = 0

                def step(ins):
                    nonlocal n
                    n += 1
                    ins.then_inc(ready, 1)
                    dve.wait_ge(ready, n)

                step(nc.vector.memset(wt[:, :, :], 0.0))
                if normalise:
                    step(nc.vector.tensor_reduce(r[:, 0, :], top[:, :, 0:2], AX.X, ALU.add))
                    step(nc.vector.reciprocal(r[:, 1, :], r[:, 0, :]))
                    step(nc.vector.tensor_tensor(top[:, :, 0:2], top[:, :, 0:2], r[:, 1, :]
                                                 .rearrange("p (t a) -> p t a", a=1).broadcast_to([P, TILES, 2]),
                                                 ALU.mult))
                for k in range(2):
                    step(nc.vector.tensor_tensor(hot[:, k, :, :], c.iota[:, 0:E].rearrange("p (a e) -> p a e", a=1)
                                                 .broadcast_to([P, TILES, E]), col(place, k), ALU.is_equal))
                    step(nc.vector.tensor_tensor(hot[:, k, :, :], hot[:, k, :, :], col(top, k), ALU.mult))
                step(nc.vector.tensor_tensor(wt[:, :, 0:E], hot[:, 0, :, :], hot[:, 1, :, :], ALU.add))
    return wt


def dense_glu_moe(c, name, gate):
    nc, d = c.nc, c.dram
    E, F = 8, 352
    NJ = -(-F // P)
    U = E * NJ
    with ExitStack() as ctx, c.phase():
        top, place = router(c, ctx, name + "r", E, "F2_router")
        wt = expert_weights(c, ctx, name + "r", E, top, place, False)

        def sb(n, shape, dt=F32):
            return ctx.enter_context(nc.sbuf_tensor(f"{name}_{n}", shape, dt))

        def ps(n, shape):
            return ctx.enter_context(nc.psum_tensor(f"{name}_{n}", shape, F32))

        def sem(n):
            return c.sem(f"{name}_{n}")

        HP, VP, YP = (ps(n, [P, 2, S]) for n in ("HP", "VP", "YP"))
        TR = ps("TR", [P, S])
        W1, V1 = sb("W1", [P, E * F]), sb("V1", [P, E * F])
        W2 = sb("W2", [P, U, P])
        bias = sb("bias", [P, 2])
        gl, hv = sb("gl", [P, 2, S]), sb("hv", [P, 3, S])
        acc = sb("acc", [P, QT, P])
        wcur = sb("wcur", [P, QT, E])
        up = sb("up", [P, S])
        (loaded, bias_made, x_updated, up_ready, hv_ready, gelued, multiplied, down_done, y_ready, w_ready, y_added,
         turned) = (sem(n) for n in ("loaded", "bias_made", "x_updated", "up_ready", "hv_ready", "gelued",
                                     "multiplied", "down_done", "y_ready", "w_ready", "y_added", "turned"))

        def tokens(b):
            return bass.ds(b * S, S)

        def wide(j):
            return min(P, F - j * P)

        with nc.Block() as block:
            @block.sync
            def _(sp):
                for dst, src in ((W1[:, :], "F2_w1"), (V1[:, :], "F2_v1"), (W2[:, :, :], "F2_w2"),
                                 (bias[:, 0:1], "F2_bias")):
                    sp.dma_start(dst, d[src]).then_inc(loaded, 16)
                sp.wait_ge(loaded, 64)

            @block.tensor
            def _(pe):
                pe.wait_ge(loaded, 64)
                with pe.Fori(0, B) as b:
                    pe.wait_ge(x_updated, b)

                    def down(u):
                        e, j = u // NJ, u % NJ
                        if j == 0 and e >= 2:
                            pe.wait_ge(y_added, b * E * QT + (e - 1) * QT)
                        pe.wait_ge(multiplied, b * U + u + 1)
                        for q in range(QT):
                            mm = nc.tensor.matmul(YP[:, e % 2, q * P:(q + 1) * P],
                                                  hv[0:wide(j), u % 3, q * P:(q + 1) * P], W2[0:wide(j), u, :],
                                                  start=(j == 0 and q == 0), stop=(j == NJ - 1),
                                                  skip_group_check=True)
                        mm.then_inc(down_done, 1)

                    for u in range(U):
                        e, j = u // NJ, u % NJ
                        at = e * F + j * P
                        if u >= 2:
                            pe.wait_ge(multiplied, b * U + u - 1)
                        nc.tensor.matmul(HP[0:wide(j), u % 2, :], W1[:, at:at + wide(j)], c.xn[:, tokens(b)],
                                         start=True, stop=True)
                        nc.tensor.matmul(VP[0:wide(j), u % 2, :], V1[:, at:at + wide(j)], c.xn[:, tokens(b)],
                                         start=True, stop=True).then_inc(hv_ready, 1)
                        if u:
                            down(u - 1)
                    down(U - 1)
                    pe.wait_ge(y_added, b * E * QT + E * QT)
                    for q in range(QT):
                        mm = nc.tensor.transpose(TR[:, q * P:(q + 1) * P], acc[:, q, :], c.ident[:, :])
                    mm.then_inc(turned, 1)

            @block.scalar
            def _(act):
                nc.scalar.preload_act_table_set(GELU)
                act.wait_ge(bias_made, 1)
                with act.Fori(0, B) as b:
                    for u in range(U):
                        f = wide(u % NJ)
                        act.wait_ge(hv_ready, b * U + u + 1)
                        nc.scalar.activation(gl[0:f, u % 2, :], HP[0:f, u % 2, :], ACT.Gelu).then_inc(gelued, 1)
                    act.wait_ge(turned, b + 1)
                    nc.scalar.activation(up[:, :], TR[:, :], ACT.Identity, bias=bias[:, 1:2],
                                         scale=c.gates[:, gate:gate + 1]).then_inc(up_ready, 1)

            @block.vector
            def _(dve):
                dve.wait_ge(loaded, 64)
                nc.vector.tensor_tensor(bias[:, 1:2], bias[:, 0:1], c.gates[:, gate:gate + 1],
                                        ALU.mult).then_inc(bias_made, 1)
                with dve.Fori(0, B) as b:
                    dve.wait_ge(y_added, b * E * QT)
                    nc.vector.tensor_copy(wcur[:, :, :], wt[:, bass.ds(b * QT, QT), 0:E]).then_inc(w_ready, 1)
                    dve.wait_ge(w_ready, b + 1)

                    def add(e):
                        dve.wait_ge(down_done, b * U + (e + 1) * NJ)
                        if e:
                            dve.wait_ge(y_added, b * E * QT + e * QT)
                        for q in range(QT):
                            y = YP[:, e % 2, q * P:(q + 1) * P]
                            if e == 0:
                                ins = nc.vector.tensor_scalar(acc[:, q, :], y, wcur[:, q, 0:1], None, ALU.mult)
                            else:
                                ins = nc.vector.scalar_tensor_tensor(out=acc[:, q, :], in0=y,
                                                                     scalar=wcur[:, q, e:e + 1], in1=acc[:, q, :],
                                                                     op0=ALU.mult, op1=ALU.add)
                            ins.then_inc(y_added, 1)

                    for u in range(U):
                        f = wide(u % NJ)
                        dve.wait_ge(gelued, b * U + u + 1)
                        if u >= 3:
                            dve.wait_ge(down_done, b * U + u - 2)
                        nc.vector.tensor_tensor(hv[0:f, u % 3, :], gl[0:f, u % 2, :], VP[0:f, u % 2, :],
                                                ALU.mult).then_inc(multiplied, 1)
                        if u and u % NJ == 0:
                            add(u // NJ - 1)
                    add(E - 1)
                    dve.wait_ge(up_ready, b + 1)
                    nc.vector.tensor_tensor(c.xT[:, tokens(b)], c.xT[:, tokens(b)], up[:, :], ALU.add)\
                        .then_inc(x_updated, 1)
                dve.wait_ge(x_updated, B)


def shared_moe(c, name, gate):
    nc, d = c.nc, c.dram
    E, HID, SH = 16, 64, 256
    NE = E * HID // P
    U = NE + SH // P
    with ExitStack() as ctx, c.phase():
        top, place = router(c, ctx, name + "r", E, "F3_router")
        wt = expert_weights(c, ctx, name + "r", E, top, place, True)

        def sb(n, shape, dt=F32):
            return ctx.enter_context(nc.sbuf_tensor(f"{name}_{n}", shape, dt))

        def ps(n, shape):
            return ctx.enter_context(nc.psum_tensor(f"{name}_{n}", shape, F32))

        def sem(n):
            return c.sem(f"{name}_{n}")

        GP, UP, BP = (ps(n, [P, 2, S]) for n in ("GP", "UP", "BP"))
        YP = ps("YP", [P, S])
        Wg, Wu, Wd = sb("Wg", [P, U, P]), sb("Wu", [P, U, P]), sb("Wd", [P, U, P])
        wsg = sb("wsg", [P, P])
        pair = sb("pair", [P, NE, P])
        wT = sb("wT", [P, T])
        sig = sb("sig", [P, T])
        sl, hu, hw = sb("sl", [P, 2, S]), sb("hu", [P, 2, S]), sb("hw", [P, 2, S])
        loaded, turned, wt_copied, sg_ready, sg_made = (
            sem(n) for n in ("loaded", "turned", "wt_copied", "sg_ready", "sg_made"))
        with nc.Block() as block:
            @block.sync
            def _(sp):
                for dst, src in ((Wg[:, :, :], "F3_Wg"), (Wu[:, :, :], "F3_Wu"), (Wd[:, :, :], "F3_Wd"),
                                 (wsg[:, :], "F3_Wsg"), (pair[:, :, :], "pair")):
                    sp.dma_start(dst, d[src]).then_inc(loaded, 16)
                sp.wait_ge(loaded, 80)

            @block.tensor
            def _(pe):
                pe.wait_ge(loaded, 80)
                for b in range(B):
                    if b >= 2:
                        pe.wait_ge(wt_copied, b - 1)
                    for q in range(QT):
                        mm = nc.tensor.transpose(GP[:, b % 2, q * P:(q + 1) * P], wt[:, b * QT + q, :], c.ident[:, :])
                    mm.then_inc(turned, 1)
                    if b >= 2:
                        pe.wait_ge(sg_made, b - 1)
                    nc.tensor.matmul(UP[:, b % 2, :], wsg[:, :], c.xn[:, b * S:(b + 1) * S], start=True,
                                     stop=True).then_inc(sg_ready, 1)

            @block.vector
            def _(dve):
                for b in range(B):
                    dve.wait_ge(turned, b + 1)
                    nc.vector.tensor_copy(wT[:, b * S:(b + 1) * S], GP[:, b % 2, :]).then_inc(wt_copied, 1)
                dve.wait_ge(wt_copied, B)

            @block.scalar
            def _(act):
                for b in range(B):
                    act.wait_ge(sg_ready, b + 1)
                    nc.scalar.activation(sig[:, b * S:(b + 1) * S], UP[:, b % 2, :], ACT.Sigmoid).then_inc(sg_made, 1)
                act.wait_ge(sg_made, B)

        x_updated, gu_ready, silued, up_mult, gated, y_ready = (
            sem(n) for n in ("x_updated", "gu_ready", "silued", "up_mult", "gated", "y_ready"))

        def tokens(b):
            return bass.ds(b * S, S)

        with nc.Block() as block:
            @block.tensor
            def _(pe):
                with pe.Fori(0, B) as b:
                    pe.wait_ge(x_updated, b)

                    def down(u):
                        pe.wait_ge(gated, b * U + u + 1)
                        mm = nc.tensor.matmul(YP[:, :], Wd[:, u, :], hw[:, u % 2, :], start=(u == 0), stop=(u == U - 1))
                        mm.then_inc(y_ready, 1)

                    for u in range(U):
                        if u >= 2:
                            pe.wait_ge(gated, b * U + u - 1)
                        nc.tensor.matmul(GP[:, u % 2, :], Wg[:, u, :], c.xn[:, tokens(b)], start=True, stop=True)
                        mm = nc.tensor.matmul(UP[:, u % 2, :], Wu[:, u, :], c.xn[:, tokens(b)], start=True, stop=True)
                        if u < NE:
                            mm = nc.tensor.matmul(BP[:, u % 2, :], pair[:, u, :], wT[:, tokens(b)], start=True,
                                                  stop=True)
                        mm.then_inc(gu_ready, 1)
                        if u:
                            down(u - 1)
                    down(U - 1)

            @block.scalar
            def _(act):
                nc.scalar.preload_act_table_set("silu_and_others")
                with act.Fori(0, B) as b:
                    for u in range(U):
                        act.wait_ge(gu_ready, b * U + u + 1)
                        nc.scalar.activation(sl[:, u % 2, :], GP[:, u % 2, :], ACT.Silu).then_inc(silued, 1)

            @block.vector
            def _(dve):
                with dve.Fori(0, B) as b:
                    for u in range(U):
                        dve.wait_ge(silued, b * U + u + 1)
                        nc.vector.tensor_tensor(hu[:, u % 2, :], sl[:, u % 2, :], UP[:, u % 2, :],
                                                ALU.mult).then_inc(up_mult, 1)
                        dve.wait_ge(up_mult, b * U + u + 1)
                        if u >= 2:
                            dve.wait_ge(y_ready, b * U + u - 1)
                        nc.vector.tensor_tensor(hw[:, u % 2, :], hu[:, u % 2, :],
                                                BP[:, u % 2, :] if u < NE else sig[:, tokens(b)],
                                                ALU.mult).then_inc(gated, 1)
                    dve.wait_ge(y_ready, b * U + U)
                    nc.vector.scalar_tensor_tensor(out=c.xT[:, tokens(b)], in0=YP[:, :],
                                                   scalar=c.gates[:, gate:gate + 1], in1=c.xT[:, tokens(b)],
                                                   op0=ALU.mult, op1=ALU.add).then_inc(x_updated, 1)
                dve.wait_ge(x_updated, B)


def perceiver_attention(c, name, gate):
    nc, d = c.nc, c.dram
    NP, HD = 8, 64
    K = SK + S
    CUT = 295
    PIECES = ((0, CUT), (CUT, K))
    KC = [(0, SK)] + [(SK + P * i, SK + P * (i + 1)) for i in range(QT)]
    NC = len(KC)
    NT = 2 * NC
    NS = 2 * QT
    BASE = 512 - CUT
    with ExitStack() as ctx, c.phase():
        def sb(n, shape, dt=F32):
            return ctx.enter_context(nc.sbuf_tensor(f"{name}_{n}", shape, dt))

        def ps(n, shape):
            return ctx.enter_context(nc.psum_tensor(f"{name}_{n}", shape, F32))

        def sem(n):
            return c.sem(f"{name}_{n}")

        cn = sb("cn", [P, B * SK])
        layer_norm(c, name + "_nx", [(c.xT[:, s:s + S], c.xn[:, s:s + S], S) for s in range(0, T, S)])
        layer_norm(c, name + "_nl", [(c.xn[:, s:s + S], c.xn[:, s:s + S], S) for s in range(0, T, S)]
                   + [(c.ctxrep[:, :, 0:SK], cn[:, :], B * SK)])
        SP = ps("SP", [P, 2 * S])
        TP = ps("TP", [P, 2, S])
        PR = ps("PR", [P, 2, S])
        O, DEN = ps("O", [P, S]), ps("DEN", [P, S])
        Wq, Wk, Wv = (sb(n, [P, NP * P]) for n in ("Wq", "Wk", "Wv"))
        Wo = sb("Wo", [P, NP, P])
        vec = sb("vec", [P, 8])
        cv = sb("cv", [P, 2])
        blk = sb("blk", [P, P])
        sel2f, sel2 = sb("sel2f", [P, 2, P]), sb("sel2", [P, 2, P], BF16)
        onesf = sb("onesf", [P, HD])
        keym = sb("keym", [P, B * SK], I32)
        negQ = sb("negQ", [P, B, SK], BF16)
        rowm = sb("rowm", [P, B], I32)
        rowneg = sb("rowneg", [P, B])
        rowcur = sb("rowcur", [P, 1])
        kv = sb("kv", [P, K])
        V = sb("V", [P, NC, NP * P])
        sq, clip, lnn, rn = (sb(n, [P, S]) for n in ("sq", "clip", "lnn", "rn"))
        qn, qnb = sb("qn", [P, 2, S]), sb("qnb", [P, 2, S], BF16)
        kz, kzb = sb("kz", [P, 4, K]), sb("kzb", [P, 4, K], BF16)
        nm = sb("nm", [P, QT, P], BF16)
        negm = sb("negm", [P, 2, S], BF16)
        prob = sb("prob", [P, 6, S])
        lnd, rden, up = (sb(n, [P, S]) for n in ("lnd", "rden", "up"))
        on = sb("on", [P, NP, S])

        loaded, prep, affine, zeroed = sem("loaded"), sem("prep"), sem("affine"), sem("zeroed")
        loads = [(Wq[:, :], "A2_Wq"), (Wk[:, :], "A2_Wk"), (Wv[:, :], "A2_Wv"), (Wo[:, :, :], "A2_Wo"),
                 (vec[:, :], "A2_vec"), (blk[:, :], "blk64"), (sel2f[:, :, :], "sel2"), (rowm[0:SK, :], "rowmask2")]
        nload = 16 * (len(loads) + 1)
        with nc.Block() as block:
            @block.sync
            def _(sp):
                for dst, src in loads:
                    sp.dma_start(dst, d[src]).then_inc(loaded, 16)
                sp.dma_start(keym[:, :], d["keymask2"].partition_broadcast(P)).then_inc(loaded, 16)
                sp.wait_ge(loaded, nload)

            @block.scalar
            def _(act):
                act.wait_ge(loaded, nload)
                for s in range(0, T, S):
                    nc.scalar.activation(c.xn[:, s:s + S], c.xn[:, s:s + S], ACT.Identity, bias=vec[:, 3:4],
                                         scale=vec[:, 2:3]).then_inc(affine, 1)
                nc.scalar.activation(cn[:, :], cn[:, :], ACT.Identity, bias=vec[:, 1:2],
                                     scale=vec[:, 0:1]).then_inc(affine, 1)
                act.wait_ge(affine, B + 1)

            @block.vector
            def _(dve):
                dve.wait_ge(loaded, nload)
                nc.vector.memset(nm[:, :, :], 0.0).then_inc(prep, 1)
                nc.vector.memset(onesf[:, :], 1.0).then_inc(prep, 1)
                nc.vector.tensor_copy(sel2[:, :, :], sel2f[:, :, :]).then_inc(prep, 1)
                nc.vector.tensor_scalar(negQ[:, :, :], keym[:, :].rearrange("p (b k) -> p b k", b=B), -NEG / P, NEG / P,
                                        ALU.mult, ALU.add).then_inc(prep, 1)
                nc.vector.tensor_scalar(rowneg[0:SK, :], rowm[0:SK, :], -NEG, NEG, ALU.mult, ALU.add).then_inc(prep, 1)
                nc.vector.tensor_scalar(cv[:, 0:1], vec[:, 4:5], HD ** -0.5, None, ALU.mult).then_inc(prep, 1)
                nc.vector.tensor_tensor(cv[:, 1:2], vec[:, 6:7], c.gates[:, gate:gate + 1], ALU.mult).then_inc(prep, 1)
                dve.wait_ge(prep, 7)

            @block.gpsimd
            def _(pool):
                nc.gpsimd.memset(kz[:, :, :], 0.0).then_inc(zeroed, 1)
                nc.gpsimd.memset(kzb[:, :, :], 0.0).then_inc(zeroed, 1)
                pool.wait_ge(zeroed, 2)

        (x_updated, kv_copied, v_ready, v_copied, pr_ready, squared, ms_ready, clipped, n_log, n_rms, normed, cast,
         s_ready, s_used, nm_turned, negm_ready, t_ready, p_ready, pv_done, den_log, den_ready, o_normed, y_ready,
         up_ready, row_copied) = (sem(n) for n in (
            "x_updated", "kv_copied", "v_ready", "v_copied", "pr_ready", "squared", "ms_ready", "clipped", "n_log",
            "n_rms", "normed", "cast", "s_ready", "s_used", "nm_turned", "negm_ready", "t_ready", "p_ready",
            "pv_done", "den_log", "den_ready", "o_normed", "y_ready", "up_ready",
            "row_copied"))
        turned = PR[:, 1, 0:S // 2].bitcast(BF16)

        def tokens(b):
            return bass.ds(b * S, S)

        def width(m):
            return S if m == 0 else PIECES[m - 1][1] - PIECES[m - 1][0]

        NN, M = 5, 3
        after_piece = (1, 3, 5)

        with nc.Block() as block:
            @block.tensor
            def _(pe):
                with pe.Fori(0, B) as b:
                    def project(p, m):
                        if m == 0 and p:
                            pe.wait_ge(negm_ready, b * NP + p)
                        if m or p:
                            pe.wait_ge(normed, (b * NP + p) * NN + (after_piece[m - 1] if m else 0))
                        w = Wq if m == 0 else Wk
                        rhs = c.xn[:, tokens(b)] if m == 0 else kv[:, PIECES[m - 1][0]:PIECES[m - 1][1]]
                        nc.tensor.matmul(PR[:, 0, 0:width(m)], w[:, p * P:(p + 1) * P], rhs, start=True,
                                         stop=True).then_inc(pr_ready, 1)

                    def squares(p, m):
                        pe.wait_ge(squared, (b * NP + p) * M + m + 1)
                        nc.tensor.matmul(PR[:, 1, 0:width(m)], blk[:, :], sq[:, 0:width(m)], start=True,
                                         stop=True).then_inc(ms_ready, 1)

                    def maxima(p, u):
                        h, q = u // QT, u % QT
                        s = 2 * (p % 2) + h
                        if u == 0:
                            pe.wait_ge(cast, (b * NP + p) * 3 + 3)
                        if u or p:
                            pe.wait_ge(s_used, (b * NP + p) * NS + u)
                        lhs = qnb[:, p % 2, q * P:(q + 1) * P]
                        nc.tensor.matmul(SP[:, BASE:512], lhs, kzb[:, s, 0:CUT], start=True, stop=False)
                        nc.tensor.matmul(SP[:, BASE:BASE + SK], c.onesb[:, :], negQ[:, bass.ds(b, 1), :], start=False,
                                         stop=True)
                        nc.tensor.matmul(SP[:, 512:BASE + K], lhs, kzb[:, s, CUT:K], start=True,
                                         stop=True).then_inc(s_ready, 1)

                    def turn(p):
                        pe.wait_ge(s_used, (b * NP + p + 1) * NS)
                        for q in range(QT):
                            mm = nc.tensor.transpose(turned[:, q * P:(q + 1) * P], nm[:, q, :], c.identb[:, :])
                        mm.then_inc(nm_turned, 1)

                    def scores(p, t):
                        kc, h = t // 2, t % 2
                        lo, hi = KC[kc]
                        if t == 0:
                            pe.wait_ge(negm_ready, b * NP + p + 1)
                        if t >= 2 or p:
                            pe.wait_ge(p_ready, (b * NP + p) * NT + t - 1)
                        out = TP[0:hi - lo, t % 2, :]
                        nc.tensor.matmul(out, kz[:, 2 * (p % 2) + h, lo:hi], qn[:, p % 2, :], start=True, stop=False)
                        nc.tensor.matmul(out, sel2[:, h, 0:hi - lo], negm[:, p % 2, :], start=False,
                                         stop=True).then_inc(t_ready, 1)

                    def values(p, kc):
                        n = KC[kc][1] - KC[kc][0]
                        if kc == 0 and p:
                            pe.wait_ge(o_normed, b * NP + p)
                        pe.wait_ge(p_ready, (b * NP + p) * NT + 2 * kc + 2)
                        first, last = kc == 0, kc == NC - 1
                        for h in range(2):
                            nc.tensor.matmul(O[HD * h:HD * h + HD, :], V[0:n, kc, p * P + HD * h:p * P + HD * h + HD],
                                             prob[0:n, (2 * kc + h) % 6, :], start=first, stop=last)
                        for h in range(2):
                            mm = nc.tensor.matmul(DEN[HD * h:HD * h + HD, :], onesf[0:n, :],
                                                  prob[0:n, (2 * kc + h) % 6, :], start=first, stop=last)
                        mm.then_inc(pv_done, 1)

                    pe.wait_ge(kv_copied, 2 * b + 2)
                    pe.wait_ge(x_updated, b)
                    for kc, (lo, hi) in enumerate(KC):
                        for half in range(2):
                            i = 2 * kc + half
                            if i >= 2:
                                pe.wait_ge(v_copied, b * 2 * NC + i - 1)
                            nc.tensor.matmul(TP[0:hi - lo, half, :], kv[:, lo:hi], Wv[:, half * S:(half + 1) * S],
                                             start=True, stop=True).then_inc(v_ready, 1)
                    for m in range(M):
                        project(0, m)
                        squares(0, m)
                    for u in range(NS):
                        maxima(0, u)
                    turn(0)
                    pe.wait_ge(v_copied, (b + 1) * 2 * NC)
                    for p in range(NP):
                        more = p + 1 < NP
                        for t in range(NT):
                            scores(p, t)
                            if more:
                                if t in (0, 2, 4):
                                    project(p + 1, t // 2)
                                if t in (1, 3, 5):
                                    squares(p + 1, t // 2)
                                if t >= 6:
                                    maxima(p + 1, 2 * (t - 6))
                                    maxima(p + 1, 2 * (t - 6) + 1)
                            if t >= 3 and t % 2:
                                values(p, t // 2 - 1)
                        values(p, NC - 1)
                        if more:
                            turn(p + 1)
                    pe.wait_ge(o_normed, (b + 1) * NP)
                    for p in range(NP):
                        mm = nc.tensor.matmul(PR[:, 0, :], Wo[:, p, :], on[:, p, :], start=(p == 0), stop=(p == NP - 1))
                    mm.then_inc(y_ready, 1)

            @block.scalar
            def _(act):
                nc.scalar.preload_act_table_set(LOG_EXP)
                with act.Fori(0, B) as b:
                    def square(p, m):
                        i = (b * NP + p) * M + m
                        act.wait_ge(pr_ready, i + 1)
                        nc.scalar.activation(sq[:, 0:width(m)], PR[:, 0, 0:width(m)], ACT.Square).then_inc(squared, 1)

                    def rms(p, m):
                        i = (b * NP + p) * M + m
                        act.wait_ge(clipped, i + 1)
                        nc.scalar.activation(lnn[:, 0:width(m)], clip[:, 0:width(m)], ACT.Ln).then_inc(n_log, 1)
                        act.wait_ge(n_log, i + 1)
                        nc.scalar.activation(rn[:, 0:width(m)], lnn[:, 0:width(m)], ACT.Exp,
                                             scale=-0.5).then_inc(n_rms, 1)

                    act.wait_ge(x_updated, b)
                    nc.scalar.copy(kv[:, 0:SK], cn[:, bass.ds(b * SK, SK)]).then_inc(kv_copied, 1)
                    nc.scalar.copy(kv[:, SK:K], c.xn[:, tokens(b)]).then_inc(kv_copied, 1)
                    nc.scalar.copy(rowcur[0:SK, :], rowneg[0:SK, bass.ds(b, 1)]).then_inc(row_copied, 1)
                    act.wait_ge(row_copied, b + 1)
                    for m in range(M):
                        square(0, m)
                        rms(0, m)
                    for p in range(NP):
                        more = p + 1 < NP
                        for t in range(NT):
                            kc, h = t // 2, t % 2
                            n = KC[kc][1] - KC[kc][0]
                            act.wait_ge(t_ready, (b * NP + p) * NT + t + 1)
                            if t >= 6:
                                act.wait_ge(pv_done, (b * NP + p) * NC + (t - 6) // 2 + 1)
                            elif p:
                                act.wait_ge(pv_done, (b * NP + p) * NC)
                            nc.scalar.activation(prob[0:n, t % 6, :], TP[0:n, t % 2, :], ACT.Exp,
                                                 bias=rowcur[0:n, :] if kc == 0 else 0.0).then_inc(p_ready, 1)
                            if more:
                                if t in (0, 2, 4):
                                    square(p + 1, t // 2)
                                if t in (1, 3, 5):
                                    rms(p + 1, t // 2)
                        act.wait_ge(pv_done, (b * NP + p + 1) * NC)
                        nc.scalar.activation(lnd[:, :], DEN[:, :], ACT.Ln).then_inc(den_log, 1)
                        act.wait_ge(den_log, b * NP + p + 1)
                        nc.scalar.activation(rden[:, :], lnd[:, :], ACT.Exp, scale=-1.0).then_inc(den_ready, 1)
                    act.wait_ge(y_ready, b + 1)
                    nc.scalar.activation(up[:, :], PR[:, 0, :], ACT.Identity, bias=cv[:, 1:2],
                                         scale=c.gates[:, gate:gate + 1]).then_inc(up_ready, 1)

            @block.vector
            def _(dve):
                with dve.Fori(0, B) as b:
                    def normalise(p, m):
                        i = (b * NP + p) * M + m
                        n = width(m)
                        dve.wait_ge(ms_ready, i + 1)
                        nc.vector.tensor_scalar(clip[:, 0:n], PR[:, 1, 0:n], 1.0 / HD, 1e-16, ALU.mult,
                                                ALU.max).then_inc(clipped, 1)
                        dve.wait_ge(n_rms, i + 1)
                        if m == 0:
                            nc.vector.scalar_tensor_tensor(out=qn[:, p % 2, :], in0=PR[:, 0, :], scalar=cv[:, 0:1],
                                                           in1=rn[:, :], op0=ALU.mult, op1=ALU.mult).then_inc(normed, 1)
                            return
                        lo, hi = PIECES[m - 1]
                        for h in range(2):
                            r = slice(HD * h, HD * h + HD)
                            nc.vector.scalar_tensor_tensor(out=kz[r, 2 * (p % 2) + h, lo:hi], in0=PR[r, 0, 0:n],
                                                           scalar=vec[r, 5:6], in1=rn[r, 0:n], op0=ALU.mult,
                                                           op1=ALU.mult).then_inc(normed, 1)

                    def reduce(p, u):
                        h, q = u // QT, u % QT
                        dve.wait_ge(s_ready, (b * NP + p) * NS + u + 1)
                        nc.vector.tensor_reduce(nm[:, q, h:h + 1], SP[:, BASE:BASE + K], AX.X, ALU.max,
                                                negate=True).then_inc(s_used, 1)

                    def shift(p):
                        dve.wait_ge(nm_turned, b * NP + p + 1)
                        nc.vector.tensor_copy(negm[:, p % 2, :], turned).then_inc(negm_ready, 1)

                    dve.wait_ge(x_updated, b)
                    for kc, (lo, hi) in enumerate(KC):
                        for half in range(2):
                            i = b * 2 * NC + 2 * kc + half
                            dve.wait_ge(v_ready, i + 1)
                            nc.vector.tensor_copy(V[0:hi - lo, kc, half * S:(half + 1) * S],
                                                  TP[0:hi - lo, half, :]).then_inc(v_copied, 1)
                    for m in range(M):
                        normalise(0, m)
                    for u in range(NS):
                        reduce(0, u)
                    shift(0)
                    for p in range(NP):
                        more = p + 1 < NP
                        if more:
                            for m in range(M):
                                normalise(p + 1, m)
                            for u in range(NS):
                                reduce(p + 1, u)
                        dve.wait_ge(den_ready, b * NP + p + 1)
                        nc.vector.tensor_tensor(on[:, p, :], O[:, :], rden[:, :], ALU.mult).then_inc(o_normed, 1)
                        if more:
                            shift(p + 1)
                    dve.wait_ge(up_ready, b + 1)
                    nc.vector.tensor_tensor(c.xT[:, tokens(b)], c.xT[:, tokens(b)], up[:, :], ALU.add)\
                        .then_inc(x_updated, 1)
                dve.wait_ge(x_updated, B)

            @block.gpsimd
            def _(pool):
                with pool.Fori(0, B) as b:
                    for p in range(NP):
                        base = (b * NP + p) * NN
                        pool.wait_ge(normed, base + 1)
                        nc.gpsimd.tensor_tensor(qnb[:, p % 2, :], qn[:, p % 2, :],
                                                onesf[:, 0:1].broadcast_to([P, S]),
                                                ALU.mult).then_inc(cast, 1)
                        for h in range(2):
                            r = slice(HD * h, HD * h + HD)
                            pool.wait_ge(normed, base + NN)
                            pool.wait_ge(cast, (b * NP + p) * 3 + h + 1)
                            k = kz[r, 2 * (p % 2) + h, :]
                            nc.gpsimd.tensor_tensor(kzb[r, 2 * (p % 2) + h, :], k, onesf[r, 0:1].broadcast_to([HD, K]),
                                                    ALU.mult).then_inc(cast, 1)
                pool.wait_ge(cast, B * NP * 3)


class ExpertRing:
    SLOTS = 8
    PAIRS = 32

    def __init__(self, c, ctx):
        R = self.SLOTS
        self.w1 = ctx.enter_context(c.nc.sbuf_tensor("ring_w1", [P, R, 8 * P], F32))
        self.w2 = ctx.enter_context(c.nc.sbuf_tensor("ring_w2", [P, R, 8 * P], F32))
        self.loaded = [c.sem(f"ring_loaded{i}") for i in range(R)]
        self.w1_dram, self.w2_dram = c.dram["F1_w1"], c.dram["F1_w2"]

    def load(self, sp, slot, pair):
        for dst, src in ((self.w1, self.w1_dram), (self.w2, self.w2_dram)):
            sp.dma_start(dst[:, slot, :], src[bass.ds(pair, 1), :, :].rearrange("a p n -> p (a n)")).then_inc(self.loaded[slot], 16)


def first_expert_loads(c, ring):
    c.disp = c.nc.dram_tensor("dispatched", [4096 + 3 * T, D], F32, kind="Internal").ap()
    c.rows_zeroed = c.sem("rows_zeroed")
    with c.nc.Block() as block:
        @block.sync
        def _(sp):
            sp.dma_start(c.disp[0:4096, :].rearrange("(p q) d -> p (q d)", p=P), c.dram["zeros"])\
                .then_inc(c.rows_zeroed, 16)
            for i in range(ring.SLOTS):
                ring.load(sp, i, i)


def capacity_moe(c, name, gate, ring):
    nc, d = c.nc, c.dram
    E, TOPK, CAP = 64, 3, 64
    PAIRS, R = ring.PAIRS, ring.SLOTS
    SLOTS = E * CAP
    G = 4
    ydram = nc.dram_tensor("expert_out", [SLOTS, D], F32, kind="Internal").ap()
    with ExitStack() as ctx, c.phase():
        top, place = router(c, ctx, name + "r", E, "F1_router", bias="F1_router_b", softmax=False)

        def sb(n, shape, dt=F32):
            return ctx.enter_context(nc.sbuf_tensor(f"{name}_{n}", shape, dt))

        def sem(n):
            return c.sem(f"{name}_{n}")

        gk = sb("gk", [P, TOPK, TILES])
        slot_in, slot_out = sb("slot_in", [P, TOPK * TILES], U32), sb("slot_out", [P, TOPK * TILES], U32)
        xs = sb("xs", [P, PAIRS, D])
        b2 = sb("b2", [P, PAIRS * D])
        b1 = sb("b1", [P, PAIRS * 8])
        bufT = sb("bufT", [P, SLOTS])
        zeroed, scattered, b_loaded = sem("zeroed"), sem("scattered"), sem("b_loaded")

        with ExitStack() as own:
            def tmp(n, shape, dt=F32):
                return own.enter_context(nc.sbuf_tensor(f"{name}_{n}", shape, dt))
            hot = tmp("hot", [P, TOPK, TILES, E])
            OH, run = tmp("OH", [P, TILES, E], BF16), tmp("run", [P, TILES, E], BF16)
            upper, upperb = tmp("upper", [P, P]), tmp("upperb", [P, P], BF16)
            prod = tmp("prod", [P, TILES, E])
            pos, valid, ge, trash, sf = (tmp(n, [P, TOPK, TILES]) for n in ("pos", "valid", "ge", "trash", "sf"))
            gs = tmp("gs", [P, 2, TILES])
            xtok = tmp("xtok", [P, TILES, D])
            PS = own.enter_context(nc.psum_tensor(name + "_PS", [P, TILES * E], F32))
            XP = own.enter_context(nc.psum_tensor(name + "_XP", [P, 2, S], F32))
            loaded, hots, counted, exped, turned, tok_ready, slots = (
                sem(n) for n in ("loaded", "hots", "counted", "exped", "turned", "tok_ready", "slots"))
            hots_done = []
            with nc.Block() as block:
                @block.sync
                def _(sp):
                    sp.dma_start(upper[:, :], d["upper"]).then_inc(loaded, 16)
                    sp.dma_start(trash[:, :, :], d["trash"]).then_inc(loaded, 16)
                    sp.dma_start(b2[:, :], d["F1_b2"]).then_inc(b_loaded, 16)
                    sp.dma_start(b1[:, :], d["F1_b1"]).then_inc(b_loaded, 16)

                @block.vector
                def _(dve):
                    n = 0

                    def step(ins):
                        nonlocal n
                        n += 1
                        ins.then_inc(hots, 1)
                        dve.wait_ge(hots, n)

                    def over(a, k):
                        return a[:, :, k:k + 1].broadcast_to([P, TILES, E])

                    for k in range(TOPK):
                        step(nc.vector.tensor_tensor(hot[:, k, :, :], c.iota[:, :].rearrange("p (a e) -> p a e", a=1)
                                                     .broadcast_to([P, TILES, E]), over(place, k), ALU.is_equal))
                    step(nc.vector.tensor_tensor(prod[:, :, :], hot[:, 0, :, :], hot[:, 1, :, :], ALU.add))
                    step(nc.vector.tensor_tensor(OH[:, :, :], prod[:, :, :], hot[:, 2, :, :], ALU.add))
                    step(nc.vector.memset(run[:, 0, :], 0.0))
                    for t in range(1, TILES):
                        step(nc.vector.tensor_tensor(run[:, t, :], run[:, t - 1, :], OH[:, t - 1, :], ALU.add))
                    dve.wait_ge(loaded, 32)
                    step(nc.vector.tensor_copy(upperb[:, :], upper[:, :]))
                    hots_done.append(n)
                    step(nc.vector.tensor_tensor(ge[:, :, :].rearrange("p k t -> p t k"), top[:, :, 0:TOPK],
                                                 top[:, :, 0:1].broadcast_to([P, TILES, TOPK]), ALU.subtract))
                    hots_done.append(n)
                    dve.wait_ge(counted, 1)
                    for k in range(TOPK):
                        step(nc.vector.tensor_tensor(prod[:, :, :], hot[:, k, :, :],
                                                     PS[:, :].rearrange("p (t e) -> p t e", t=TILES), ALU.mult))
                        step(nc.vector.tensor_reduce(pos[:, k, :], prod[:, :, :], AX.X, ALU.add))
                    step(nc.vector.tensor_scalar(valid[:, :, :], pos[:, :, :], float(CAP), None, ALU.is_lt))
                    step(nc.vector.tensor_scalar(pos[:, :, :], pos[:, :, :], float(CAP - 1), None, ALU.min))
                    step(nc.vector.scalar_tensor_tensor(out=pos[:, :, :], in0=place[:, :, 0:TOPK]
                                                        .rearrange("p t k -> p k t"), scalar=float(CAP),
                                                        in1=pos[:, :, :], op0=ALU.mult, op1=ALU.add))
                    step(nc.vector.tensor_copy(slot_out[:, :].rearrange("p (k t) -> p k t", k=TOPK), pos[:, :, :]))
                    step(nc.vector.tensor_tensor(sf[:, :, :], pos[:, :, :], trash[:, :, :], ALU.subtract))
                    step(nc.vector.tensor_tensor(sf[:, :, :], sf[:, :, :], valid[:, :, :], ALU.mult))
                    step(nc.vector.tensor_tensor(sf[:, :, :], sf[:, :, :], trash[:, :, :], ALU.add))
                    nc.vector.tensor_copy(slot_in[:, :].rearrange("p (k t) -> p k t", k=TOPK),
                                          sf[:, :, :]).then_inc(slots, 1)
                    dve.wait_ge(exped, 1)
                    step(nc.vector.tensor_reduce(gs[:, 0, :], gk[:, :, :].rearrange("p k t -> p t k"), AX.X, ALU.add))
                    step(nc.vector.reciprocal(gs[:, 1, :], gs[:, 0, :]))
                    step(nc.vector.tensor_tensor(gk[:, :, :], gk[:, :, :], gs[:, 1:2, :]
                                                 .broadcast_to([P, TOPK, TILES]), ALU.mult))
                    step(nc.vector.tensor_tensor(gk[:, :, :], gk[:, :, :], valid[:, :, :], ALU.mult))

                @block.tensor
                def _(pe):
                    for g in range(G):
                        if g >= 2:
                            pe.wait_ge(tok_ready, g - 1)
                        for q in range(QT):
                            t = g * QT + q
                            mm = nc.tensor.transpose(XP[:, g % 2, q * P:(q + 1) * P], c.xn[:, t * P:(t + 1) * P],
                                                     c.ident[:, :])
                        mm.then_inc(turned, 1)
                    pe.wait_ge(hots, 21 + 1)
                    for t in range(TILES):
                        nc.tensor.matmul(PS[:, t * E:(t + 1) * E], upperb[:, :], OH[:, t, :], start=True, stop=False)
                        mm = nc.tensor.matmul(PS[:, t * E:(t + 1) * E], c.onesb[:, :], run[:, t, :], start=False,
                                              stop=True)
                    mm.then_inc(counted, 1)

                @block.scalar
                def _(act):
                    nc.scalar.preload_act_table_set(LOG_EXP)
                    for g in range(G):
                        act.wait_ge(turned, g + 1)
                        nc.scalar.copy(xtok[:, g * QT:(g + 1) * QT, :], XP[:, g % 2, :]
                                       .rearrange("p (q d) -> p q d", q=QT)).then_inc(tok_ready, 1)
                    act.wait_ge(hots, 21 + 2)
                    nc.scalar.activation(gk[:, :, :], ge[:, :, :], ACT.Exp).then_inc(exped, 1)

                @block.gpsimd
                def _(pool):
                    pool.wait_ge(slots, 1)
                    pool.wait_ge(tok_ready, G)
                    pool.wait_ge(c.rows_zeroed, 16)
                    for t in range(TILES):
                        for k in range(TOPK):
                            i = k * TILES + t
                            nc.gpsimd.indirect_dma_start(
                                out=c.disp[:, :], out_offset=bass.IndirectOffsetOnAxis(ap=slot_in[:, i:i + 1], axis=0),
                                in_=xtok[:, t, :], in_offset=None).then_inc(scattered, 16)
                    pool.wait_ge(scattered, 16 * TILES * TOPK)
            assert hots_done == [22, 23]

        HP = ctx.enter_context(nc.psum_tensor(name + "_HP", [P, 2, 512], F32))
        YP = ctx.enter_context(nc.psum_tensor(name + "_YP", [P, 2, 512], F32))
        XT = ctx.enter_context(nc.psum_tensor(name + "_XT", [P, 2, 512], F32))
        hb, hg = sb("hb", [P, 2, 512]), sb("hg", [P, 2, 512])
        (rows_in, rows_turned, buf_ready, h_ready, b_added, gelued, y_ready, y_kept, stored) = (
            sem(n) for n in ("rows_in", "rows_turned", "buf_ready", "h_ready", "b_added", "gelued", "y_ready",
                             "y_kept", "stored"))
        rows = [sem(f"rows{i}") for i in range(4)]
        with nc.Block() as block:
            @block.sync
            def _(sp):
                for i in range(4):
                    sp.dma_start(xs[:, 8 * i:8 * i + 8, :], c.disp[1024 * i:1024 * (i + 1), :]
                                 .rearrange("(q p) d -> p q d", p=P)).then_inc(rows[i], 16)

            @block.tensor
            def _(pe):
                for g in range(PAIRS // 4):
                    if g % 2 == 0:
                        pe.wait_ge(rows[g // 2], 16)
                    if g >= 2:
                        pe.wait_ge(buf_ready, g - 1)
                    for q in range(4):
                        mm = nc.tensor.transpose(XT[:, g % 2, q * P:(q + 1) * P], xs[:, 4 * g + q, :], c.ident[:, :])
                    mm.then_inc(rows_turned, 1)

            @block.scalar
            def _(act):
                for g in range(PAIRS // 4):
                    act.wait_ge(rows_turned, g + 1)
                    nc.scalar.copy(bufT[:, g * 512:(g + 1) * 512], XT[:, g % 2, :]).then_inc(buf_ready, 1)
                act.wait_ge(buf_ready, PAIRS // 4)

        ys = xs
        with nc.Block() as block:
            @block.sync
            def _(sp):
                def store(it):
                    sp.wait_ge(y_kept, (it + 1) * R)
                    sp.dma_start(ydram[bass.ds(it * (R * P), R * P), :].rearrange("(q p) d -> p q d", p=P),
                                 ys[:, bass.ds(it * R, R), :]).then_inc(stored, 16)

                with sp.Fori(0, PAIRS // R - 1) as it:
                    for i in range(R):
                        sp.wait_ge(y_ready, it * R + i + 1)
                        ring.load(sp, i, (it + 1) * R + i)
                    store(it)
                store(PAIRS // R - 1)
                sp.wait_ge(stored, 16 * (PAIRS // R))

            @block.tensor
            def _(pe):
                with pe.Fori(0, PAIRS // R) as it:
                    def up(i):
                        n = it * R + i
                        pe.wait_ge(ring.loaded[i], 32 * it + 32)
                        if i >= 2:
                            pe.wait_ge(b_added, n - 1)
                        else:
                            pe.wait_ge(b_added, it * R)
                        for e in range(2):
                            for j in range(4):
                                m = 4 * e + j
                                mm = nc.tensor.matmul(HP[:, i % 2, m * CAP:(m + 1) * CAP],
                                                      ring.w1[:, i, m * P:(m + 1) * P],
                                                      bufT[:, bass.ds(n * 2 * CAP + e * CAP, CAP)],
                                                      start=True, stop=True)
                        mm.then_inc(h_ready, 1)

                    def down(i):
                        n = it * R + i
                        pe.wait_ge(gelued, n + 1)
                        if i >= 2:
                            pe.wait_ge(y_kept, n - 1)
                        else:
                            pe.wait_ge(y_kept, it * R)
                        for j in range(4):
                            for e in range(2):
                                m = 4 * e + j
                                mm = nc.tensor.matmul(YP[CAP * e:CAP * e + CAP, i % 2, 0:D],
                                                      hg[:, i % 2, m * CAP:(m + 1) * CAP],
                                                      ring.w2[:, i, m * P:(m + 1) * P],
                                                      start=(j == 0), stop=(j == 3))
                        mm.then_inc(y_ready, 1)

                    for i in range(R):
                        up(i)
                        if i:
                            down(i - 1)
                    down(R - 1)

            @block.vector
            def _(dve):
                dve.wait_ge(b_loaded, 32)
                with dve.Fori(0, PAIRS // R) as it:
                    def add(i):
                        n = it * R + i
                        dve.wait_ge(h_ready, n + 1)
                        if i >= 2:
                            dve.wait_ge(gelued, n - 1)
                        else:
                            dve.wait_ge(gelued, it * R)
                        nc.vector.tensor_tensor(
                            hb[:, i % 2, :].rearrange("p (m s) -> p m s", m=8),
                            HP[:, i % 2, :].rearrange("p (m s) -> p m s", m=8),
                            b1[:, bass.ds(n * 8, 8)].rearrange("p (m a) -> p m a", a=1).broadcast_to([P, 8, CAP]),
                            ALU.add).then_inc(b_added, 1)

                    def keep(i):
                        n = it * R + i
                        dve.wait_ge(y_ready, n + 1)
                        nc.vector.tensor_tensor(ys[:, bass.ds(n, 1), :].rearrange("p a d -> p (a d)"),
                                                YP[:, i % 2, 0:D], b2[:, bass.ds(n * D, D)],
                                                ALU.add).then_inc(y_kept, 1)

                    for i in range(R):
                        add(i)
                        if i:
                            keep(i - 1)
                    keep(R - 1)

            @block.scalar
            def _(act):
                nc.scalar.preload_act_table_set(GELU)
                with act.Fori(0, PAIRS // R) as it:
                    for i in range(R):
                        n = it * R + i
                        act.wait_ge(b_added, n + 1)
                        if i >= 2:
                            act.wait_ge(y_ready, n - 1)
                        else:
                            act.wait_ge(y_ready, it * R)
                        nc.scalar.activation(hg[:, i % 2, :], hb[:, i % 2, :], ACT.Gelu).then_inc(gelued, 1)

        with ExitStack() as own:
            yg = own.enter_context(nc.sbuf_tensor(name + "_yg", [P, TOPK * TILES, D], F32))
            acc = own.enter_context(nc.sbuf_tensor(name + "_acc", [P, TILES, D], F32))
            TR = own.enter_context(nc.psum_tensor(name + "_TR", [P, 2, S], F32))
            gathered = [sem(f"gathered{g}") for g in range(G)]
            summed, back, x_updated = sem("summed"), sem("back"), sem("x_updated")
            with nc.Block() as block:
                @block.gpsimd
                def _(pool):
                    for t in range(TILES):
                        for k in range(TOPK):
                            i = k * TILES + t
                            nc.gpsimd.indirect_dma_start(
                                out=yg[:, i, :], out_offset=None, in_=ydram[:, :],
                                in_offset=bass.IndirectOffsetOnAxis(ap=slot_out[:, i:i + 1], axis=0))\
                                .then_inc(gathered[t // QT], 16)

                @block.vector
                def _(dve):
                    for g in range(G):
                        dve.wait_ge(gathered[g], 16 * TOPK * QT)
                        for k in range(TOPK):
                            if k:
                                dve.wait_ge(summed, (g * TOPK + k) * QT)
                            for q in range(QT):
                                t = g * QT + q
                                y = yg[:, k * TILES + t, :]
                                if k == 0:
                                    ins = nc.vector.tensor_scalar(acc[:, t, :], y, gk[:, k, t:t + 1], None, ALU.mult)
                                else:
                                    ins = nc.vector.scalar_tensor_tensor(out=acc[:, t, :], in0=y,
                                                                         scalar=gk[:, k, t:t + 1], in1=acc[:, t, :],
                                                                         op0=ALU.mult, op1=ALU.add)
                                ins.then_inc(summed, 1)
                        dve.wait_ge(back, g + 1)
                        nc.vector.scalar_tensor_tensor(out=c.xT[:, g * S:(g + 1) * S], in0=TR[:, g % 2, :],
                                                       scalar=c.gates[:, gate:gate + 1], in1=c.xT[:, g * S:(g + 1) * S],
                                                       op0=ALU.mult, op1=ALU.add).then_inc(x_updated, 1)
                    dve.wait_ge(x_updated, G)

                @block.tensor
                def _(pe):
                    for g in range(G):
                        pe.wait_ge(summed, (g + 1) * TOPK * QT)
                        if g >= 2:
                            pe.wait_ge(x_updated, g - 1)
                        for q in range(QT):
                            mm = nc.tensor.transpose(TR[:, g % 2, q * P:(q + 1) * P], acc[:, g * QT + q, :],
                                                     c.ident[:, :])
                        mm.then_inc(back, 1)


def flamingo_kernel(nc, dram, out):
    with ExitStack() as ctx:
        c = Core(nc, ctx, dram)
        load_shared(c)
        with ExitStack() as until_moe:
            ring = ExpertRing(c, until_moe)
            first_expert_loads(c, ring)
            norm_x(c, "n0")
            head_attention(c, "a0", 0, "L0_Wq", "L0_Wk", "L0_Wv", bq=True, bk=True, bv=True, mask=True)
            norm_x(c, "n1")
            ternary_ffn(c, "f0", 4)
            norm_x(c, "n2")
            head_attention(c, "a1", 1, "L1_Wq", "L1_Wk", "L1_Wv", bq=True, bk=True, bv=True, wo="L1_Wo", bo=True,
                           relbias=True)
            norm_x(c, "n3")
            capacity_moe(c, "f1", 5, ring)
        perceiver_attention(c, "a2", 2)
        norm_x(c, "n5")
        dense_glu_moe(c, "f2", 6)
        norm_x(c, "n6")
        head_attention(c, "a3", 3, "L3_Wq", "L3_Wk", "L3_Wv", wo="L3_Wo", rope=True)
        norm_x(c, "n7")
        shared_moe(c, "f3", 7)
        stored = c.sem("stored")
        with nc.Block() as block:
            @block.sync
            def _(sp):
                sp.dma_start(out, c.xT[:, :]).then_inc(stored, 16)
                sp.wait_ge(stored, 16)
def shape_constants():
    f = np.float32
    k = {}
    k["center"] = (np.eye(P) - 1.0 / P).astype(f)
    k["mean"] = np.full((P, P), 1.0 / P, f)
    k["ident"] = np.eye(P, dtype=f)
    d = np.arange(P)
    k["headmask"] = (d[:, None] // DH == np.arange(H)[None]).astype(f)
    row = np.arange(CH * CR)
    rm = ((row[:, None] // SK == np.arange(32)[None] // DH) & (row[:, None] < ROWS)).astype(f)
    k["rowmask"] = np.zeros((P, CH, 32), f)
    k["rowmask"][:CR] = rm.reshape(CH, CR, 32).transpose(1, 0, 2)
    k["self"] = (d[:, None] == np.arange(QUAD * ROWS)[None] // SK).astype(f)
    k["blk8"] = (d[:, None] // DH == d[None] // DH).astype(f)
    k["blk64"] = (d[:, None] // 64 == d[None] // 64).astype(f)

    def rope(n, theta):
        freqs = f(theta) ** (-np.arange(0, DH, 2, dtype=f) / f(DH))
        ang = np.arange(n, dtype=f)[:, None] * freqs[None]
        half = d % DH % (DH // 2)
        sign = np.where(d % DH < DH // 2, -1.0, 1.0).astype(f)
        return np.cos(ang)[:, half].T.astype(f), (np.sin(ang)[:, half].T * sign[:, None]).astype(f)

    k["qcs"] = np.stack(rope(S, 32.0), 1)
    kc, ks = rope(SK, 1000.0)
    k["kcs"] = np.stack([np.tile(kc[:, ::-1], (1, B)), np.tile(ks[:, ::-1], (1, B))], 1)
    k["zeros"] = np.zeros((P, 32 * P), f)
    k["trash"] = (4096 + np.arange(3)[None, :, None] * T + np.arange(TILES)[None, None] * P + d[:, None, None]).astype(f)
    k["iota"] = np.tile(np.arange(64, dtype=f), (P, 1))
    k["pair"] = (d[:, None, None] == 2 * np.arange(8)[None, :, None] + d[None, None] // 64).astype(f)
    k["sel2"] = (d[:, None, None] == np.arange(2)[None, :, None] + 0 * d[None, None]).astype(f)
    k["upper"] = (d[:, None] < d[None]).astype(f)
    return k


def layout(i):
    a = {n: np.asarray(v) for n, v in i.items()}
    f = np.float32
    o = {"xT": a["x"].reshape(T, D).T}
    ctxT = a["ctx_1024"].transpose(2, 0, 1)[:, :, ::-1]
    o["ctxrep"] = np.tile(ctxT, (1, 1, HQ))
    o["gates"] = np.tile(np.concatenate([a["g_xattn"], a["g_ffn"]])[None], (P, 1))

    def vectors(**cols):
        v = np.zeros((P, 8), f)
        for n, col in cols.items():
            v[:, int(n[1])] = col
        return v

    def reps(w):
        return np.tile(w, H)

    half = DH // 2
    partner = np.arange(P) // DH * DH + (np.arange(P) % DH + half) % DH
    for n in ("Wq", "Wk", "Wv"):
        o[f"L0_{n}"] = a[f"L0_xattn_{n}"].T
        o[f"L1_{n}"] = a[f"L1_xattn_{n}"]
        o[f"L3_{n}"] = a[f"L3_xattn_{n}"].T
    o["L1_Wo"], o["L3_Wo"] = a["L1_xattn_Wo"], a["L3_xattn_Wo"].T
    o["L3_Wq_p"], o["L3_Wk_p"] = o["L3_Wq"][:, partner], o["L3_Wk"][:, partner]
    o["a0_vec"] = vectors(c0=a["L0_xattn_bq"], c1=a["L0_xattn_bk"], c2=a["L0_xattn_bv"])
    o["a1_vec"] = vectors(c0=a["L1_xattn_bq"], c1=a["L1_xattn_bk"], c2=a["L1_xattn_bv"], c3=a["L1_xattn_bo"],
                          c4=np.repeat(a["L1_xattn_logit_scale"], DH))
    qw, kw = reps(a["L3_xattn_q_norm_w"]), reps(a["L3_xattn_k_norm_w"])
    o["a3_vec"] = vectors(c4=kw, c5=kw[partner], c6=qw, c7=qw[partner])
    m = a["mask_BxSxS2_ff1"][:, :, ::-1]
    mt = np.zeros((B, CH * CR, S), f)
    mt[:, :ROWS] = np.tile(m.transpose(0, 2, 1), (1, HQ, 1))
    o["maskT"] = mt.reshape(B * CH, CR, S).transpose(1, 0, 2)
    o["maskQ"] = m.reshape(B * QT, P, SK).transpose(1, 0, 2)

    def words(m):
        w = np.zeros(m.shape + (4,), np.uint8)
        w[..., 0] = m
        return w.view(np.int32)[..., 0]

    km = words(a["mask_BxS2_bf0"][:, ::-1])
    o["keymask"] = km.reshape(B * SK)
    rk = np.zeros((B, CH * CR), np.int32)
    rk[:, :ROWS] = np.tile(km, (1, HQ))
    o["rowkeymask"] = rk.reshape(B * CH, CR).T
    key = SK - 1 - np.arange(SK)
    rel = np.clip(key[None] - np.arange(S)[:, None], -128, 128) + 128
    bias = a["L1_xattn_bias_table"][rel].transpose(2, 1, 0)
    bt = np.zeros((QUAD, CH * CR, S), f)
    bt[:, :ROWS] = bias.reshape(QUAD, ROWS, S)
    o["biasT"] = bt.reshape(QUAD * CH, CR, S).transpose(1, 0, 2)
    o["biasQ"] = bias.reshape(H * SK, S).T[:3 * P].reshape(3, P, H * SK).transpose(1, 0, 2)

    def hidden_rows(w):
        return w.reshape(-1, P, w.shape[-1]).transpose(1, 0, 2)

    o["F0_W1"] = a["L0_ffn_W_fc"].T
    o["F0_W2"] = hidden_rows(a["L0_ffn_W_proj"].T).reshape(P, -1)
    o["F0_ln"] = np.concatenate([a[f"L0_ffn_ln_{n}"].reshape(-1, P).T for n in "wb"], 1)
    o["F2_router"] = a["L2_ffn_router_w"]
    for n in ("w1", "v1"):
        o[f"F2_{n}"] = a[f"L2_ffn_{n}"].transpose(1, 0, 2).reshape(P, -1)
    w2 = np.zeros((8, 3 * P, P), f)
    w2[:, :352] = a["L2_ffn_w2"]
    o["F2_w2"] = hidden_rows(w2.reshape(-1, P))
    o["F2_bias"] = a["L2_ffn_bias"].reshape(P, 1)
    o["F3_router"] = a["L3_ffn_Wg"].T
    for n, e, s in (("Wg", "We_gate", "Ws_gate"), ("Wu", "We_up", "Ws_up")):
        w = np.concatenate([a[f"L3_ffn_{e}"].reshape(-1, P), a[f"L3_ffn_{s}"]])
        o[f"F3_{n}"] = w.T.reshape(P, -1, P)
    wd = np.concatenate([a["L3_ffn_We_down"].transpose(0, 2, 1).reshape(-1, P), a["L3_ffn_Ws_down"].T])
    o["F3_Wd"] = hidden_rows(wd)
    o["F3_Wsg"] = np.tile(a["L3_ffn_Wsg"].T, (1, P))
    o["F1_router"], o["F1_router_b"] = a["L1_ffn_gate_w"], a["L1_ffn_gate_b"]
    o["F1_w1"] = a["L1_ffn_w1"].reshape(32, 2, P, 512).transpose(0, 2, 1, 3).reshape(32, P, 1024)
    o["F1_w2"] = a["L1_ffn_w2"].reshape(32, 8, P, P).transpose(0, 2, 1, 3).reshape(32, P, 1024)
    o["F1_b1"] = a["L1_ffn_b1"].reshape(32 * 8, P).T
    o["F1_b2"] = np.repeat(a["L1_ffn_b2"].reshape(32, 2, P).transpose(1, 0, 2).reshape(2, 32 * P), 64, axis=0)
    o["A2_Wq"] = a["L2_xattn_Wq"]
    o["A2_Wk"], o["A2_Wv"] = a["L2_xattn_Wkv"][:, :1024], a["L2_xattn_Wkv"][:, 1024:]
    o["A2_Wo"] = hidden_rows(a["L2_xattn_Wout"])
    o["A2_vec"] = vectors(c0=a["L2_xattn_ln_x_g"], c1=a["L2_xattn_ln_x_b"], c2=a["L2_xattn_ln_l_g"],
                          c3=a["L2_xattn_ln_l_b"], c4=np.tile(a["L2_xattn_qn_g"], 2),
                          c5=np.tile(a["L2_xattn_kn_g"], 2), c6=a["L2_xattn_bout"])
    km2 = words(a["mask_BxS2_bf1"][:, ::-1])
    o["keymask2"], o["rowmask2"] = km2.reshape(B * SK), km2.T
    return o


def kernel(**inputs):
    import numpy as _np
    import concourse.bacc as _bacc
    from concourse import mybir as _mybir
    from concourse.bass_utils import run_bass_kernel_spmd as _run

    nc = _bacc.Bacc("TRN2", target_bir_lowering=False, num_devices=1)
    arrays, dram = {}, {}
    for name, a in {**layout(inputs), **shape_constants()}.items():
        a = _np.ascontiguousarray(a)
        arrays[f"in_{name}"] = a
        dram[name] = nc.dram_tensor(f"in_{name}", a.shape, _mybir.dt.from_np(a.dtype), kind="ExternalInput").ap()
    out = nc.dram_tensor("out_xT", (P, T), F32, kind="ExternalOutput").ap()
    flamingo_kernel(nc, dram, out)
    r = _run(nc, [arrays], core_ids=[0])
    return _np.ascontiguousarray(r.results[0]["out_xT"].T).reshape(B, S, D)
```

```python
from contextlib import ExitStack, contextmanager

import concourse.bass as bass
import numpy as np
from concourse import mybir

F32 = mybir.dt.float32
BF16 = mybir.dt.bfloat16
I32 = mybir.dt.int32
U32 = mybir.dt.uint32
ALU = mybir.AluOpType
ACT = mybir.ActivationFunctionType
AX = mybir.AxisListType

B, S, D = 4, 512, 128
T = B * S
P = 128
TILES = T // P
QT = S // P
SK = 77
H, DH = 16, 8
QUAD, HQ = 4, 4
ROWS = HQ * SK
CH = 3
CR = -(-ROWS // CH)
NEG = -131072.0
LN_EPS = 1e-5
LOG_EXP = "natural_log_exp_and_others"
GELU = "gelu_and_others"


def rows_of(i):
    return min(CR, ROWS - i * CR)


class Core:

    def __init__(self, nc, ctx, dram):
        self.nc, self.ctx, self.dram = nc, ctx, dram
        self.phases = []

    def sem(self, name):
        if self.phases:
            self.phases[-1].append(self.nc.alloc_semaphore(name))
            return self.phases[-1][-1]
        return self.ctx.enter_context(self.nc.semaphore(name))

    @contextmanager
    def phase(self):
        self.phases.append([])
        yield
        self.nc.clear_and_free_semaphores(self.phases.pop())
        self.nc.all_engine_barrier()

    def keep(self, name, shape, dt=F32):
        return self.ctx.enter_context(self.nc.sbuf_tensor(name, shape, dt))


def load_shared(c):
    nc, d = c.nc, c.dram
    c.xT = c.keep("xT", [P, T])
    c.xn = c.keep("xn", [P, T])
    c.center = c.keep("center", [P, P])
    c.mean = c.keep("mean", [P, P])
    c.ident = c.keep("ident", [P, P])
    c.identb = c.keep("identb", [P, P], BF16)
    c.onesb = c.keep("onesb", [P, P], BF16)
    c.headmask = c.keep("headmask", [P, H])
    c.rowmask = c.keep("rowmask", [P, CH, 32])
    c.sel = c.keep("sel", [P, QUAD * ROWS], BF16)
    c.self = c.keep("self", [P, QUAD * ROWS])
    c.ctxrep = c.keep("ctxrep", [P, B, ROWS])
    c.iota = c.keep("iota", [P, 64])
    c.gates = c.keep("gates", [P, 8])
    loaded, got, x_in = c.sem("shared_loaded"), c.sem("shared_cast"), c.sem("x_loaded")
    with nc.Block() as block:
        @block.sync
        def _(sp):
            sp.dma_start(c.xT[:, :], d["xT"]).then_inc(x_in, 16)
            for dst, src in ((c.center, "center"), (c.mean, "mean"), (c.ident, "ident"), (c.gates, "gates"),
                             (c.headmask, "headmask"), (c.self, "self"), (c.iota, "iota")):
                sp.dma_start(dst[:, :], d[src]).then_inc(loaded, 16)
            sp.dma_start(c.rowmask[:, :, :], d["rowmask"]).then_inc(loaded, 16)
            sp.dma_start(c.ctxrep[:, :, :], d["ctxrep"]).then_inc(loaded, 16)
            sp.wait_ge(x_in, 16)
            sp.wait_ge(loaded, 9 * 16)

        @block.scalar
        def _(act):
            act.wait_ge(loaded, 9 * 16)
            nc.scalar.activation(c.gates[:, :], c.gates[:, :], ACT.Tanh).then_inc(got, 1)

        @block.vector
        def _(dve):
            dve.wait_ge(loaded, 9 * 16)
            nc.vector.tensor_copy(c.identb[:, :], c.ident[:, :]).then_inc(got, 1)
            nc.vector.tensor_copy(c.sel[:, :], c.self[:, :]).then_inc(got, 1)
            nc.vector.memset(c.onesb[:, :], 1.0).then_inc(got, 1)
            dve.wait_ge(got, 4)


def layer_norm(c, name, pieces, loads=None, scratch=None, eps=LN_EPS):
    nc = c.nc
    n = len(pieces)
    with ExitStack() as ctx, c.phase():
        cen = ctx.enter_context(nc.psum_tensor(name + "_cen", [P, 4, 512], F32))
        var = ctx.enter_context(nc.psum_tensor(name + "_var", [P, 4, 512], F32))
        if scratch is None:
            scratch = ctx.enter_context(nc.sbuf_tensor(name + "_scratch", [P, 6, 512], F32))
        sq, lnv, rstd = scratch[:, 0:2, :], scratch[:, 2:4, :], scratch[:, 4:6, :]
        centred, squared, var_ready, logged, rstd_ready, normed = (
            c.sem(f"{name}_{s}") for s in ("centred", "squared", "var_ready", "logged", "rstd_ready", "normed"))
        with nc.Block() as block:
            if loads:
                @block.sync
                def _(sp):
                    loads(sp)

            @block.tensor
            def _(pe):
                def variance(i):
                    w = pieces[i][2]
                    pe.wait_ge(squared, i + 1)
                    nc.tensor.matmul(var[:, i % 4, :w], c.mean[:, :], sq[:, i % 2, :w],
                                     start=True, stop=True).then_inc(var_ready, 1)

                for i, (src, _, w) in enumerate(pieces):
                    if i >= 4:
                        pe.wait_ge(normed, i - 3)
                    nc.tensor.matmul(cen[:, i % 4, :w], c.center[:, :], src,
                                     start=True, stop=True).then_inc(centred, 1)
                    if i >= 1:
                        variance(i - 1)
                variance(n - 1)

            @block.scalar
            def _(act):
                def scale(i):
                    w = pieces[i][2]
                    act.wait_ge(var_ready, i + 1)
                    if i >= 2:
                        act.wait_ge(normed, i - 1)
                    nc.scalar.activation(lnv[:, i % 2, :w], var[:, i % 4, :w], ACT.Ln, bias=eps).then_inc(logged, 1)
                    act.wait_ge(logged, i + 1)
                    nc.scalar.activation(rstd[:, i % 2, :w], lnv[:, i % 2, :w], ACT.Exp,
                                         scale=-0.5).then_inc(rstd_ready, 1)

                nc.scalar.preload_act_table_set(LOG_EXP)
                for i, (_, _, w) in enumerate(pieces):
                    act.wait_ge(centred, i + 1)
                    if i >= 2:
                        act.wait_ge(var_ready, i - 1)
                    nc.scalar.activation(sq[:, i % 2, :w], cen[:, i % 4, :w], ACT.Square).then_inc(squared, 1)
                    if i >= 1:
                        scale(i - 1)
                scale(n - 1)

            @block.vector
            def _(dve):
                for i, (_, dst, w) in enumerate(pieces):
                    dve.wait_ge(rstd_ready, i + 1)
                    nc.vector.tensor_tensor(dst, cen[:, i % 4, :w], rstd[:, i % 2, :w], ALU.mult).then_inc(normed, 1)
                dve.wait_ge(normed, n)


def norm_x(c, name, loads=None, scratch=None):
    layer_norm(c, name, [(c.xT[:, s:s + S], c.xn[:, s:s + S], S) for s in range(0, T, S)], loads, scratch)


def head_attention(c, name, gate, wq, wk, wv, bq=None, bk=None, bv=None, wo=None, bo=None,
                   mask=False, relbias=False, rope=False):
    nc, d = c.nc, c.dram
    with ExitStack() as ctx, c.phase():
        def sb(n, shape, dt=F32):
            return ctx.enter_context(nc.sbuf_tensor(f"{name}_{n}", shape, dt))

        def ps(n, shape):
            return ctx.enter_context(nc.psum_tensor(f"{name}_{n}", shape, F32))

        def sem(n):
            return c.sem(f"{name}_{n}")

        Wq, Wk, Wv = sb("Wq", [P, P]), sb("Wk", [P, P]), sb("Wv", [P, P])
        vec = sb("vec", [P, 8])
        cv = sb("cv", [P, 4])
        kT = sb("kT", [P, B * SK])
        vexp = sb("vexp", [P, B, CH * P])
        kexp = sb("kexp", [P, QUAD * ROWS])
        kexpb = sb("kexpb", [P, QUAD * ROWS], BF16)
        kcur = sb("kcur", [P, SK])
        vcur = sb("vcur", [P, CH * P])
        qT = sb("qT", [P, T])
        qb = sb("qb", [P, S], BF16)
        nm = sb("nm", [P, QT, P], BF16)
        negm = sb("negm", [P, T], BF16)
        prob = sb("prob", [P, 8, 512])
        lnd = sb("lnd", [P, S])
        rden = sb("rden", [P, S])
        on = sb("on", [P, S])
        up = sb("up", [P, S])
        if wo:
            Wo = sb("Wo", [P, P])
            on2 = sb("on2", [P, S])
        if mask or relbias:
            added = sb("added", [P, 2, 512])
        if mask:
            maskT = sb("maskT", [P, B * CH, S])
            maskQ = sb("maskQ", [P, B * QT, SK])
            maskQb = sb("maskQb", [P, B * QT, SK], BF16)
        if relbias:
            biasT = sb("biasT", [P, QUAD * CH, S])
            biasQ = sb("biasQ", [P, 3, QUAD * ROWS])
            biasQb = sb("biasQb", [P, 3, QUAD * ROWS], BF16)
            keym = sb("keym", [P, B * SK], I32)
            negQ = sb("negQ", [P, B, SK], BF16)
            keep = sb("keep", [P, B * SK])
            rowm = sb("rowm", [P, B * CH], I32)
            rowkeep = sb("rowkeep", [P, B, 2 * CH])
            rowcur = sb("rowcur", [P, 2 * CH])
        if rope:
            Wqp, Wkp = sb("Wqp", [P, P]), sb("Wkp", [P, P])
            blk8 = sb("blk8", [P, P])
            qcs = sb("qcs", [P, 2, S])
            kcs = sb("kcs", [P, 2, B * SK])
            rsq, rln, rr, ra, rb = (sb(n, [P, S]) for n in ("rsq", "rln", "rr", "ra", "rb"))

        loaded, prep, kproj, kready, vproj, vready = (
            sem(n) for n in ("loaded", "prep", "kproj", "kready", "vproj", "vready"))
        x_updated, vec_done, expscale = sem("x_updated"), sem("vec_done"), sem("expscale")

        loads = [(Wq[:, :], d[wq]), (Wk[:, :], d[wk]), (Wv[:, :], d[wv]), (vec[:, :], d[name + "_vec"])]
        if wo:
            loads.append((Wo[:, :], d[wo]))
        if mask:
            loads += [(maskT[0:CR, :, :], d["maskT"]), (maskQ[:, :, :], d["maskQ"])]
        if relbias:
            loads += [(keym[:, :], d["keymask"].partition_broadcast(P)), (rowm[0:CR, :], d["rowkeymask"])]
        if rope:
            loads += [(Wqp[:, :], d[wq + "_p"]), (Wkp[:, :], d[wk + "_p"]), (blk8[:, :], d["blk8"]),
                      (qcs[:, :, :], d["qcs"]), (kcs[:, :, :], d["kcs"])]
        nload = 16 * len(loads)
        bq_loaded, bq_cast, bt_loaded = sem("biasq_loaded"), sem("biasq_cast"), sem("biast_loaded")

        def start_loads(sp):
            if relbias:
                sp.dma_start(biasQ[:, :, :], d["biasQ"]).then_inc(bq_loaded, 16)
            for dst, src in loads:
                sp.dma_start(dst, src).then_inc(loaded, 16)
            if relbias:
                sp.dma_start(biasT[0:CR, :, :], d["biasT"]).then_inc(bt_loaded, 16)

        norm_x(c, name + "_n", start_loads, prob)
        A = ps("A", [P, 4, 512])
        TP = ps("TP", [P, 2, 512])
        O = ps("O", [P, 512])
        DEN = ps("DEN", [P, 512])
        with nc.Block() as block:
            @block.tensor
            def _(pe):
                pe.wait_ge(loaded, nload)
                ctxall = c.ctxrep[:, :, 0:SK]
                nc.tensor.matmul(DEN[:, 0:B * SK], Wk[:, :], ctxall, start=True, stop=True).then_inc(kproj, 1)
                if rope:
                    nc.tensor.matmul(O[:, 0:B * SK], Wkp[:, :], ctxall, start=True, stop=True).then_inc(kproj, 1)
                    pe.wait_ge(prep, 1)
                    nc.tensor.matmul(A[:, 0, 0:B * SK], blk8[:, :], rsq[:, 0:B * SK],
                                     start=True, stop=True).then_inc(kproj, 1)
                for b in range(B):
                    if b >= 2:
                        pe.wait_ge(vready, b - 1)
                    for i in range(CH):
                        mm = nc.tensor.matmul(TP[0:rows_of(i), b % 2, i * P:(i + 1) * P],
                                              c.ctxrep[:, b, i * CR:i * CR + rows_of(i)], Wv[:, :],
                                              start=True, stop=True)
                    mm.then_inc(vproj, 1)

            @block.scalar
            def _(act):
                nc.scalar.preload_act_table_set(LOG_EXP)
                act.wait_ge(loaded, nload)
                if relbias:
                    nc.scalar.activation(cv[:, 3:4], vec[:, 4:5], ACT.Exp).then_inc(expscale, 1)
                if rope:
                    act.wait_ge(kproj, 1)
                    nc.scalar.activation(rsq[:, 0:B * SK], DEN[:, 0:B * SK], ACT.Square).then_inc(prep, 1)
                    act.wait_ge(kproj, 3)
                    nc.scalar.activation(rln[:, 0:B * SK], A[:, 0, 0:B * SK], ACT.Ln, bias=1e-6,
                                         scale=1.0 / DH).then_inc(prep, 1)
                    act.wait_ge(prep, 2)
                    nc.scalar.activation(rr[:, 0:B * SK], rln[:, 0:B * SK], ACT.Exp, scale=-0.5).then_inc(prep, 1)
                else:
                    act.wait_ge(kproj, 1)
                    nc.scalar.activation(kT[:, :], DEN[:, 0:B * SK], ACT.Identity, bias=vec[:, 1:2]).then_inc(prep, 1)

            @block.vector
            def _(dve):
                dve.wait_ge(loaded, nload)
                nc.vector.memset(nm[:, :, :], 0.0).then_inc(kready, 1)
                nc.vector.memset(vexp[:, :, :], 0.0).then_inc(vec_done, 1)
                if relbias:
                    dve.wait_ge(expscale, 1)
                    nc.vector.tensor_scalar(cv[:, 0:1], cv[:, 3:4], 4.0, DH ** -0.5, ALU.min,
                                            ALU.mult).then_inc(vec_done, 1)
                else:
                    nc.vector.memset(cv[:, 0:1], DH ** -0.5).then_inc(vec_done, 1)
                dve.wait_ge(vec_done, 2)
                nc.vector.tensor_tensor(cv[:, 1:2], vec[:, 0:1], cv[:, 0:1], ALU.mult).then_inc(vec_done, 1)
                nc.vector.tensor_tensor(cv[:, 2:3], vec[:, 3:4] if wo else vec[:, 2:3], c.gates[:, gate:gate + 1],
                                        ALU.mult).then_inc(vec_done, 1)
                dve.wait_ge(vec_done, 4)
                if rope:
                    dve.wait_ge(kproj, 2)
                    dve.wait_ge(prep, 1)
                    nc.vector.scalar_tensor_tensor(out=ra[:, 0:B * SK], in0=DEN[:, 0:B * SK], scalar=vec[:, 4:5],
                                                   in1=kcs[:, 0, :], op0=ALU.mult, op1=ALU.mult).then_inc(kready, 1)
                    nc.vector.scalar_tensor_tensor(out=rb[:, 0:B * SK], in0=O[:, 0:B * SK], scalar=vec[:, 5:6],
                                                   in1=kcs[:, 1, :], op0=ALU.mult, op1=ALU.mult).then_inc(kready, 1)
                    dve.wait_ge(kready, 3)
                    nc.vector.tensor_tensor(kT[:, :], ra[:, 0:B * SK], rb[:, 0:B * SK], ALU.add).then_inc(kready, 1)
                    dve.wait_ge(kready, 4)
                    dve.wait_ge(prep, 3)
                    nc.vector.tensor_tensor(kT[:, :], kT[:, :], rr[:, 0:B * SK], ALU.mult).then_inc(kready, 1)
                    dve.wait_ge(kready, 5)
                if relbias:
                    nc.vector.tensor_scalar(keep[:, :], keym[:, :], -1.0, 1.0, ALU.mult, ALU.add).then_inc(kready, 1)
                    nc.vector.tensor_scalar(negQ[:, :, :], keym[:, :].rearrange("p (b k) -> p b k", b=B), NEG / P,
                                            None, ALU.mult).then_inc(kready, 1)
                    rows = rowm[0:CR, :].rearrange("p (b i) -> p b i", b=B)
                    nc.vector.tensor_scalar(rowkeep[0:CR, :, 0:CH], rows, -1.0, 1.0, ALU.mult,
                                            ALU.add).then_inc(kready, 1)
                    nc.vector.tensor_scalar(rowkeep[0:CR, :, CH:], rows, NEG, None, ALU.mult).then_inc(kready, 1)
                    dve.wait_ge(kready, 5)
                    dve.wait_ge(prep, 1)
                    nc.vector.tensor_tensor(kT[:, :], kT[:, :], keep[:, :], ALU.mult).then_inc(kready, 1)
                    dve.wait_ge(kready, 6)
                if mask:
                    nc.vector.tensor_scalar(maskQb[:, :, :], maskQ[:, :, :], 1e4, -1e4, ALU.mult,
                                            ALU.add).then_inc(kready, 1)
                    nc.vector.tensor_scalar(maskT[0:CR, :, :], maskT[0:CR, :, :], 1e4, -1e4, ALU.mult,
                                            ALU.add).then_inc(kready, 1)
                    dve.wait_ge(kready, 3)
                for b in range(B):
                    dve.wait_ge(vproj, b + 1)
                    for i in range(CH):
                        r = rows_of(i)
                        ins = nc.vector.tensor_tensor(
                            vexp[0:r, b, i * P:(i + 1) * P].rearrange("p (g e) -> p g e", g=QUAD),
                            TP[0:r, b % 2, i * P:(i + 1) * P].rearrange("p (g e) -> p g e", g=QUAD),
                            c.rowmask[0:r, i:i + 1, :].broadcast_to([r, QUAD, 32]), ALU.mult)
                    ins.then_inc(vready, 1)
                dve.wait_ge(vready, B)

            @block.gpsimd
            def _(pool):
                if relbias:
                    pool.wait_ge(bq_loaded, 16)
                    nc.gpsimd.tensor_copy(biasQb[:, 0:1, :], biasQ[:, 0:1, :]).then_inc(bq_cast, 1)
                    nc.gpsimd.tensor_copy(biasQb[:, 1:3, :], biasQ[:, 1:3, :]).then_inc(bq_cast, 1)
                    pool.wait_ge(bq_cast, 2)

        (q_proj, q_sq, q_ms, q_log, q_rms, q_made, q_cast, k_cur, kb_made, k_made, row_made, v_copied, s_ready,
         s_used, nm_turned, negm_ready, t_ready, t_added, p_ready, pv_done, den_log, den_ready, o_normed, o_biased,
         y_ready, up_ready) = (sem(n) for n in (
            "q_proj", "q_sq", "q_ms", "q_log", "q_rms", "q_made", "q_cast", "k_cur", "kb_made", "k_made", "row_made",
            "v_copied", "s_ready", "s_used", "nm_turned", "negm_ready", "t_ready", "t_added", "p_ready", "pv_done",
            "den_log", "den_ready", "o_normed", "o_biased", "y_ready", "up_ready"))
        U = QUAD * CH
        NS = 2 * QT
        FIRST = U - NS
        NQ = 4 if rope else 1
        NP = 2 if rope else 1
        adds = mask or relbias
        turned = A[:, 0, 0:S // 2].bitcast(BF16)

        def tokens(b):
            return bass.ds(b * S, S)

        with nc.Block() as block:
            @block.tensor
            def _(pe):
                def project(b):
                    nc.tensor.matmul(A[:, 0, :], Wq[:, :], c.xn[:, tokens(b)], start=True, stop=True)\
                        .then_inc(q_proj, 1)
                    if rope:
                        nc.tensor.matmul(A[:, 1, :], Wqp[:, :], c.xn[:, tokens(b)], start=True, stop=True)\
                            .then_inc(q_proj, 1)

                def squares(b):
                    pe.wait_ge(q_sq, b + 1)
                    nc.tensor.matmul(A[:, 2, :], blk8[:, :], rsq[:, :], start=True, stop=True).then_inc(q_ms, 1)

                def maxima(b, u):
                    qt, half = u // 2, u % 2
                    if u == 0:
                        pe.wait_ge(q_cast, b + 1)
                        pe.wait_ge(kb_made, b + 1)
                    if u >= 2:
                        pe.wait_ge(s_used, b * NS + u - 1)
                    for j in range(2):
                        g = 2 * half + j
                        out = A[:, 2 * (u % 2) + j, 0:ROWS]
                        out3 = out.rearrange("p (h k) -> p h k", h=HQ)
                        mm = nc.tensor.matmul(out, qb[:, qt * P:(qt + 1) * P],
                                              kexpb[:, g * ROWS:(g + 1) * ROWS], start=True, stop=not adds)
                        if mask:
                            mm = nc.tensor.matmul(
                                out3, c.identb[:, :],
                                maskQb[:, bass.ds(b * QT + qt, 1), :].broadcast_to([P, HQ, SK]),
                                start=False, stop=True)
                        if relbias:
                            nc.tensor.matmul(out, c.identb[:, :],
                                             biasQb[:, min(qt, 2), g * ROWS:(g + 1) * ROWS],
                                             start=False, stop=False)
                            mm = nc.tensor.matmul(
                                out3, c.onesb[:, :], negQ[:, bass.ds(b, 1), :].broadcast_to([P, HQ, SK]),
                                start=False, stop=True)
                    mm.then_inc(s_ready, 1)

                def turn(b):
                    pe.wait_ge(s_used, b * NS + NS)
                    for qt in range(QT):
                        mm = nc.tensor.transpose(turned[:, qt * P:(qt + 1) * P], nm[:, qt, :], c.identb[:, :])
                    mm.then_inc(nm_turned, 1)

                def scores(b, t):
                    i, g = t // QUAD, t % QUAD
                    r, at = rows_of(i), g * ROWS + i * CR
                    if t >= 2:
                        pe.wait_ge(t_added if adds else p_ready, b * U + t - 1)
                    nc.tensor.matmul(TP[0:r, t % 2, :], kexp[:, at:at + r], qT[:, tokens(b)], start=True, stop=False)
                    nc.tensor.matmul(TP[0:r, t % 2, :], c.sel[:, at:at + r], negm[:, tokens(b)], start=False,
                                     stop=True).then_inc(t_ready, 1)

                def values(b, i):
                    r = rows_of(i)
                    if i == 0:
                        pe.wait_ge(v_copied, b + 1)
                        pe.wait_ge(o_normed, b)
                    pe.wait_ge(p_ready, b * U + QUAD * (i + 1))
                    for g in range(QUAD):
                        nc.tensor.matmul(O[32 * g:32 * g + 32, :], vcur[0:r, i * P + 32 * g:i * P + 32 * g + 32],
                                         prob[0:r, (QUAD * i + g) % 8, :], start=(i == 0), stop=(i == CH - 1))
                    for g in range(QUAD):
                        mm = nc.tensor.matmul(DEN[32 * g:32 * g + 32, :], c.rowmask[0:r, i, :],
                                              prob[0:r, (QUAD * i + g) % 8, :], start=(i == 0), stop=(i == CH - 1))
                    mm.then_inc(pv_done, 1)

                def batch(b, last):
                    pe.wait_ge(negm_ready, b + 1)
                    pe.wait_ge(k_made, b + 1)
                    for t in range(U):
                        scores(b, t)
                        if not last:
                            if t == 0:
                                if wo:
                                    pe.wait_ge(up_ready, b)
                                project(b + 1)
                            if t == 1 and rope:
                                squares(b + 1)
                            if t >= FIRST:
                                maxima(b + 1, t - FIRST)
                        if t % QUAD == QUAD - 1 and t > QUAD:
                            values(b, t // QUAD - 1)
                    if not last:
                        turn(b + 1)
                    values(b, CH - 1)
                    if wo:
                        pe.wait_ge(o_biased if bv else o_normed, b + 1)
                        nc.tensor.matmul(A[:, 1, :], Wo[:, :], (on2 if bv else on)[:, :],
                                         start=True, stop=True).then_inc(y_ready, 1)

                project(0)
                if rope:
                    squares(0)
                for u in range(NS):
                    maxima(0, u)
                turn(0)
                with pe.Fori(0, B - 1) as b:
                    batch(b, False)
                batch(B - 1, True)

            @block.scalar
            def _(act):
                def queries(b):
                    act.wait_ge(q_proj, b * NP + 1)
                    if rope:
                        nc.scalar.activation(rsq[:, :], A[:, 0, :], ACT.Square).then_inc(q_sq, 1)
                    else:
                        nc.scalar.activation(qT[:, tokens(b)], A[:, 0, :], ACT.Identity, bias=cv[:, 1:2],
                                             scale=cv[:, 0:1]).then_inc(q_made, 1)

                def rms(b):
                    act.wait_ge(q_ms, b + 1)
                    nc.scalar.activation(rln[:, :], A[:, 2, :], ACT.Ln, bias=DH * 1e-6).then_inc(q_log, 1)
                    act.wait_ge(q_log, b + 1)
                    nc.scalar.activation(rr[:, :], rln[:, :], ACT.Exp, scale=-0.5).then_inc(q_rms, 1)

                def batch(b, last):
                    act.wait_ge(pv_done, b * CH)
                    nc.scalar.copy(vcur[:, :], vexp[:, bass.ds(b, 1), :]).then_inc(v_copied, 1)
                    for t in range(U):
                        i = t // QUAD
                        r = rows_of(i)
                        act.wait_ge(t_added if adds else t_ready, b * U + t + 1)
                        if t >= 8:
                            act.wait_ge(pv_done, b * CH + t // QUAD - 1)
                        nc.scalar.activation(prob[0:r, t % 8, :], (added if adds else TP)[0:r, t % 2, :], ACT.Exp,
                                             bias=rowcur[0:r, CH + i:CH + i + 1] if relbias else 0.0)\
                            .then_inc(p_ready, 1)
                        if not last and t == 0:
                            queries(b + 1)
                        if not last and t == 1 and rope:
                            rms(b + 1)
                    act.wait_ge(pv_done, b * CH + CH)
                    nc.scalar.activation(lnd[:, :], DEN[:, :], ACT.Ln).then_inc(den_log, 1)
                    act.wait_ge(den_log, b + 1)
                    nc.scalar.activation(rden[:, :], lnd[:, :], ACT.Exp, scale=-1.0).then_inc(den_ready, 1)
                    act.wait_ge(o_normed, b + 1)
                    if bv and wo:
                        nc.scalar.activation(on2[:, :], on[:, :], ACT.Identity, bias=vec[:, 2:3])\
                            .then_inc(o_biased, 1)
                    if wo:
                        act.wait_ge(y_ready, b + 1)
                    act.wait_ge(x_updated, b)
                    nc.scalar.activation(up[:, :], A[:, 1, :] if wo else on[:, :], ACT.Identity, bias=cv[:, 2:3],
                                         scale=c.gates[:, gate:gate + 1]).then_inc(up_ready, 1)

                nc.scalar.preload_act_table_set(LOG_EXP)
                queries(0)
                if rope:
                    rms(0)
                with act.Fori(0, B - 1) as b:
                    batch(b, False)
                batch(B - 1, True)

            @block.vector
            def _(dve):
                def spread(b):
                    nc.vector.tensor_tensor(kexp[:, :].rearrange("p (h k) -> p h k", h=H),
                                            kT[:, bass.ds(b * SK, SK)].rearrange("p (a k) -> p a k", a=1)
                                            .broadcast_to([P, H, SK]),
                                            c.headmask[:, :].rearrange("p (h a) -> p h a", a=1)
                                            .broadcast_to([P, H, SK]), ALU.mult).then_inc(k_made, 1)

                def queries(b):
                    if rope:
                        dve.wait_ge(q_rms, b + 1)
                        dve.wait_ge(q_proj, b * 2 + 2)
                        nc.vector.scalar_tensor_tensor(out=ra[:, :], in0=A[:, 0, :], scalar=vec[:, 6:7],
                                                       in1=qcs[:, 0, :], op0=ALU.mult, op1=ALU.mult).then_inc(q_made, 1)
                        nc.vector.scalar_tensor_tensor(out=rb[:, :], in0=A[:, 1, :], scalar=vec[:, 7:8],
                                                       in1=qcs[:, 1, :], op0=ALU.mult, op1=ALU.mult).then_inc(q_made, 1)
                        dve.wait_ge(q_made, b * 4 + 2)
                        nc.vector.tensor_tensor(ra[:, :], ra[:, :], rb[:, :], ALU.add).then_inc(q_made, 1)
                        dve.wait_ge(q_made, b * 4 + 3)
                        nc.vector.tensor_tensor(qT[:, tokens(b)], ra[:, :], rr[:, :], ALU.mult).then_inc(q_made, 1)
                    dve.wait_ge(q_made, b * NQ + NQ)
                    nc.vector.tensor_scalar(qb[:, :], qT[:, tokens(b)], 1.0, None, ALU.mult).then_inc(q_cast, 1)

                def reduce(b, u):
                    qt, half = u // 2, u % 2
                    dve.wait_ge(s_ready, b * NS + u + 1)
                    nc.vector.tensor_reduce(
                        nm[:, qt, 8 * half:8 * half + 8].rearrange("p (a h) -> p a h", a=2),
                        A[:, 2 * (u % 2):2 * (u % 2) + 2, 0:ROWS].rearrange("p a (h k) -> p a h k", h=HQ),
                        AX.X, ALU.max, negate=True).then_inc(s_used, 1)

                def shift(b):
                    dve.wait_ge(nm_turned, b + 1)
                    nc.vector.tensor_scalar(negm[:, tokens(b)], turned, 1.0, None, ALU.mult).then_inc(negm_ready, 1)

                def add(b, t):
                    i, g = t // QUAD, t % QUAD
                    r = rows_of(i)
                    dve.wait_ge(t_ready, b * U + t + 1)
                    if t >= 2:
                        dve.wait_ge(p_ready, b * U + t - 1)
                    if mask:
                        nc.vector.tensor_tensor(added[0:r, t % 2, :], TP[0:r, t % 2, :],
                                                maskT[0:r, bass.ds(b * CH + i, 1), :], ALU.add)\
                            .then_inc(t_added, 1)
                    else:
                        nc.vector.scalar_tensor_tensor(
                            out=added[0:r, t % 2, :], in0=biasT[0:r, g * CH + i, :],
                            scalar=rowcur[0:r, i:i + 1], in1=TP[0:r, t % 2, :], op0=ALU.mult,
                            op1=ALU.add).then_inc(t_added, 1)

                def batch(b, last):
                    if relbias:
                        dve.wait_ge(p_ready, b * U)
                        nc.vector.tensor_copy(rowcur[0:CR, :], rowkeep[0:CR, bass.ds(b, 1), :]).then_inc(row_made, 1)
                        dve.wait_ge(row_made, b + 1)
                    if not last:
                        nc.vector.tensor_scalar(kcur[:, :], kT[:, bass.ds(b * SK + SK, SK)], 1.0, None,
                                                ALU.mult).then_inc(k_cur, 1)
                    for t in range(U):
                        if adds:
                            add(b, t)
                        if not last and t == 2:
                            queries(b + 1)
                        if not last and t >= FIRST:
                            reduce(b + 1, t - FIRST)
                    if not last:
                        dve.wait_ge(t_ready, b * U + U)
                        spread(b + 1)
                        shift(b + 1)
                    dve.wait_ge(den_ready, b + 1)
                    nc.vector.tensor_tensor(on[:, :], O[:, :], rden[:, :], ALU.mult).then_inc(o_normed, 1)
                    dve.wait_ge(up_ready, b + 1)
                    nc.vector.tensor_tensor(c.xT[:, tokens(b)], c.xT[:, tokens(b)], up[:, :], ALU.add)\
                        .then_inc(x_updated, 1)

                nc.vector.tensor_copy(kcur[:, :], kT[:, 0:SK]).then_inc(k_cur, 1)
                spread(0)
                queries(0)
                for u in range(NS):
                    reduce(0, u)
                shift(0)
                if relbias:
                    dve.wait_ge(bt_loaded, 16)
                with dve.Fori(0, B - 1) as b:
                    batch(b, False)
                batch(B - 1, True)
                dve.wait_ge(x_updated, B)

            @block.gpsimd
            def _(pool):
                def spread(b):
                    pool.wait_ge(k_cur, b + 1)
                    nc.gpsimd.tensor_tensor(kexpb[:, :].rearrange("p (h k) -> p h k", h=H),
                                            kcur[:, :].rearrange("p (a k) -> p a k", a=1).broadcast_to([P, H, SK]),
                                            c.headmask[:, :].rearrange("p (h a) -> p h a", a=1)
                                            .broadcast_to([P, H, SK]), ALU.mult).then_inc(kb_made, 1)

                spread(0)
                with pool.Fori(0, B - 1) as b:
                    spread(b + 1)
                pool.wait_ge(kb_made, B)


def ternary_ffn(c, name, gate):
    nc, d = c.nc, c.dram
    NJ = 4
    HID = NJ * P
    with ExitStack() as ctx, c.phase():
        def sb(n, shape, dt=F32):
            return ctx.enter_context(nc.sbuf_tensor(f"{name}_{n}", shape, dt))

        def ps(n, shape):
            return ctx.enter_context(nc.psum_tensor(f"{name}_{n}", shape, F32))

        def sem(n):
            return c.sem(f"{name}_{n}")

        Wf, Wp = sb("Wf", [P, HID]), sb("Wp", [P, HID])
        Qf, Qp, Wc = sb("Qf", [P, HID]), sb("Qp", [P, HID]), sb("Wc", [P, HID])
        low = sb("low", [P, HID])
        ln = sb("ln", [P, 2 * NJ])
        st = sb("st", [P, 12])
        h, hs = sb("h", [P, NJ, S]), sb("hs", [P, NJ, S])
        mu2, v, lnv, rstd, yn, up = (sb(n, [P, S]) for n in ("mu2", "v", "lnv", "rstd", "yn", "up"))
        loaded, rounded, totals, summed, folded = (sem(n) for n in ("loaded", "rounded", "totals", "summed", "folded"))

        def start_loads(sp):
            for dst, src in ((Wf, "F0_W1"), (Wp, "F0_W2"), (ln, "F0_ln")):
                sp.dma_start(dst[:, :], d[src]).then_inc(loaded, 16)

        norm_x(c, name + "_n", start_loads)
        HP = ps("HP", [P, 2, S])
        MU, M2, Y, PRE = (ps(n, [P, S]) for n in ("MU", "M2", "Y", "PRE"))
        with nc.Block() as block:
            @block.vector
            def _(dve):
                dve.wait_ge(loaded, 48)
                for n, w in ((0, Wf), (1, Wp)):
                    nc.vector.scalar_tensor_tensor(out=low[:, :], in0=w[:, :], scalar=-1.0, in1=w[:, :],
                                                   op0=ALU.mult, op1=ALU.max).then_inc(rounded, 1)
                    dve.wait_ge(rounded, 2 * n + 1)
                    nc.vector.tensor_reduce(st[:, n:n + 1], low[:, :], AX.X, ALU.add).then_inc(rounded, 1)
                    dve.wait_ge(rounded, 2 * n + 2)
                dve.wait_ge(summed, 1)
                nc.vector.tensor_scalar(st[:, 2:4], PRE[:, 0:2], float(P) / (P * HID), 1e-6, ALU.mult,
                                        ALU.add).then_inc(rounded, 1)
                dve.wait_ge(rounded, 5)
                nc.vector.tensor_scalar(st[:, 4:6], st[:, 2:4], 0.5, None, ALU.mult).then_inc(rounded, 1)
                nc.vector.tensor_scalar(st[:, 6:8], st[:, 2:4], -0.5, None, ALU.mult).then_inc(rounded, 1)
                dve.wait_ge(rounded, 7)
                for n, w, q in ((0, Wf, Qf), (1, Wp, Qp)):
                    nc.vector.tensor_scalar(low[:, :], w[:, :], st[:, 6 + n:7 + n], None, ALU.is_lt).then_inc(rounded, 1)
                    dve.wait_ge(rounded, 8 + 2 * n)
                    nc.vector.scalar_tensor_tensor(out=q[:, :], in0=w[:, :], scalar=st[:, 4 + n:5 + n], in1=low[:, :],
                                                   op0=ALU.is_gt, op1=ALU.subtract).then_inc(rounded, 1)
                    dve.wait_ge(rounded, 9 + 2 * n)
                for j in range(NJ):
                    nc.vector.tensor_scalar(Wc[:, j * P:(j + 1) * P], Qp[:, j * P:(j + 1) * P], ln[:, j:j + 1], None,
                                            ALU.mult).then_inc(rounded, 1)
                dve.wait_ge(summed, 2)
                dve.wait_ge(rounded, 15)
                for j in range(NJ):
                    nc.vector.scalar_tensor_tensor(out=Wc[:, j * P:(j + 1) * P], in0=PRE[:, P:2 * P], scalar=-1.0 / NJ,
                                                   in1=Wc[:, j * P:(j + 1) * P], op0=ALU.mult,
                                                   op1=ALU.add).then_inc(folded, 1)
                nc.vector.tensor_tensor(st[:, 8:9], PRE[:, 2 * P:2 * P + 1], c.gates[:, gate:gate + 1],
                                        ALU.mult).then_inc(folded, 1)
                dve.wait_ge(folded, NJ + 1)

            @block.tensor
            def _(pe):
                pe.wait_ge(rounded, 4)
                nc.tensor.matmul(PRE[:, 0:2], c.mean[:, :], st[:, 0:2], start=True, stop=True).then_inc(summed, 1)
                pe.wait_ge(rounded, 15)
                for j in range(NJ):
                    nc.tensor.matmul(PRE[:, P:2 * P], c.mean[:, :], Wc[:, j * P:(j + 1) * P], start=(j == 0),
                                     stop=(j == NJ - 1))
                for j in range(NJ):
                    mm = nc.tensor.matmul(PRE[:, 2 * P:2 * P + 1], Qp[:, j * P:(j + 1) * P], ln[:, NJ + j:NJ + j + 1],
                                          start=(j == 0), stop=(j == NJ - 1))
                mm.then_inc(summed, 1)

        (x_updated, h_ready, gelued, squared, acc_ready, mu_sq, var_made, var_log, rstd_ready, y_scaled, up_ready) = (
            sem(n) for n in ("x_updated", "h_ready", "gelued", "squared", "acc_ready", "mu_sq", "var_made", "var_log",
                             "rstd_ready", "y_scaled", "up_ready"))

        def tokens(b):
            return bass.ds(b * S, S)

        with nc.Block() as block:
            @block.tensor
            def _(pe):
                with pe.Fori(0, B) as b:
                    pe.wait_ge(x_updated, b)

                    def down(j):
                        first, last = j == 0, j == NJ - 1
                        pe.wait_ge(gelued, b * NJ + j + 1)
                        nc.tensor.matmul(MU[:, :], c.mean[:, :], h[:, j, :], start=first, stop=last)
                        nc.tensor.matmul(Y[:, :], Wc[:, j * P:(j + 1) * P], h[:, j, :], start=first, stop=last)
                        pe.wait_ge(squared, b * NJ + j + 1)
                        mm = nc.tensor.matmul(M2[:, :], c.mean[:, :], hs[:, j, :], start=first, stop=last)
                        if last:
                            mm.then_inc(acc_ready, 1)

                    for j in range(NJ):
                        if j >= 2:
                            pe.wait_ge(gelued, b * NJ + j - 1)
                        nc.tensor.matmul(HP[:, j % 2, :], Qf[:, j * P:(j + 1) * P], c.xn[:, tokens(b)], start=True,
                                         stop=True).then_inc(h_ready, 1)
                        if j:
                            down(j - 1)
                    down(NJ - 1)

            @block.scalar
            def _(act):
                with act.Fori(0, B) as b:
                    nc.scalar.preload_act_table_set(GELU)
                    for j in range(NJ):
                        act.wait_ge(h_ready, b * NJ + j + 1)
                        nc.scalar.activation(h[:, j, :], HP[:, j % 2, :], ACT.Gelu).then_inc(gelued, 1)
                    nc.scalar.preload_act_table_set(LOG_EXP)
                    act.wait_ge(acc_ready, b + 1)
                    nc.scalar.activation(mu2[:, :], MU[:, :], ACT.Square, scale=1.0 / NJ).then_inc(mu_sq, 1)
                    act.wait_ge(var_made, b + 1)
                    nc.scalar.activation(lnv[:, :], v[:, :], ACT.Ln, bias=LN_EPS).then_inc(var_log, 1)
                    act.wait_ge(var_log, b + 1)
                    nc.scalar.activation(rstd[:, :], lnv[:, :], ACT.Exp, scale=-0.5).then_inc(rstd_ready, 1)
                    act.wait_ge(y_scaled, b + 1)
                    nc.scalar.activation(up[:, :], yn[:, :], ACT.Identity, bias=st[:, 8:9],
                                         scale=c.gates[:, gate:gate + 1]).then_inc(up_ready, 1)

            @block.vector
            def _(dve):
                with dve.Fori(0, B) as b:
                    for j in range(NJ):
                        dve.wait_ge(gelued, b * NJ + j + 1)
                        nc.vector.tensor_tensor(hs[:, j, :], h[:, j, :], h[:, j, :], ALU.mult).then_inc(squared, 1)
                    dve.wait_ge(mu_sq, b + 1)
                    nc.vector.scalar_tensor_tensor(out=v[:, :], in0=M2[:, :], scalar=1.0 / NJ, in1=mu2[:, :],
                                                   op0=ALU.mult, op1=ALU.subtract).then_inc(var_made, 1)
                    dve.wait_ge(rstd_ready, b + 1)
                    nc.vector.tensor_tensor(yn[:, :], Y[:, :], rstd[:, :], ALU.mult).then_inc(y_scaled, 1)
                    dve.wait_ge(up_ready, b + 1)
                    nc.vector.tensor_tensor(c.xT[:, tokens(b)], c.xT[:, tokens(b)], up[:, :], ALU.add)\
                        .then_inc(x_updated, 1)
                dve.wait_ge(x_updated, B)


class Router:

    def __init__(self, c, ctx, name, E, weight, bias=None):
        self.c, self.name, self.E, self.weight, self.bias = c, name, E, weight, bias
        self.w = ctx.enter_context(c.nc.sbuf_tensor(name + "_w", [P, E], F32))
        self.bb = ctx.enter_context(c.nc.sbuf_tensor(name + "_bb", [P, E], F32))
        self.loaded = c.sem(name + "_loaded")

    def load(self, sp):
        sp.dma_start(self.w[:, :], self.c.dram[self.weight]).then_inc(self.loaded, 16)
        if self.bias:
            sp.dma_start(self.bb[:, :], self.c.dram[self.bias].partition_broadcast(P)).then_inc(self.loaded, 16)


def route(c, ctx, router, softmax=True):
    nc, name, E, w, bb, loaded = c.nc, router.name, router.E, router.w, router.bb, router.loaded
    top = ctx.enter_context(nc.sbuf_tensor(name + "_top", [P, TILES, 8], F32))
    place = ctx.enter_context(nc.sbuf_tensor(name + "_place", [P, TILES, 8], F32))
    with ExitStack() as own:
        L = own.enter_context(nc.psum_tensor(name + "_L", [P, TILES * 64], F32))
        s = own.enter_context(nc.sbuf_tensor(name + "_s", [P, TILES, E], F32))
        e = own.enter_context(nc.sbuf_tensor(name + "_e", [P, TILES, E], F32))
        r = own.enter_context(nc.sbuf_tensor(name + "_r", [P, 3, TILES], F32))
        pl = own.enter_context(nc.sbuf_tensor(name + "_pl", [P, TILES, 8], U32))
        logits, made, exped, found = (c.sem(f"{name}_{n}") for n in ("logits", "made", "exped", "found"))
        Lt = L[:, 0:TILES * E].rearrange("p (t e) -> p t e", t=TILES)
        nload = 32 if router.bias else 16

        def per_tile(i):
            return r[:, i, :].rearrange("p (t a) -> p t a", a=1).broadcast_to([P, TILES, E])

        with nc.Block() as block:
            @block.tensor
            def _(pe):
                pe.wait_ge(loaded, nload)
                for t in range(TILES):
                    mm = nc.tensor.matmul(L[:, t * E:(t + 1) * E], c.xn[:, t * P:(t + 1) * P], w[:, :],
                                          start=True, stop=True)
                mm.then_inc(logits, 1)

            @block.scalar
            def _(act):
                if softmax:
                    nc.scalar.preload_act_table_set(LOG_EXP)
                    act.wait_ge(made, 2)
                    nc.scalar.activation(e[:, :, :], s[:, :, :], ACT.Exp).then_inc(exped, 1)

            @block.vector
            def _(dve):
                dve.wait_ge(loaded, nload)
                dve.wait_ge(logits, 1)
                if softmax:
                    nc.vector.tensor_reduce(r[:, 0, :], Lt, AX.X, ALU.max).then_inc(made, 1)
                    dve.wait_ge(made, 1)
                    nc.vector.tensor_tensor(s[:, :, :], Lt, per_tile(0), ALU.subtract).then_inc(made, 1)
                    dve.wait_ge(exped, 1)
                    nc.vector.tensor_reduce(r[:, 1, :], e[:, :, :], AX.X, ALU.add).then_inc(made, 1)
                    dve.wait_ge(made, 3)
                    nc.vector.reciprocal(r[:, 2, :], r[:, 1, :]).then_inc(made, 1)
                    dve.wait_ge(made, 4)
                    nc.vector.tensor_tensor(s[:, :, :], e[:, :, :], per_tile(2), ALU.mult).then_inc(made, 1)
                    dve.wait_ge(made, 5)
                else:
                    nc.vector.tensor_tensor(s[:, :, :], Lt, bb[:, :].rearrange("p (a e) -> p a e", a=1)
                                            .broadcast_to([P, TILES, E]), ALU.add).then_inc(made, 1)
                    dve.wait_ge(made, 1)
                for t in range(TILES):
                    nc.vector.max(out=top[:, t, :], in_=s[:, t, :]).then_inc(found, 1)
                dve.wait_ge(found, TILES)
                for t in range(TILES):
                    nc.vector.max_index(out=pl[:, t, :], in_max=top[:, t, :], in_values=s[:, t, :]).then_inc(found, 1)
                dve.wait_ge(found, 2 * TILES)
                nc.vector.tensor_copy(place[:, :, :], pl[:, :, :]).then_inc(found, 1)
                dve.wait_ge(found, 2 * TILES + 1)
    return top, place


def expert_weights(c, ctx, name, E, top, place, normalise):
    nc = c.nc
    wt = ctx.enter_context(nc.sbuf_tensor(name + "_wt", [P, TILES, P], F32))
    with ExitStack() as own:
        hot = own.enter_context(nc.sbuf_tensor(name + "_hot", [P, 2, TILES, E], F32))
        r = own.enter_context(nc.sbuf_tensor(name + "_nr", [P, 2, TILES], F32))
        ready = c.sem(name + "_weights")

        def col(a, k):
            return a[:, :, k:k + 1].broadcast_to([P, TILES, E])

        with nc.Block() as block:
            @block.vector
            def _(dve):
                n = 0

                def step(ins):
                    nonlocal n
                    n += 1
                    ins.then_inc(ready, 1)
                    dve.wait_ge(ready, n)

                step(nc.vector.memset(wt[:, :, :], 0.0))
                if normalise:
                    step(nc.vector.tensor_reduce(r[:, 0, :], top[:, :, 0:2], AX.X, ALU.add))
                    step(nc.vector.reciprocal(r[:, 1, :], r[:, 0, :]))
                    step(nc.vector.tensor_tensor(top[:, :, 0:2], top[:, :, 0:2], r[:, 1, :]
                                                 .rearrange("p (t a) -> p t a", a=1).broadcast_to([P, TILES, 2]),
                                                 ALU.mult))
                for k in range(2):
                    step(nc.vector.tensor_tensor(hot[:, k, :, :], c.iota[:, 0:E].rearrange("p (a e) -> p a e", a=1)
                                                 .broadcast_to([P, TILES, E]), col(place, k), ALU.is_equal))
                    step(nc.vector.tensor_tensor(hot[:, k, :, :], hot[:, k, :, :], col(top, k), ALU.mult))
                step(nc.vector.tensor_tensor(wt[:, :, 0:E], hot[:, 0, :, :], hot[:, 1, :, :], ALU.add))
    return wt


def dense_glu_moe(c, name, gate):
    nc, d = c.nc, c.dram
    E, F = 8, 352
    NJ = -(-F // P)
    U = E * NJ
    with ExitStack() as ctx, c.phase():
        router = Router(c, ctx, name + "r", E, "F2_router")

        def sb(n, shape, dt=F32):
            return ctx.enter_context(nc.sbuf_tensor(f"{name}_{n}", shape, dt))

        def ps(n, shape):
            return ctx.enter_context(nc.psum_tensor(f"{name}_{n}", shape, F32))

        def sem(n):
            return c.sem(f"{name}_{n}")

        W1, V1 = sb("W1", [P, E * F]), sb("V1", [P, E * F])
        W2 = sb("W2", [P, U, P])
        bias = sb("bias", [P, 2])
        gl, hv = sb("gl", [P, 2, S]), sb("hv", [P, 3, S])
        acc = sb("acc", [P, QT, P])
        wcur = sb("wcur", [P, QT, E])
        up = sb("up", [P, S])
        (loaded, bias_made, x_updated, up_ready, hv_ready, gelued, multiplied, down_done, y_ready, w_ready, y_added,
         turned) = (sem(n) for n in ("loaded", "bias_made", "x_updated", "up_ready", "hv_ready", "gelued",
                                     "multiplied", "down_done", "y_ready", "w_ready", "y_added", "turned"))

        def tokens(b):
            return bass.ds(b * S, S)

        def wide(j):
            return min(P, F - j * P)

        def start_loads(sp):
            router.load(sp)
            for dst, src in ((W1[:, :], "F2_w1"), (V1[:, :], "F2_v1"), (W2[:, :, :], "F2_w2"),
                             (bias[:, 0:1], "F2_bias")):
                sp.dma_start(dst, d[src]).then_inc(loaded, 16)

        norm_x(c, name + "_n", start_loads)
        top, place = route(c, ctx, router)
        wt = expert_weights(c, ctx, name + "r", E, top, place, False)
        HP, VP, YP = (ps(n, [P, 2, S]) for n in ("HP", "VP", "YP"))
        TR = ps("TR", [P, S])
        with nc.Block() as block:
            @block.tensor
            def _(pe):
                pe.wait_ge(loaded, 64)
                with pe.Fori(0, B) as b:
                    pe.wait_ge(x_updated, b)

                    def down(u):
                        e, j = u // NJ, u % NJ
                        if j == 0 and e >= 2:
                            pe.wait_ge(y_added, b * E * QT + (e - 1) * QT)
                        pe.wait_ge(multiplied, b * U + u + 1)
                        for q in range(QT):
                            mm = nc.tensor.matmul(YP[:, e % 2, q * P:(q + 1) * P],
                                                  hv[0:wide(j), u % 3, q * P:(q + 1) * P], W2[0:wide(j), u, :],
                                                  start=(j == 0 and q == 0), stop=(j == NJ - 1),
                                                  skip_group_check=True)
                        mm.then_inc(down_done, 1)

                    for u in range(U):
                        e, j = u // NJ, u % NJ
                        at = e * F + j * P
                        if u >= 2:
                            pe.wait_ge(multiplied, b * U + u - 1)
                        nc.tensor.matmul(HP[0:wide(j), u % 2, :], W1[:, at:at + wide(j)], c.xn[:, tokens(b)],
                                         start=True, stop=True)
                        nc.tensor.matmul(VP[0:wide(j), u % 2, :], V1[:, at:at + wide(j)], c.xn[:, tokens(b)],
                                         start=True, stop=True).then_inc(hv_ready, 1)
                        if u:
                            down(u - 1)
                    down(U - 1)
                    pe.wait_ge(y_added, b * E * QT + E * QT)
                    for q in range(QT):
                        mm = nc.tensor.transpose(TR[:, q * P:(q + 1) * P], acc[:, q, :], c.ident[:, :])
                    mm.then_inc(turned, 1)

            @block.scalar
            def _(act):
                nc.scalar.preload_act_table_set(GELU)
                act.wait_ge(bias_made, 1)
                with act.Fori(0, B) as b:
                    for u in range(U):
                        f = wide(u % NJ)
                        act.wait_ge(hv_ready, b * U + u + 1)
                        nc.scalar.activation(gl[0:f, u % 2, :], HP[0:f, u % 2, :], ACT.Gelu).then_inc(gelued, 1)
                    act.wait_ge(turned, b + 1)
                    nc.scalar.activation(up[:, :], TR[:, :], ACT.Identity, bias=bias[:, 1:2],
                                         scale=c.gates[:, gate:gate + 1]).then_inc(up_ready, 1)

            @block.vector
            def _(dve):
                dve.wait_ge(loaded, 64)
                nc.vector.tensor_tensor(bias[:, 1:2], bias[:, 0:1], c.gates[:, gate:gate + 1],
                                        ALU.mult).then_inc(bias_made, 1)
                with dve.Fori(0, B) as b:
                    dve.wait_ge(y_added, b * E * QT)
                    nc.vector.tensor_copy(wcur[:, :, :], wt[:, bass.ds(b * QT, QT), 0:E]).then_inc(w_ready, 1)
                    dve.wait_ge(w_ready, b + 1)

                    def add(e):
                        dve.wait_ge(down_done, b * U + (e + 1) * NJ)
                        if e:
                            dve.wait_ge(y_added, b * E * QT + e * QT)
                        for q in range(QT):
                            y = YP[:, e % 2, q * P:(q + 1) * P]
                            if e == 0:
                                ins = nc.vector.tensor_scalar(acc[:, q, :], y, wcur[:, q, 0:1], None, ALU.mult)
                            else:
                                ins = nc.vector.scalar_tensor_tensor(out=acc[:, q, :], in0=y,
                                                                     scalar=wcur[:, q, e:e + 1], in1=acc[:, q, :],
                                                                     op0=ALU.mult, op1=ALU.add)
                            ins.then_inc(y_added, 1)

                    for u in range(U):
                        f = wide(u % NJ)
                        dve.wait_ge(gelued, b * U + u + 1)
                        if u >= 3:
                            dve.wait_ge(down_done, b * U + u - 2)
                        nc.vector.tensor_tensor(hv[0:f, u % 3, :], gl[0:f, u % 2, :], VP[0:f, u % 2, :],
                                                ALU.mult).then_inc(multiplied, 1)
                        if u and u % NJ == 0:
                            add(u // NJ - 1)
                    add(E - 1)
                    dve.wait_ge(up_ready, b + 1)
                    nc.vector.tensor_tensor(c.xT[:, tokens(b)], c.xT[:, tokens(b)], up[:, :], ALU.add)\
                        .then_inc(x_updated, 1)
                dve.wait_ge(x_updated, B)


def shared_moe(c, name, gate):
    nc, d = c.nc, c.dram
    E, HID, SH = 16, 64, 256
    NE = E * HID // P
    U = NE + SH // P
    with ExitStack() as ctx, c.phase():
        router = Router(c, ctx, name + "r", E, "F3_router")

        def sb(n, shape, dt=F32):
            return ctx.enter_context(nc.sbuf_tensor(f"{name}_{n}", shape, dt))

        def ps(n, shape):
            return ctx.enter_context(nc.psum_tensor(f"{name}_{n}", shape, F32))

        def sem(n):
            return c.sem(f"{name}_{n}")

        Wg, Wu, Wd = sb("Wg", [P, U, P]), sb("Wu", [P, U, P]), sb("Wd", [P, U, P])
        wsg = sb("wsg", [P, P])
        pair = sb("pair", [P, NE, P])
        wT = sb("wT", [P, T])
        sig = sb("sig", [P, T])
        sl, hu, hw = sb("sl", [P, 2, S]), sb("hu", [P, 2, S]), sb("hw", [P, 2, S])
        loaded, turned, wt_copied, sg_ready, sg_made = (
            sem(n) for n in ("loaded", "turned", "wt_copied", "sg_ready", "sg_made"))

        def start_loads(sp):
            router.load(sp)
            for dst, src in ((Wg[:, :, :], "F3_Wg"), (Wu[:, :, :], "F3_Wu"), (Wd[:, :, :], "F3_Wd"),
                             (wsg[:, :], "F3_Wsg"), (pair[:, :, :], "pair")):
                sp.dma_start(dst, d[src]).then_inc(loaded, 16)

        norm_x(c, name + "_n", start_loads)
        top, place = route(c, ctx, router)
        wt = expert_weights(c, ctx, name + "r", E, top, place, True)
        GP, UP, BP = (ps(n, [P, 2, S]) for n in ("GP", "UP", "BP"))
        YP = ps("YP", [P, S])
        with nc.Block() as block:
            @block.tensor
            def _(pe):
                pe.wait_ge(loaded, 80)
                for b in range(B):
                    if b >= 2:
                        pe.wait_ge(wt_copied, b - 1)
                    for q in range(QT):
                        mm = nc.tensor.transpose(GP[:, b % 2, q * P:(q + 1) * P], wt[:, b * QT + q, :], c.ident[:, :])
                    mm.then_inc(turned, 1)
                    if b >= 2:
                        pe.wait_ge(sg_made, b - 1)
                    nc.tensor.matmul(UP[:, b % 2, :], wsg[:, :], c.xn[:, b * S:(b + 1) * S], start=True,
                                     stop=True).then_inc(sg_ready, 1)

            @block.vector
            def _(dve):
                for b in range(B):
                    dve.wait_ge(turned, b + 1)
                    nc.vector.tensor_copy(wT[:, b * S:(b + 1) * S], GP[:, b % 2, :]).then_inc(wt_copied, 1)
                dve.wait_ge(wt_copied, B)

            @block.scalar
            def _(act):
                for b in range(B):
                    act.wait_ge(sg_ready, b + 1)
                    nc.scalar.activation(sig[:, b * S:(b + 1) * S], UP[:, b % 2, :], ACT.Sigmoid).then_inc(sg_made, 1)
                act.wait_ge(sg_made, B)

        x_updated, gu_ready, silued, up_mult, gated, y_ready = (
            sem(n) for n in ("x_updated", "gu_ready", "silued", "up_mult", "gated", "y_ready"))

        def tokens(b):
            return bass.ds(b * S, S)

        with nc.Block() as block:
            @block.tensor
            def _(pe):
                with pe.Fori(0, B) as b:
                    pe.wait_ge(x_updated, b)

                    def down(u):
                        pe.wait_ge(gated, b * U + u + 1)
                        mm = nc.tensor.matmul(YP[:, :], Wd[:, u, :], hw[:, u % 2, :], start=(u == 0), stop=(u == U - 1))
                        mm.then_inc(y_ready, 1)

                    for u in range(U):
                        if u >= 2:
                            pe.wait_ge(gated, b * U + u - 1)
                        nc.tensor.matmul(GP[:, u % 2, :], Wg[:, u, :], c.xn[:, tokens(b)], start=True, stop=True)
                        mm = nc.tensor.matmul(UP[:, u % 2, :], Wu[:, u, :], c.xn[:, tokens(b)], start=True, stop=True)
                        if u < NE:
                            mm = nc.tensor.matmul(BP[:, u % 2, :], pair[:, u, :], wT[:, tokens(b)], start=True,
                                                  stop=True)
                        mm.then_inc(gu_ready, 1)
                        if u:
                            down(u - 1)
                    down(U - 1)

            @block.scalar
            def _(act):
                nc.scalar.preload_act_table_set("silu_and_others")
                with act.Fori(0, B) as b:
                    for u in range(U):
                        act.wait_ge(gu_ready, b * U + u + 1)
                        nc.scalar.activation(sl[:, u % 2, :], GP[:, u % 2, :], ACT.Silu).then_inc(silued, 1)

            @block.vector
            def _(dve):
                with dve.Fori(0, B) as b:
                    for u in range(U):
                        dve.wait_ge(silued, b * U + u + 1)
                        nc.vector.tensor_tensor(hu[:, u % 2, :], sl[:, u % 2, :], UP[:, u % 2, :],
                                                ALU.mult).then_inc(up_mult, 1)
                        dve.wait_ge(up_mult, b * U + u + 1)
                        if u >= 2:
                            dve.wait_ge(y_ready, b * U + u - 1)
                        nc.vector.tensor_tensor(hw[:, u % 2, :], hu[:, u % 2, :],
                                                BP[:, u % 2, :] if u < NE else sig[:, tokens(b)],
                                                ALU.mult).then_inc(gated, 1)
                    dve.wait_ge(y_ready, b * U + U)
                    nc.vector.scalar_tensor_tensor(out=c.xT[:, tokens(b)], in0=YP[:, :],
                                                   scalar=c.gates[:, gate:gate + 1], in1=c.xT[:, tokens(b)],
                                                   op0=ALU.mult, op1=ALU.add).then_inc(x_updated, 1)
                dve.wait_ge(x_updated, B)


def perceiver_attention(c, name, gate):
    nc, d = c.nc, c.dram
    NP, HD = 8, 64
    K = SK + S
    CUT = 295
    PIECES = ((0, CUT), (CUT, K))
    KC = [(0, SK)] + [(SK + P * i, SK + P * (i + 1)) for i in range(QT)]
    NC = len(KC)
    NT = 2 * NC
    NS = 2 * QT
    BASE = 512 - CUT
    with ExitStack() as ctx, c.phase():
        def sb(n, shape, dt=F32):
            return ctx.enter_context(nc.sbuf_tensor(f"{name}_{n}", shape, dt))

        def ps(n, shape):
            return ctx.enter_context(nc.psum_tensor(f"{name}_{n}", shape, F32))

        def sem(n):
            return c.sem(f"{name}_{n}")

        cn = sb("cn", [P, B * SK])
        Wq, Wk, Wv = (sb(n, [P, NP * P]) for n in ("Wq", "Wk", "Wv"))
        Wo = sb("Wo", [P, NP, P])
        vec = sb("vec", [P, 8])
        cv = sb("cv", [P, 2])
        blk = sb("blk", [P, P])
        sel2f, sel2 = sb("sel2f", [P, 2, P]), sb("sel2", [P, 2, P], BF16)
        onesf = sb("onesf", [P, HD])
        keym = sb("keym", [P, B * SK], I32)
        negQ = sb("negQ", [P, B, SK], BF16)
        rowm = sb("rowm", [P, B], I32)
        rowneg = sb("rowneg", [P, B])
        rowcur = sb("rowcur", [P, 1])
        kv = sb("kv", [P, K])
        V = sb("V", [P, 4, NC, P])
        sq, clip, lnn, rn = (sb(n, [P, S]) for n in ("sq", "clip", "lnn", "rn"))
        qn, qnb = sb("qn", [P, 4, S]), sb("qnb", [P, 2, S], BF16)
        kz, kzb = sb("kz", [P, 8, K]), sb("kzb", [P, 4, K], BF16)
        nm = sb("nm", [P, QT, P], BF16)
        negm = sb("negm", [P, 2, S], BF16)
        prob = sb("prob", [P, 8, S])
        acc = sb("acc", [P, 2, S])
        lnd, rden, up = (sb(n, [P, S]) for n in ("lnd", "rden", "up"))
        on = sb("on", [P, NP, S])

        loaded, prep, affine, zeroed = sem("loaded"), sem("prep"), sem("affine"), sem("zeroed")
        loads = [(Wq[:, :], "A2_Wq"), (Wk[:, :], "A2_Wk"), (Wv[:, :], "A2_Wv"), (Wo[:, :, :], "A2_Wo"),
                 (vec[:, :], "A2_vec"), (blk[:, :], "blk64"), (sel2f[:, :, :], "sel2"), (rowm[0:SK, :], "rowmask2")]
        nload = 16 * (len(loads) + 1)

        def start_loads(sp):
            for dst, src in loads:
                sp.dma_start(dst, d[src]).then_inc(loaded, 16)
            sp.dma_start(keym[:, :], d["keymask2"].partition_broadcast(P)).then_inc(loaded, 16)

        norm_x(c, name + "_nx", start_loads)
        layer_norm(c, name + "_nl", [(c.xn[:, s:s + S], c.xn[:, s:s + S], S) for s in range(0, T, S)]
                   + [(c.ctxrep[:, :, 0:SK], cn[:, :], B * SK)])
        SP = ps("SP", [P, 2 * S])
        TP = ps("TP", [P, 2, S])
        PR = ps("PR", [P, 2, S])
        O, DEN = ps("O", [P, S]), ps("DEN", [P, S])
        with nc.Block() as block:
            @block.scalar
            def _(act):
                act.wait_ge(loaded, nload)
                for s in range(0, T, S):
                    nc.scalar.activation(c.xn[:, s:s + S], c.xn[:, s:s + S], ACT.Identity, bias=vec[:, 3:4],
                                         scale=vec[:, 2:3]).then_inc(affine, 1)
                nc.scalar.activation(cn[:, :], cn[:, :], ACT.Identity, bias=vec[:, 1:2],
                                     scale=vec[:, 0:1]).then_inc(affine, 1)
                act.wait_ge(affine, B + 1)

            @block.vector
            def _(dve):
                dve.wait_ge(loaded, nload)
                nc.vector.memset(nm[:, :, :], 0.0).then_inc(prep, 1)
                nc.vector.memset(onesf[:, :], 1.0).then_inc(prep, 1)
                nc.vector.tensor_copy(sel2[:, :, :], sel2f[:, :, :]).then_inc(prep, 1)
                nc.vector.tensor_scalar(negQ[:, :, :], keym[:, :].rearrange("p (b k) -> p b k", b=B), -NEG / P, NEG / P,
                                        ALU.mult, ALU.add).then_inc(prep, 1)
                nc.vector.tensor_scalar(rowneg[0:SK, :], rowm[0:SK, :], -NEG, NEG, ALU.mult, ALU.add).then_inc(prep, 1)
                nc.vector.tensor_scalar(cv[:, 0:1], vec[:, 4:5], HD ** -0.5, None, ALU.mult).then_inc(prep, 1)
                nc.vector.tensor_tensor(cv[:, 1:2], vec[:, 6:7], c.gates[:, gate:gate + 1], ALU.mult).then_inc(prep, 1)
                dve.wait_ge(prep, 7)

            @block.gpsimd
            def _(pool):
                nc.gpsimd.memset(kz[:, :, :], 0.0).then_inc(zeroed, 1)
                nc.gpsimd.memset(kzb[:, :, :], 0.0).then_inc(zeroed, 1)
                pool.wait_ge(zeroed, 2)

        (x_updated, kv_copied, pr_ready, squared, ms_ready, clipped, n_log, n_rms, normed, v_copied, cast,
         s_ready, s_used, nm_turned, negm_ready, t_ready, p_ready, summed, pv_done, den_log, den_ready, o_normed,
         y_ready, up_ready, row_copied) = (sem(n) for n in (
            "x_updated", "kv_copied", "pr_ready", "squared", "ms_ready", "clipped", "n_log", "n_rms", "normed",
            "v_copied", "cast", "s_ready", "s_used", "nm_turned", "negm_ready", "t_ready", "p_ready", "summed",
            "pv_done", "den_log", "den_ready", "o_normed", "y_ready", "up_ready", "row_copied"))
        ctx_added = sem("ctx_added")
        turned = PR[:, 1, 0:S // 2].bitcast(BF16)

        NM, NN, NV, NPV, NA = 3, 5, 2, NC + 1, 6
        after_piece = (1, 3, 5)
        PROJECT, SQUARES, RMS = {0: 0, 3: 1, 6: 2, 9: 3}, {1: 0, 4: 1, 7: 2}, {2: 0, 5: 1, 8: 2}
        VCTX = S - P

        def tokens(b):
            return bass.ds(b * S, S)

        def width(m):
            return S if m == 0 else PIECES[m - 1][1] - PIECES[m - 1][0]

        def later(b, p, n):
            return (b, p + n) if p + n < NP else (b + 1, p + n - NP)

        with nc.Block() as block:
            @block.tensor
            def _(pe):
                def project(b, p, m, first=False):
                    g = b * NP + p
                    if m == 0 and not first:
                        pe.wait_ge(v_copied, g * NV)
                    if m:
                        pe.wait_ge(normed, g * NN + after_piece[m - 1])
                    if m == 1 and p == 0:
                        pe.wait_ge(kv_copied, 2 * b + 2)
                    if m == 3:
                        pe.wait_ge(v_copied, g * NV + 1)
                        for kc in range(1, NC):
                            mm = nc.tensor.matmul(PR[:, 0, (kc - 1) * P:kc * P], kv[:, KC[kc][0]:KC[kc][1]],
                                                  Wv[:, p * P:(p + 1) * P], start=True, stop=True)
                        mm.then_inc(pr_ready, 1)
                        return
                    w = Wq if m == 0 else Wk
                    rhs = c.xn[:, tokens(b)] if m == 0 else kv[:, PIECES[m - 1][0]:PIECES[m - 1][1]]
                    mm = nc.tensor.matmul(PR[:, 0, 0:width(m)], w[:, p * P:(p + 1) * P], rhs, start=True, stop=True)
                    if m == 2:
                        mm = nc.tensor.matmul(PR[0:SK, 0, VCTX:S], kv[:, 0:SK], Wv[:, p * P:(p + 1) * P], start=True,
                                              stop=True)
                    mm.then_inc(pr_ready, 1)

                def squares(b, p, m):
                    pe.wait_ge(squared, (b * NP + p) * NM + m + 1)
                    nc.tensor.matmul(PR[:, 1, 0:width(m)], blk[:, :], sq[:, 0:width(m)], start=True,
                                     stop=True).then_inc(ms_ready, 1)

                def maxima(b, p, u, first=False):
                    g, h, q = b * NP + p, u // QT, u % QT
                    if u == 0:
                        pe.wait_ge(cast, g * NM + NM)
                    if u or not first:
                        pe.wait_ge(s_used, g * NS + u)
                    s = 2 * (p % 2) + h
                    lhs = qnb[:, p % 2, q * P:(q + 1) * P]
                    nc.tensor.matmul(SP[:, BASE:512], lhs, kzb[:, s, 0:CUT], start=True, stop=False)
                    nc.tensor.matmul(SP[:, BASE:BASE + SK], c.onesb[:, :], negQ[:, bass.ds(b, 1), :], start=False,
                                     stop=True)
                    nc.tensor.matmul(SP[:, 512:BASE + K], lhs, kzb[:, s, CUT:K], start=True,
                                     stop=True).then_inc(s_ready, 1)

                def turn(b, p, prepared):
                    g = b * NP + p
                    pe.wait_ge(clipped, (g + prepared) * NM)
                    pe.wait_ge(s_used, (g + 1) * NS)
                    for q in range(QT):
                        mm = nc.tensor.transpose(turned[:, q * P:(q + 1) * P], nm[:, q, :], c.identb[:, :])
                    mm.then_inc(nm_turned, 1)

                def scores(b, p, t):
                    g, kc, h = b * NP + p, t // 2, t % 2
                    lo, hi = KC[kc]
                    if t == 0:
                        pe.wait_ge(negm_ready, g + 1)
                    if t >= 2:
                        pe.wait_ge(p_ready, g * NT + t - 1)
                    out = TP[0:hi - lo, t % 2, :]
                    nc.tensor.matmul(out, kz[:, 2 * (p % 4) + h, lo:hi], qn[:, p % 4, :], start=True, stop=False)
                    nc.tensor.matmul(out, sel2[:, h, 0:hi - lo], negm[:, p % 2, :], start=False,
                                     stop=True).then_inc(t_ready, 1)

                def values(b, p, kc):
                    g, n = b * NP + p, KC[kc][1] - KC[kc][0]
                    if kc == 0:
                        pe.wait_ge(o_normed, g)
                    pe.wait_ge(p_ready, g * NT + 2 * kc + 2)
                    for h in range(2):
                        mm = nc.tensor.matmul(O[HD * h:HD * h + HD, :], V[0:n, p % 4, kc, HD * h:HD * h + HD],
                                              prob[0:n, (2 * kc + h) % 8, :], start=kc == 0, stop=kc == NC - 1)
                    mm.then_inc(pv_done, 1)

                def sums(b, p):
                    pe.wait_ge(summed, (b * NP + p + 1) * NA)
                    for h in range(2):
                        mm = nc.tensor.matmul(DEN[HD * h:HD * h + HD, :], onesf[:, :], acc[:, h, :], start=True,
                                              stop=True)
                    mm.then_inc(pv_done, 1)

                def batch(b, last):
                    for p in range(NP):
                        follows, prepares = not last or p + 1 < NP, not last or p + 2 < NP
                        for t in range(NT):
                            scores(b, p, t)
                            if follows and 1 <= t <= NS:
                                maxima(*later(b, p, 1), t - 1)
                            if follows and t == NT - 1:
                                turn(*later(b, p, 1), 2 if prepares else 1)
                            if t == 0 and p == 0:
                                pe.wait_ge(up_ready, b)
                            if prepares and t in SQUARES:
                                squares(*later(b, p, 2), SQUARES[t])
                            if t >= 3 and t % 2:
                                values(b, p, t // 2 - 1)
                            if prepares and t in PROJECT and t < NT - 1:
                                project(*later(b, p, 2), PROJECT[t])
                        if prepares:
                            project(*later(b, p, 2), 3)
                        values(b, p, NC - 1)
                        sums(b, p)
                    if not last:
                        pe.wait_ge(v_copied, (b * NP + NP + 2) * NV)
                    for p in range(NP):
                        pe.wait_ge(o_normed, b * NP + p + 1)
                        mm = nc.tensor.matmul(PR[:, 0, :], Wo[:, p, :], on[:, p, :], start=(p == 0), stop=(p == NP - 1))
                    mm.then_inc(y_ready, 1)

                for p in range(2):
                    for m in range(NM):
                        project(0, p, m, first=p == 0)
                        squares(0, p, m)
                    project(0, p, 3)
                for u in range(NS):
                    maxima(0, 0, u, first=True)
                turn(0, 0, 2)
                pe.wait_ge(v_copied, 2 * NV)
                with pe.Fori(0, B - 1) as b:
                    batch(b, False)
                batch(B - 1, True)

            @block.scalar
            def _(act):
                def inputs(b):
                    nc.scalar.copy(kv[:, 0:SK], cn[:, bass.ds(b * SK, SK)]).then_inc(kv_copied, 1)
                    nc.scalar.copy(kv[:, SK:K], c.xn[:, tokens(b)]).then_inc(kv_copied, 1)

                def square(b, p, m):
                    act.wait_ge(pr_ready, (b * NP + p) * 4 + m + 1)
                    nc.scalar.activation(sq[:, 0:width(m)], PR[:, 0, 0:width(m)], ACT.Square).then_inc(squared, 1)
                    if m == 2:
                        nc.scalar.copy(V[0:SK, p % 4, 0, :], PR[0:SK, 0, VCTX:S]).then_inc(v_copied, 1)

                def rms(b, p, m):
                    i = (b * NP + p) * NM + m
                    act.wait_ge(clipped, i + 1)
                    nc.scalar.activation(lnn[:, 0:width(m)], clip[:, 0:width(m)], ACT.Ln).then_inc(n_log, 1)
                    act.wait_ge(n_log, i + 1)
                    nc.scalar.activation(rn[:, 0:width(m)], lnn[:, 0:width(m)], ACT.Exp, scale=-0.5).then_inc(n_rms, 1)

                def keep_values(b, p):
                    act.wait_ge(pr_ready, (b * NP + p) * 4 + 4)
                    nc.scalar.copy(V[:, p % 4, 1:NC, :], PR[:, 0, :].rearrange("q (k f) -> q k f", k=QT))\
                        .then_inc(v_copied, 1)
                    if p == NP - 1 and not (isinstance(b, int) and b == B - 1):
                        inputs(b + 1)

                def batch(b, last):
                    act.wait_ge(pv_done, b * NP * NPV)
                    nc.scalar.copy(rowcur[0:SK, :], rowneg[0:SK, bass.ds(b, 1)]).then_inc(row_copied, 1)
                    act.wait_ge(row_copied, b + 1)
                    for p in range(NP):
                        g, prepares = b * NP + p, not last or p + 2 < NP
                        for t in range(NT):
                            kc, h = t // 2, t % 2
                            n = KC[kc][1] - KC[kc][0]
                            act.wait_ge(t_ready, g * NT + t + 1)
                            if t >= 8:
                                act.wait_ge(pv_done, g * NPV + (t - 8) // 2 + 1)
                                act.wait_ge(ctx_added, g * 2 + t - 7)
                            else:
                                act.wait_ge(pv_done, g * NPV)
                            nc.scalar.activation(prob[0:n, t % 8, :], TP[0:n, t % 2, :], ACT.Exp,
                                                 bias=rowcur[0:n, :] if kc == 0 else 0.0).then_inc(p_ready, 1)
                            if prepares and t in PROJECT and PROJECT[t] < 3:
                                square(*later(b, p, 2), PROJECT[t])
                            if prepares and t in RMS:
                                rms(*later(b, p, 2), RMS[t])
                        if prepares:
                            keep_values(*later(b, p, 2))
                        act.wait_ge(pv_done, (g + 1) * NPV)
                        nc.scalar.activation(lnd[:, :], DEN[:, :], ACT.Ln).then_inc(den_log, 1)
                        act.wait_ge(den_log, g + 1)
                        nc.scalar.activation(rden[:, :], lnd[:, :], ACT.Exp, scale=-1.0).then_inc(den_ready, 1)
                    act.wait_ge(y_ready, b + 1)
                    act.wait_ge(x_updated, b)
                    nc.scalar.activation(up[:, :], PR[:, 0, :], ACT.Identity, bias=cv[:, 1:2],
                                         scale=c.gates[:, gate:gate + 1]).then_inc(up_ready, 1)

                nc.scalar.preload_act_table_set(LOG_EXP)
                inputs(0)
                for p in range(2):
                    for m in range(NM):
                        square(0, p, m)
                        rms(0, p, m)
                    keep_values(0, p)
                with act.Fori(0, B - 1) as b:
                    batch(b, False)
                batch(B - 1, True)

            @block.vector
            def _(dve):
                def clipping(b, p, m):
                    dve.wait_ge(ms_ready, (b * NP + p) * NM + m + 1)
                    nc.vector.tensor_scalar(clip[:, 0:width(m)], PR[:, 1, 0:width(m)], 1.0 / HD, 1e-16, ALU.mult,
                                            ALU.max).then_inc(clipped, 1)

                def normalise(b, p, m):
                    n = width(m)
                    dve.wait_ge(n_rms, (b * NP + p) * NM + m + 1)
                    if m == 0:
                        nc.vector.scalar_tensor_tensor(out=qn[:, p % 4, :], in0=PR[:, 0, :], scalar=cv[:, 0:1],
                                                       in1=rn[:, :], op0=ALU.mult, op1=ALU.mult).then_inc(normed, 1)
                        return
                    lo, hi = PIECES[m - 1]
                    for h in range(2):
                        r = slice(HD * h, HD * h + HD)
                        nc.vector.scalar_tensor_tensor(out=kz[r, 2 * (p % 4) + h, lo:hi], in0=PR[r, 0, 0:n],
                                                       scalar=vec[r, 5:6], in1=rn[r, 0:n], op0=ALU.mult,
                                                       op1=ALU.mult).then_inc(normed, 1)

                def reduce(b, p, u):
                    g, h, q = b * NP + p, u // QT, u % QT
                    dve.wait_ge(s_ready, g * NS + u + 1)
                    nc.vector.tensor_reduce(nm[:, q, h:h + 1], SP[:, BASE:BASE + K], AX.X, ALU.max,
                                            negate=True).then_inc(s_used, 1)

                def shift(b, p):
                    dve.wait_ge(nm_turned, b * NP + p + 1)
                    nc.vector.tensor_copy(negm[:, p % 2, :], turned).then_inc(negm_ready, 1)

                def add_context(b, p, h):
                    g = b * NP + p
                    dve.wait_ge(p_ready, g * NT + h + 1)
                    dve.wait_ge(summed, g * NA + h + 1)
                    nc.vector.tensor_tensor(acc[0:SK, h, :], acc[0:SK, h, :], prob[0:SK, h, :],
                                            ALU.add).then_inc(ctx_added, 1)

                def batch(b, last):
                    for p in range(NP):
                        follows, prepares = not last or p + 1 < NP, not last or p + 2 < NP
                        for t in range(1, NT):
                            if follows and t <= NS:
                                reduce(*later(b, p, 1), t - 1)
                            if prepares and t in SQUARES:
                                clipping(*later(b, p, 2), SQUARES[t])
                            if prepares and t in RMS:
                                normalise(*later(b, p, 2), RMS[t])
                            if t == 6:
                                for h in range(2):
                                    add_context(b, p, h)
                        if follows:
                            shift(*later(b, p, 1))
                        dve.wait_ge(den_ready, b * NP + p + 1)
                        nc.vector.tensor_tensor(on[:, p, :], O[:, :], rden[:, :], ALU.mult).then_inc(o_normed, 1)
                    dve.wait_ge(up_ready, b + 1)
                    nc.vector.tensor_tensor(c.xT[:, tokens(b)], c.xT[:, tokens(b)], up[:, :], ALU.add)\
                        .then_inc(x_updated, 1)

                for p in range(2):
                    for m in range(NM):
                        clipping(0, p, m)
                        normalise(0, p, m)
                for u in range(NS):
                    reduce(0, 0, u)
                shift(0, 0)
                with dve.Fori(0, B - 1) as b:
                    batch(b, False)
                batch(B - 1, True)
                dve.wait_ge(x_updated, B)

            @block.gpsimd
            def _(pool):
                def cast_queries(b, p):
                    g = b * NP + p
                    pool.wait_ge(normed, g * NN + 1)
                    nc.gpsimd.tensor_tensor(qnb[:, p % 2, :], qn[:, p % 4, :], onesf[:, 0:1].broadcast_to([P, S]),
                                            ALU.mult).then_inc(cast, 1)

                def cast_keys(b, p, m):
                    lo, hi = PIECES[m - 1]
                    pool.wait_ge(normed, (b * NP + p) * NN + after_piece[m])
                    nc.gpsimd.tensor_tensor(kzb[:, 2 * (p % 2):2 * (p % 2) + 2, lo:hi],
                                            kz[:, 2 * (p % 4):2 * (p % 4) + 2, lo:hi],
                                            onesf[:, 0:1].broadcast_to([P, 2, hi - lo]),
                                            ALU.mult).then_inc(cast, 1)

                def add(b, p, kc, h):
                    g, i = b * NP + p, 2 * (kc - 2) + h
                    pool.wait_ge(p_ready, g * NT + 2 * kc + h + 1)
                    if kc == 3:
                        pool.wait_ge(ctx_added, g * 2 + h + 1)
                    if kc > 2:
                        pool.wait_ge(summed, g * NA + i - 1)
                    before = prob[:, 2 + h, :] if kc == 2 else acc[:, h, :]
                    nc.gpsimd.tensor_tensor(acc[:, h, :], before, prob[:, (2 * kc + h) % 8, :],
                                            ALU.add).then_inc(summed, 1)

                def batch(b, last):
                    for p in range(NP):
                        prepares = not last or p + 2 < NP
                        if prepares:
                            cast_queries(*later(b, p, 2))
                        for kc in range(2, NC):
                            for h in range(2):
                                add(b, p, kc, h)
                            if kc > 2 and prepares:
                                cast_keys(*later(b, p, 2), kc - 2)

                for p in range(2):
                    cast_queries(0, p)
                    cast_keys(0, p, 1)
                    cast_keys(0, p, 2)
                with pool.Fori(0, B - 1) as b:
                    batch(b, False)
                batch(B - 1, True)
                pool.wait_ge(summed, B * NP * NA)


class ExpertRing:
    SLOTS, EARLY = 16, 8
    PAIRS = 32

    def __init__(self, c, ctx):
        R = self.SLOTS
        self.slots = [self.buffers(c, ctx, i) for i in range(self.EARLY)]
        self.loaded = [c.sem(f"ring_loaded{i}") for i in range(R)]
        self.w1_dram, self.w2_dram = c.dram["F1_w1"], c.dram["F1_w2"]

    @staticmethod
    def buffers(c, ctx, i):
        return [ctx.enter_context(c.nc.sbuf_tensor(f"ring_w{n}_{i}", [P, 8 * P], F32)) for n in (1, 2)]

    def extend(self, c, ctx):
        self.slots += [self.buffers(c, ctx, i) for i in range(self.EARLY, self.SLOTS)]

    def load(self, sp, slot, pair):
        for dst, src in zip(self.slots[slot], (self.w1_dram, self.w2_dram)):
            sp.dma_start(dst[:, :], src[bass.ds(pair, 1), :, :].rearrange("a p n -> p (a n)"))\
                .then_inc(self.loaded[slot], 16)


def first_expert_loads(c, ring):
    c.disp = c.nc.dram_tensor("dispatched", [4096 + 3 * T, D], F32, kind="Internal").ap()
    c.rows_zeroed = c.sem("rows_zeroed")
    with c.nc.Block() as block:
        @block.sync
        def _(sp):
            sp.dma_start(c.disp[0:4096, :].rearrange("(p q) d -> p (q d)", p=P), c.dram["zeros"])\
                .then_inc(c.rows_zeroed, 16)
            for i in range(ring.EARLY):
                ring.load(sp, i, i)


def capacity_moe(c, name, gate, ring):
    nc, d = c.nc, c.dram
    E, TOPK, CAP = 64, 3, 64
    PAIRS, R = ring.PAIRS, ring.SLOTS
    SLOTS = E * CAP
    G = 4
    ydram = nc.dram_tensor("expert_out", [SLOTS, D], F32, kind="Internal").ap()
    with ExitStack() as whole, ExitStack() as ctx, c.phase():
        gk = whole.enter_context(nc.sbuf_tensor(name + "_gk", [P, TOPK, TILES], F32))
        slot_out = whole.enter_context(nc.sbuf_tensor(name + "_slot_out", [P, TOPK * TILES], U32))
        ring.extend(c, ctx)
        router = Router(c, ctx, name + "r", E, "F1_router", bias="F1_router_b")
        b2 = ctx.enter_context(nc.sbuf_tensor(name + "_b2", [P, PAIRS * D], F32))
        b1 = ctx.enter_context(nc.sbuf_tensor(name + "_b1", [P, PAIRS * 8], F32))
        b_loaded = c.sem(name + "_b_loaded")

        def start_loads(sp):
            router.load(sp)
            sp.dma_start(b2[:, :], d["F1_b2"]).then_inc(b_loaded, 16)
            sp.dma_start(b1[:, :], d["F1_b1"]).then_inc(b_loaded, 16)
            for i in range(ring.EARLY, R):
                ring.load(sp, i, i)

        norm_x(c, name + "_n", start_loads)
        top, place = route(c, ctx, router, softmax=False)

        def sb(n, shape, dt=F32):
            return ctx.enter_context(nc.sbuf_tensor(f"{name}_{n}", shape, dt))

        def sem(n):
            return c.sem(f"{name}_{n}")

        slot_in = sb("slot_in", [P, TOPK * TILES], U32)
        scattered = sem("scattered")

        with ExitStack() as own:
            def tmp(n, shape, dt=F32):
                return own.enter_context(nc.sbuf_tensor(f"{name}_{n}", shape, dt))
            hot = tmp("hot", [P, TOPK, TILES, E])
            OH, run = tmp("OH", [P, TILES, E], BF16), tmp("run", [P, TILES, E], BF16)
            upper, upperb = tmp("upper", [P, P]), tmp("upperb", [P, P], BF16)
            prod = tmp("prod", [P, TILES, E])
            pos, valid, ge, trash, sf = (tmp(n, [P, TOPK, TILES]) for n in ("pos", "valid", "ge", "trash", "sf"))
            gs = tmp("gs", [P, 2, TILES])
            xtok = tmp("xtok", [P, TILES, D])
            PS = own.enter_context(nc.psum_tensor(name + "_PS", [P, TILES * E], F32))
            XP = own.enter_context(nc.psum_tensor(name + "_XP", [P, 2, S], F32))
            loaded, hots, counted, exped, turned, tok_ready, slots = (
                sem(n) for n in ("loaded", "hots", "counted", "exped", "turned", "tok_ready", "slots"))
            hots_done = []
            with nc.Block() as block:
                @block.sync
                def _(sp):
                    sp.dma_start(upper[:, :], d["upper"]).then_inc(loaded, 16)
                    sp.dma_start(trash[:, :, :], d["trash"]).then_inc(loaded, 16)

                @block.vector
                def _(dve):
                    n = 0

                    def step(ins):
                        nonlocal n
                        n += 1
                        ins.then_inc(hots, 1)
                        dve.wait_ge(hots, n)

                    def over(a, k):
                        return a[:, :, k:k + 1].broadcast_to([P, TILES, E])

                    for k in range(TOPK):
                        step(nc.vector.tensor_tensor(hot[:, k, :, :], c.iota[:, :].rearrange("p (a e) -> p a e", a=1)
                                                     .broadcast_to([P, TILES, E]), over(place, k), ALU.is_equal))
                    step(nc.vector.tensor_tensor(prod[:, :, :], hot[:, 0, :, :], hot[:, 1, :, :], ALU.add))
                    step(nc.vector.tensor_tensor(OH[:, :, :], prod[:, :, :], hot[:, 2, :, :], ALU.add))
                    step(nc.vector.memset(run[:, 0, :], 0.0))
                    for t in range(1, TILES):
                        step(nc.vector.tensor_tensor(run[:, t, :], run[:, t - 1, :], OH[:, t - 1, :], ALU.add))
                    dve.wait_ge(loaded, 32)
                    step(nc.vector.tensor_copy(upperb[:, :], upper[:, :]))
                    hots_done.append(n)
                    step(nc.vector.tensor_tensor(ge[:, :, :].rearrange("p k t -> p t k"), top[:, :, 0:TOPK],
                                                 top[:, :, 0:1].broadcast_to([P, TILES, TOPK]), ALU.subtract))
                    hots_done.append(n)
                    dve.wait_ge(counted, 1)
                    for k in range(TOPK):
                        step(nc.vector.tensor_tensor(prod[:, :, :], hot[:, k, :, :],
                                                     PS[:, :].rearrange("p (t e) -> p t e", t=TILES), ALU.mult))
                        step(nc.vector.tensor_reduce(pos[:, k, :], prod[:, :, :], AX.X, ALU.add))
                    step(nc.vector.tensor_scalar(valid[:, :, :], pos[:, :, :], float(CAP), None, ALU.is_lt))
                    step(nc.vector.tensor_scalar(pos[:, :, :], pos[:, :, :], float(CAP - 1), None, ALU.min))
                    step(nc.vector.scalar_tensor_tensor(out=pos[:, :, :], in0=place[:, :, 0:TOPK]
                                                        .rearrange("p t k -> p k t"), scalar=float(CAP),
                                                        in1=pos[:, :, :], op0=ALU.mult, op1=ALU.add))
                    step(nc.vector.tensor_copy(slot_out[:, :].rearrange("p (k t) -> p k t", k=TOPK), pos[:, :, :]))
                    step(nc.vector.tensor_tensor(sf[:, :, :], pos[:, :, :], trash[:, :, :], ALU.subtract))
                    step(nc.vector.tensor_tensor(sf[:, :, :], sf[:, :, :], valid[:, :, :], ALU.mult))
                    step(nc.vector.tensor_tensor(sf[:, :, :], sf[:, :, :], trash[:, :, :], ALU.add))
                    nc.vector.tensor_copy(slot_in[:, :].rearrange("p (k t) -> p k t", k=TOPK),
                                          sf[:, :, :]).then_inc(slots, 1)
                    dve.wait_ge(exped, 1)
                    step(nc.vector.tensor_reduce(gs[:, 0, :], gk[:, :, :].rearrange("p k t -> p t k"), AX.X, ALU.add))
                    step(nc.vector.reciprocal(gs[:, 1, :], gs[:, 0, :]))
                    step(nc.vector.tensor_tensor(gk[:, :, :], gk[:, :, :], gs[:, 1:2, :]
                                                 .broadcast_to([P, TOPK, TILES]), ALU.mult))
                    step(nc.vector.tensor_tensor(gk[:, :, :], gk[:, :, :], valid[:, :, :], ALU.mult))

                @block.tensor
                def _(pe):
                    for g in range(G):
                        if g >= 2:
                            pe.wait_ge(tok_ready, g - 1)
                        for q in range(QT):
                            t = g * QT + q
                            mm = nc.tensor.transpose(XP[:, g % 2, q * P:(q + 1) * P], c.xn[:, t * P:(t + 1) * P],
                                                     c.ident[:, :])
                        mm.then_inc(turned, 1)
                    pe.wait_ge(hots, 21 + 1)
                    for t in range(TILES):
                        nc.tensor.matmul(PS[:, t * E:(t + 1) * E], upperb[:, :], OH[:, t, :], start=True, stop=False)
                        mm = nc.tensor.matmul(PS[:, t * E:(t + 1) * E], c.onesb[:, :], run[:, t, :], start=False,
                                              stop=True)
                    mm.then_inc(counted, 1)

                @block.scalar
                def _(act):
                    nc.scalar.preload_act_table_set(LOG_EXP)
                    for g in range(G):
                        act.wait_ge(turned, g + 1)
                        nc.scalar.copy(xtok[:, g * QT:(g + 1) * QT, :], XP[:, g % 2, :]
                                       .rearrange("p (q d) -> p q d", q=QT)).then_inc(tok_ready, 1)
                    act.wait_ge(hots, 21 + 2)
                    nc.scalar.activation(gk[:, :, :], ge[:, :, :], ACT.Exp).then_inc(exped, 1)

                @block.gpsimd
                def _(pool):
                    pool.wait_ge(slots, 1)
                    pool.wait_ge(tok_ready, G)
                    pool.wait_ge(c.rows_zeroed, 16)
                    for t in range(TILES):
                        for k in range(TOPK):
                            i = k * TILES + t
                            nc.gpsimd.indirect_dma_start(
                                out=c.disp[:, :], out_offset=bass.IndirectOffsetOnAxis(ap=slot_in[:, i:i + 1], axis=0),
                                in_=xtok[:, t, :], in_offset=None).then_inc(scattered, 16)
                    pool.wait_ge(scattered, 16 * TILES * TOPK)
            assert hots_done == [22, 23]

        HP = ctx.enter_context(nc.psum_tensor(name + "_HP", [P, 2, 512], F32))
        YP = ctx.enter_context(nc.psum_tensor(name + "_YP", [P, 2, 512], F32))
        XT = ctx.enter_context(nc.psum_tensor(name + "_XT", [P, 2, 512], F32))
        xs = sb("xs", [P, PAIRS, D])
        bufT = xs[:, :, :].rearrange("p q d -> p (q d)")
        hb, hg = sb("hb", [P, 2, 512]), sb("hg", [P, 2, 512])
        (rows_in, rows_turned, buf_ready, h_ready, b_added, gelued, y_ready, y_kept, stored) = (
            sem(n) for n in ("rows_in", "rows_turned", "buf_ready", "h_ready", "b_added", "gelued", "y_ready",
                             "y_kept", "stored"))
        rows = [sem(f"rows{i}") for i in range(4)]
        with nc.Block() as block:
            @block.sync
            def _(sp):
                for i in range(4):
                    sp.dma_start(xs[:, 8 * i:8 * i + 8, :], c.disp[1024 * i:1024 * (i + 1), :]
                                 .rearrange("(q p) d -> p q d", p=P)).then_inc(rows[i], 16)

            @block.tensor
            def _(pe):
                for g in range(PAIRS // 4):
                    if g % 2 == 0:
                        pe.wait_ge(rows[g // 2], 16)
                    if g >= 2:
                        pe.wait_ge(buf_ready, g - 1)
                    for q in range(4):
                        mm = nc.tensor.transpose(XT[:, g % 2, q * P:(q + 1) * P], xs[:, 4 * g + q, :], c.ident[:, :])
                    mm.then_inc(rows_turned, 1)

            @block.scalar
            def _(act):
                for g in range(PAIRS // 4):
                    act.wait_ge(rows_turned, g + 1)
                    nc.scalar.copy(bufT[:, g * 512:(g + 1) * 512], XT[:, g % 2, :]).then_inc(buf_ready, 1)
                act.wait_ge(buf_ready, PAIRS // 4)

        ys = xs
        with nc.Block() as block:
            @block.sync
            def _(sp):
                def store(it):
                    sp.wait_ge(y_kept, (it + 1) * R)
                    sp.dma_start(ydram[bass.ds(it * (R * P), R * P), :].rearrange("(q p) d -> p q d", p=P),
                                 ys[:, bass.ds(it * R, R), :]).then_inc(stored, 16)

                with sp.Fori(0, PAIRS // R - 1) as it:
                    for i in range(R):
                        sp.wait_ge(y_ready, it * R + i + 1)
                        ring.load(sp, i, (it + 1) * R + i)
                    store(it)
                store(PAIRS // R - 1)
                sp.wait_ge(stored, 16 * (PAIRS // R))

            @block.tensor
            def _(pe):
                with pe.Fori(0, PAIRS // R) as it:
                    def up(i):
                        n = it * R + i
                        pe.wait_ge(ring.loaded[i], 32 * it + 32)
                        if i >= 2:
                            pe.wait_ge(b_added, n - 1)
                        else:
                            pe.wait_ge(b_added, it * R)
                        for e in range(2):
                            for j in range(4):
                                m = 4 * e + j
                                mm = nc.tensor.matmul(HP[:, i % 2, m * CAP:(m + 1) * CAP],
                                                      ring.slots[i][0][:, m * P:(m + 1) * P],
                                                      bufT[:, bass.ds(n * 2 * CAP + e * CAP, CAP)],
                                                      start=True, stop=True)
                        mm.then_inc(h_ready, 1)

                    def down(i):
                        n = it * R + i
                        pe.wait_ge(gelued, n + 1)
                        if i >= 2:
                            pe.wait_ge(y_kept, n - 1)
                        else:
                            pe.wait_ge(y_kept, it * R)
                        for j in range(4):
                            for e in range(2):
                                m = 4 * e + j
                                mm = nc.tensor.matmul(YP[CAP * e:CAP * e + CAP, i % 2, 0:D],
                                                      hg[:, i % 2, m * CAP:(m + 1) * CAP],
                                                      ring.slots[i][1][:, m * P:(m + 1) * P],
                                                      start=(j == 0), stop=(j == 3))
                        mm.then_inc(y_ready, 1)

                    for i in range(R):
                        up(i)
                        if i:
                            down(i - 1)
                    down(R - 1)

            @block.vector
            def _(dve):
                dve.wait_ge(b_loaded, 32)
                with dve.Fori(0, PAIRS // R) as it:
                    def add(i):
                        n = it * R + i
                        dve.wait_ge(h_ready, n + 1)
                        if i >= 2:
                            dve.wait_ge(gelued, n - 1)
                        else:
                            dve.wait_ge(gelued, it * R)
                        nc.vector.tensor_tensor(
                            hb[:, i % 2, :].rearrange("p (m s) -> p m s", m=8),
                            HP[:, i % 2, :].rearrange("p (m s) -> p m s", m=8),
                            b1[:, bass.ds(n * 8, 8)].rearrange("p (m a) -> p m a", a=1).broadcast_to([P, 8, CAP]),
                            ALU.add).then_inc(b_added, 1)

                    def keep(i):
                        n = it * R + i
                        dve.wait_ge(y_ready, n + 1)
                        nc.vector.tensor_tensor(ys[:, bass.ds(n, 1), :].rearrange("p a d -> p (a d)"),
                                                YP[:, i % 2, 0:D], b2[:, bass.ds(n * D, D)],
                                                ALU.add).then_inc(y_kept, 1)

                    for i in range(R):
                        add(i)
                        if i:
                            keep(i - 1)
                    keep(R - 1)

            @block.scalar
            def _(act):
                nc.scalar.preload_act_table_set(GELU)
                with act.Fori(0, PAIRS // R) as it:
                    for i in range(R):
                        n = it * R + i
                        act.wait_ge(b_added, n + 1)
                        if i >= 2:
                            act.wait_ge(y_ready, n - 1)
                        else:
                            act.wait_ge(y_ready, it * R)
                        nc.scalar.activation(hg[:, i % 2, :], hb[:, i % 2, :], ACT.Gelu).then_inc(gelued, 1)

        ctx.close()
        with ExitStack() as own:
            yg = own.enter_context(nc.sbuf_tensor(name + "_yg", [P, TOPK * TILES, D], F32))
            acc = own.enter_context(nc.sbuf_tensor(name + "_acc", [P, TILES, D], F32))
            TR = own.enter_context(nc.psum_tensor(name + "_TR", [P, 2, S], F32))
            gathered = [sem(f"gathered{g}") for g in range(G)]
            summed, back, x_updated = sem("summed"), sem("back"), sem("x_updated")
            with nc.Block() as block:
                @block.gpsimd
                def _(pool):
                    for t in range(TILES):
                        for k in range(TOPK):
                            i = k * TILES + t
                            nc.gpsimd.indirect_dma_start(
                                out=yg[:, i, :], out_offset=None, in_=ydram[:, :],
                                in_offset=bass.IndirectOffsetOnAxis(ap=slot_out[:, i:i + 1], axis=0))\
                                .then_inc(gathered[t // QT], 16)

                @block.vector
                def _(dve):
                    for g in range(G):
                        dve.wait_ge(gathered[g], 16 * TOPK * QT)
                        for k in range(TOPK):
                            if k:
                                dve.wait_ge(summed, (g * TOPK + k) * QT)
                            for q in range(QT):
                                t = g * QT + q
                                y = yg[:, k * TILES + t, :]
                                if k == 0:
                                    ins = nc.vector.tensor_scalar(acc[:, t, :], y, gk[:, k, t:t + 1], None, ALU.mult)
                                else:
                                    ins = nc.vector.scalar_tensor_tensor(out=acc[:, t, :], in0=y,
                                                                         scalar=gk[:, k, t:t + 1], in1=acc[:, t, :],
                                                                         op0=ALU.mult, op1=ALU.add)
                                ins.then_inc(summed, 1)
                        dve.wait_ge(back, g + 1)
                        nc.vector.scalar_tensor_tensor(out=c.xT[:, g * S:(g + 1) * S], in0=TR[:, g % 2, :],
                                                       scalar=c.gates[:, gate:gate + 1], in1=c.xT[:, g * S:(g + 1) * S],
                                                       op0=ALU.mult, op1=ALU.add).then_inc(x_updated, 1)
                    dve.wait_ge(x_updated, G)

                @block.tensor
                def _(pe):
                    for g in range(G):
                        pe.wait_ge(summed, (g + 1) * TOPK * QT)
                        if g >= 2:
                            pe.wait_ge(x_updated, g - 1)
                        for q in range(QT):
                            mm = nc.tensor.transpose(TR[:, g % 2, q * P:(q + 1) * P], acc[:, g * QT + q, :],
                                                     c.ident[:, :])
                        mm.then_inc(back, 1)


def flamingo_kernel(nc, dram, out):
    with ExitStack() as ctx:
        c = Core(nc, ctx, dram)
        load_shared(c)
        with ExitStack() as until_moe:
            ring = ExpertRing(c, until_moe)
            first_expert_loads(c, ring)
            head_attention(c, "a0", 0, "L0_Wq", "L0_Wk", "L0_Wv", bq=True, bk=True, bv=True, mask=True)
            ternary_ffn(c, "f0", 4)
            head_attention(c, "a1", 1, "L1_Wq", "L1_Wk", "L1_Wv", bq=True, bk=True, bv=True, wo="L1_Wo", bo=True,
                           relbias=True)
            capacity_moe(c, "f1", 5, ring)
        perceiver_attention(c, "a2", 2)
        dense_glu_moe(c, "f2", 6)
        head_attention(c, "a3", 3, "L3_Wq", "L3_Wk", "L3_Wv", wo="L3_Wo", rope=True)
        shared_moe(c, "f3", 7)
        stored = c.sem("stored")
        with nc.Block() as block:
            @block.sync
            def _(sp):
                sp.dma_start(out, c.xT[:, :]).then_inc(stored, 16)
                sp.wait_ge(stored, 16)
def shape_constants():
    f = np.float32
    k = {}
    k["center"] = (np.eye(P) - 1.0 / P).astype(f)
    k["mean"] = np.full((P, P), 1.0 / P, f)
    k["ident"] = np.eye(P, dtype=f)
    d = np.arange(P)
    k["headmask"] = (d[:, None] // DH == np.arange(H)[None]).astype(f)
    row = np.arange(CH * CR)
    rm = ((row[:, None] // SK == np.arange(32)[None] // DH) & (row[:, None] < ROWS)).astype(f)
    k["rowmask"] = np.zeros((P, CH, 32), f)
    k["rowmask"][:CR] = rm.reshape(CH, CR, 32).transpose(1, 0, 2)
    k["self"] = (d[:, None] == np.arange(QUAD * ROWS)[None] // SK).astype(f)
    k["blk8"] = (d[:, None] // DH == d[None] // DH).astype(f)
    k["blk64"] = (d[:, None] // 64 == d[None] // 64).astype(f)

    def rope(n, theta):
        freqs = f(theta) ** (-np.arange(0, DH, 2, dtype=f) / f(DH))
        ang = np.arange(n, dtype=f)[:, None] * freqs[None]
        half = d % DH % (DH // 2)
        sign = np.where(d % DH < DH // 2, -1.0, 1.0).astype(f)
        return np.cos(ang)[:, half].T.astype(f), (np.sin(ang)[:, half].T * sign[:, None]).astype(f)

    k["qcs"] = np.stack(rope(S, 32.0), 1)
    kc, ks = rope(SK, 1000.0)
    k["kcs"] = np.stack([np.tile(kc[:, ::-1], (1, B)), np.tile(ks[:, ::-1], (1, B))], 1)
    k["zeros"] = np.zeros((P, 32 * P), f)
    k["trash"] = (4096 + np.arange(3)[None, :, None] * T + np.arange(TILES)[None, None] * P + d[:, None, None]).astype(f)
    k["iota"] = np.tile(np.arange(64, dtype=f), (P, 1))
    k["pair"] = (d[:, None, None] == 2 * np.arange(8)[None, :, None] + d[None, None] // 64).astype(f)
    k["sel2"] = (d[:, None, None] == np.arange(2)[None, :, None] + 0 * d[None, None]).astype(f)
    k["upper"] = (d[:, None] < d[None]).astype(f)
    return k


def layout(i):
    a = {n: np.asarray(v) for n, v in i.items()}
    f = np.float32
    o = {"xT": a["x"].reshape(T, D).T}
    ctxT = a["ctx_1024"].transpose(2, 0, 1)[:, :, ::-1]
    o["ctxrep"] = np.tile(ctxT, (1, 1, HQ))
    o["gates"] = np.tile(np.concatenate([a["g_xattn"], a["g_ffn"]])[None], (P, 1))

    def vectors(**cols):
        v = np.zeros((P, 8), f)
        for n, col in cols.items():
            v[:, int(n[1])] = col
        return v

    def reps(w):
        return np.tile(w, H)

    half = DH // 2
    partner = np.arange(P) // DH * DH + (np.arange(P) % DH + half) % DH
    for n in ("Wq", "Wk", "Wv"):
        o[f"L0_{n}"] = a[f"L0_xattn_{n}"].T
        o[f"L1_{n}"] = a[f"L1_xattn_{n}"]
        o[f"L3_{n}"] = a[f"L3_xattn_{n}"].T
    o["L1_Wo"], o["L3_Wo"] = a["L1_xattn_Wo"], a["L3_xattn_Wo"].T
    o["L3_Wq_p"], o["L3_Wk_p"] = o["L3_Wq"][:, partner], o["L3_Wk"][:, partner]
    o["a0_vec"] = vectors(c0=a["L0_xattn_bq"], c1=a["L0_xattn_bk"], c2=a["L0_xattn_bv"])
    o["a1_vec"] = vectors(c0=a["L1_xattn_bq"], c1=a["L1_xattn_bk"], c2=a["L1_xattn_bv"], c3=a["L1_xattn_bo"],
                          c4=np.repeat(a["L1_xattn_logit_scale"], DH))
    qw, kw = reps(a["L3_xattn_q_norm_w"]), reps(a["L3_xattn_k_norm_w"])
    o["a3_vec"] = vectors(c4=kw, c5=kw[partner], c6=qw, c7=qw[partner])
    m = a["mask_BxSxS2_ff1"][:, :, ::-1]
    mt = np.zeros((B, CH * CR, S), f)
    mt[:, :ROWS] = np.tile(m.transpose(0, 2, 1), (1, HQ, 1))
    o["maskT"] = mt.reshape(B * CH, CR, S).transpose(1, 0, 2)
    o["maskQ"] = m.reshape(B * QT, P, SK).transpose(1, 0, 2)

    def words(m):
        w = np.zeros(m.shape + (4,), np.uint8)
        w[..., 0] = m
        return w.view(np.int32)[..., 0]

    km = words(a["mask_BxS2_bf0"][:, ::-1])
    o["keymask"] = km.reshape(B * SK)
    rk = np.zeros((B, CH * CR), np.int32)
    rk[:, :ROWS] = np.tile(km, (1, HQ))
    o["rowkeymask"] = rk.reshape(B * CH, CR).T
    key = SK - 1 - np.arange(SK)
    rel = np.clip(key[None] - np.arange(S)[:, None], -128, 128) + 128
    bias = a["L1_xattn_bias_table"][rel].transpose(2, 1, 0)
    bt = np.zeros((QUAD, CH * CR, S), f)
    bt[:, :ROWS] = bias.reshape(QUAD, ROWS, S)
    o["biasT"] = bt.reshape(QUAD * CH, CR, S).transpose(1, 0, 2)
    o["biasQ"] = bias.reshape(H * SK, S).T[:3 * P].reshape(3, P, H * SK).transpose(1, 0, 2)

    def hidden_rows(w):
        return w.reshape(-1, P, w.shape[-1]).transpose(1, 0, 2)

    o["F0_W1"] = a["L0_ffn_W_fc"].T
    o["F0_W2"] = hidden_rows(a["L0_ffn_W_proj"].T).reshape(P, -1)
    o["F0_ln"] = np.concatenate([a[f"L0_ffn_ln_{n}"].reshape(-1, P).T for n in "wb"], 1)
    o["F2_router"] = a["L2_ffn_router_w"]
    for n in ("w1", "v1"):
        o[f"F2_{n}"] = a[f"L2_ffn_{n}"].transpose(1, 0, 2).reshape(P, -1)
    w2 = np.zeros((8, 3 * P, P), f)
    w2[:, :352] = a["L2_ffn_w2"]
    o["F2_w2"] = hidden_rows(w2.reshape(-1, P))
    o["F2_bias"] = a["L2_ffn_bias"].reshape(P, 1)
    o["F3_router"] = a["L3_ffn_Wg"].T
    for n, e, s in (("Wg", "We_gate", "Ws_gate"), ("Wu", "We_up", "Ws_up")):
        w = np.concatenate([a[f"L3_ffn_{e}"].reshape(-1, P), a[f"L3_ffn_{s}"]])
        o[f"F3_{n}"] = w.T.reshape(P, -1, P)
    wd = np.concatenate([a["L3_ffn_We_down"].transpose(0, 2, 1).reshape(-1, P), a["L3_ffn_Ws_down"].T])
    o["F3_Wd"] = hidden_rows(wd)
    o["F3_Wsg"] = np.tile(a["L3_ffn_Wsg"].T, (1, P))
    o["F1_router"], o["F1_router_b"] = a["L1_ffn_gate_w"], a["L1_ffn_gate_b"]
    o["F1_w1"] = a["L1_ffn_w1"].reshape(32, 2, P, 512).transpose(0, 2, 1, 3).reshape(32, P, 1024)
    o["F1_w2"] = a["L1_ffn_w2"].reshape(32, 8, P, P).transpose(0, 2, 1, 3).reshape(32, P, 1024)
    o["F1_b1"] = a["L1_ffn_b1"].reshape(32 * 8, P).T
    o["F1_b2"] = np.repeat(a["L1_ffn_b2"].reshape(32, 2, P).transpose(1, 0, 2).reshape(2, 32 * P), 64, axis=0)
    o["A2_Wq"] = a["L2_xattn_Wq"]
    o["A2_Wk"], o["A2_Wv"] = a["L2_xattn_Wkv"][:, :1024], a["L2_xattn_Wkv"][:, 1024:]
    o["A2_Wo"] = hidden_rows(a["L2_xattn_Wout"])
    o["A2_vec"] = vectors(c0=a["L2_xattn_ln_x_g"], c1=a["L2_xattn_ln_x_b"], c2=a["L2_xattn_ln_l_g"],
                          c3=a["L2_xattn_ln_l_b"], c4=np.tile(a["L2_xattn_qn_g"], 2),
                          c5=np.tile(a["L2_xattn_kn_g"], 2), c6=a["L2_xattn_bout"])
    km2 = words(a["mask_BxS2_bf1"][:, ::-1])
    o["keymask2"], o["rowmask2"] = km2.reshape(B * SK), km2.T
    return o


def kernel(**inputs):
    import numpy as _np
    import concourse.bacc as _bacc
    from concourse import mybir as _mybir
    from concourse.bass_utils import run_bass_kernel_spmd as _run

    nc = _bacc.Bacc("TRN2", target_bir_lowering=False, num_devices=1)
    arrays, dram = {}, {}
    for name, a in {**layout(inputs), **shape_constants()}.items():
        a = _np.ascontiguousarray(a)
        arrays[f"in_{name}"] = a
        dram[name] = nc.dram_tensor(f"in_{name}", a.shape, _mybir.dt.from_np(a.dtype), kind="ExternalInput").ap()
    out = nc.dram_tensor("out_xT", (P, T), F32, kind="ExternalOutput").ap()
    flamingo_kernel(nc, dram, out)
    r = _run(nc, [arrays], core_ids=[0])
    return _np.ascontiguousarray(r.results[0]["out_xT"].T).reshape(B, S, D)
```
